# Optimizing a Trainium2 kernel written in Bass

```python
import numpy as np
import jax
import jax.numpy as jnp

def _softmax(x, axis=-1):
    return jax.nn.softmax(x, axis=axis)

def _gelu(x):
    return jax.nn.gelu(x, approximate=True)

def _silu(x):
    return jax.nn.silu(x)

def _sigmoid(x):
    return jax.nn.sigmoid(x)

def _layernorm(x, axis=-1, eps=1e-05):
    m = jnp.mean(x, axis=axis, keepdims=True)
    v = jnp.var(x, axis=axis, keepdims=True)
    return (x - m) / jnp.sqrt(v + eps)

def _scatter_add(tgt, idx, src, axis=0):
    return tgt.at[idx].add(src)

def _segment_sum(src, seg, n):
    return jax.ops.segment_sum(src, seg, n)
kernel_name = 'mk_hybrid_d1_jaxref_r4_928baa'

def setup_inputs(seed: int=0):
    np.random.seed(seed)
    _w = jnp.asarray

    def _L0_attn_a_setup():
        import jax, jax.numpy as jnp
        import numpy as np
        from jax import lax
        B_SZ, SEQ, D_MODEL = (4, 256, 256)
        D_STATE, D_CONV, EXPAND = (16, 4, 2)
        D_INNER = EXPAND * D_MODEL
        EPS = 1e-06

        def layernorm(x, alpha, bias):
            mean = x.mean(axis=-1, keepdims=True)
            std = jnp.sqrt(jnp.var(x, axis=-1, keepdims=True, ddof=1))
            return alpha * (x - mean) / (std + EPS) + bias

        def selective_scan(x_conv, delta, A, Bm, Cm, D_param):
            L = x_conv.shape[1]

            def step(h, inp):
                xt, dt, bt, ct, t = inp
                dA = jnp.exp(jnp.clip(dt[..., None] * A, -10.0, 0.0))
                dBx = dt[..., None] * bt[:, None, :] * xt[..., None]
                h = dA * h + dBx
                hn = jnp.clip(jnp.linalg.norm(h, axis=-1, keepdims=True), 1e-06, None)
                scale = jnp.where(hn > 10.0, 10.0 / hn, jnp.ones_like(hn))
                h = jnp.where(t % 16 == 15, h * scale, h)
                y = jnp.einsum('bn,ben->be', ct, h) + D_param * xt
                return (h, y)
            h0 = jnp.zeros((x_conv.shape[0], x_conv.shape[2], A.shape[1]), x_conv.dtype)
            xs = (x_conv.swapaxes(0, 1), delta.swapaxes(0, 1), Bm.swapaxes(0, 1), Cm.swapaxes(0, 1), jnp.arange(L))
            _, ys = lax.scan(step, h0, xs)
            return ys.swapaxes(0, 1)
        key = jax.random.key(seed)
        ks = jax.random.split(key, 8)
        std = 0.02
        A = jnp.tile(jnp.arange(1, D_STATE + 1, dtype=jnp.float32)[None, :], (D_INNER, 1))
        return {'x': jax.random.normal(ks[0], (B_SZ, SEQ, D_MODEL), jnp.float32), 'in_proj_w': jax.random.normal(ks[1], (2 * D_INNER, D_MODEL), jnp.float32) * std, 'in_proj_b': jnp.zeros((2 * D_INNER,), jnp.float32), 'conv_w': jax.random.normal(ks[2], (D_INNER, 1, D_CONV), jnp.float32) * std, 'conv_b': jnp.zeros((D_INNER,), jnp.float32), 'x_proj_w': jax.random.normal(ks[3], (2 * D_STATE, D_INNER), jnp.float32) * std, 'x_proj_b': jnp.zeros((2 * D_STATE,), jnp.float32), 'dt_proj_w': jax.random.normal(ks[4], (D_INNER, D_INNER), jnp.float32) * std, 'dt_proj_b': jnp.zeros((D_INNER,), jnp.float32), 'A_log': jnp.log(A), 'D_param': jnp.ones((D_INNER,), jnp.float32), 'out_proj_w': jax.random.normal(ks[5], (D_MODEL, D_INNER), jnp.float32) * std, 'out_proj_b': jnp.zeros((D_MODEL,), jnp.float32), 'norm_alpha': jnp.ones((D_MODEL,), jnp.float32), 'norm_bias': jnp.zeros((D_MODEL,), jnp.float32), 'in_norm_alpha': jnp.ones((D_MODEL,), jnp.float32), 'in_norm_bias': jnp.zeros((D_MODEL,), jnp.float32)}
    _L0_attn_a_in = _L0_attn_a_setup()

    def _L0_attn_b_setup():
        import jax, jax.numpy as jnp
        import numpy as np
        B, L, D_MODEL, H = (4, 512, 256, 16)
        HD = D_MODEL // H
        EPS = 1e-06
        key = jax.random.key(seed)
        ks = jax.random.split(key, 9)
        s = 1.0 / np.sqrt(D_MODEL)
        return {'x': jax.random.normal(ks[0], (B, L, D_MODEL), dtype=jnp.float32), 'Wq': jax.random.normal(ks[1], (D_MODEL, D_MODEL), dtype=jnp.float32) * s, 'bq': jax.random.normal(ks[2], (D_MODEL,), dtype=jnp.float32) * 0.01, 'Wk': jax.random.normal(ks[3], (D_MODEL, D_MODEL), dtype=jnp.float32) * s, 'bk': jax.random.normal(ks[4], (D_MODEL,), dtype=jnp.float32) * 0.01, 'Wv': jax.random.normal(ks[5], (D_MODEL, D_MODEL), dtype=jnp.float32) * s, 'bv': jax.random.normal(ks[6], (D_MODEL,), dtype=jnp.float32) * 0.01, 'Wo': jax.random.normal(ks[7], (D_MODEL, D_MODEL), dtype=jnp.float32) * s, 'bo': jax.random.normal(ks[8], (D_MODEL,), dtype=jnp.float32) * 0.01}
    _L0_attn_b_in = _L0_attn_b_setup()

    def _L0_ffn_setup():
        import jax, jax.numpy as jnp
        import numpy as np
        HIDDEN = 256
        NUM_EXPERTS = 16
        TOP_K = 6
        EPS = 1e-10
        key = jax.random.key(seed)
        k1, k2, k3, k4 = jax.random.split(key, 4)
        tokens = jax.random.normal(k1, (4, 512, HIDDEN), dtype=jnp.float32)
        bound = 1.0 / np.sqrt(HIDDEN)
        router_w = jax.random.uniform(k2, (NUM_EXPERTS, HIDDEN), jnp.float32, -bound, bound)
        router_b = jax.random.uniform(k3, (NUM_EXPERTS,), jnp.float32, -bound, bound)
        expert_w = jax.random.normal(k4, (NUM_EXPERTS, HIDDEN, HIDDEN), dtype=jnp.float32) / np.sqrt(HIDDEN)
        return {'tokens': tokens, 'router_w': router_w, 'router_b': router_b, 'expert_w': expert_w}
    _L0_ffn_in = _L0_ffn_setup()
    _d = {'L0_attn_a_x': _L0_attn_a_in['x'], 'L0_attn_a_in_proj_w': _L0_attn_a_in['in_proj_w'], 'L0_attn_a_in_proj_b': _L0_attn_a_in['in_proj_b'], 'L0_attn_a_conv_w': _L0_attn_a_in['conv_w'], 'L0_attn_a_conv_b': _L0_attn_a_in['conv_b'], 'L0_attn_a_x_proj_w': _L0_attn_a_in['x_proj_w'], 'L0_attn_a_x_proj_b': _L0_attn_a_in['x_proj_b'], 'L0_attn_a_dt_proj_w': _L0_attn_a_in['dt_proj_w'], 'L0_attn_a_dt_proj_b': _L0_attn_a_in['dt_proj_b'], 'L0_attn_a_A_log': _L0_attn_a_in['A_log'], 'L0_attn_a_D_param': _L0_attn_a_in['D_param'], 'L0_attn_a_out_proj_w': _L0_attn_a_in['out_proj_w'], 'L0_attn_a_out_proj_b': _L0_attn_a_in['out_proj_b'], 'L0_attn_a_norm_alpha': _L0_attn_a_in['norm_alpha'], 'L0_attn_a_norm_bias': _L0_attn_a_in['norm_bias'], 'L0_attn_a_in_norm_alpha': _L0_attn_a_in['in_norm_alpha'], 'L0_attn_a_in_norm_bias': _L0_attn_a_in['in_norm_bias'], 'L0_attn_b_Wq': _L0_attn_b_in['Wq'], 'L0_attn_b_bq': _L0_attn_b_in['bq'], 'L0_attn_b_Wk': _L0_attn_b_in['Wk'], 'L0_attn_b_bk': _L0_attn_b_in['bk'], 'L0_attn_b_Wv': _L0_attn_b_in['Wv'], 'L0_attn_b_bv': _L0_attn_b_in['bv'], 'L0_attn_b_Wo': _L0_attn_b_in['Wo'], 'L0_attn_b_bo': _L0_attn_b_in['bo'], 'L0_ffn_router_w': _L0_ffn_in['router_w'], 'L0_ffn_router_b': _L0_ffn_in['router_b'], 'L0_ffn_expert_w': _L0_ffn_in['expert_w']}
    _x0 = _d['L0_attn_a_x']
    _d['L0_attn_a_x'] = jax.random.normal(jax.random.fold_in(jax.random.key(seed), 1), (8, 1024, 256), dtype=_x0.dtype)
    del _x0
    return _d

def reference(L0_attn_a_x, L0_attn_a_in_proj_w, L0_attn_a_in_proj_b, L0_attn_a_conv_w, L0_attn_a_conv_b, L0_attn_a_x_proj_w, L0_attn_a_x_proj_b, L0_attn_a_dt_proj_w, L0_attn_a_dt_proj_b, L0_attn_a_A_log, L0_attn_a_D_param, L0_attn_a_out_proj_w, L0_attn_a_out_proj_b, L0_attn_a_norm_alpha, L0_attn_a_norm_bias, L0_attn_a_in_norm_alpha, L0_attn_a_in_norm_bias, L0_attn_b_Wq, L0_attn_b_bq, L0_attn_b_Wk, L0_attn_b_bk, L0_attn_b_Wv, L0_attn_b_bv, L0_attn_b_Wo, L0_attn_b_bo, L0_ffn_router_w, L0_ffn_router_b, L0_ffn_expert_w):

    def _L0_attn_a_ref(x, in_proj_w, in_proj_b, conv_w, conv_b, x_proj_w, x_proj_b, dt_proj_w, dt_proj_b, A_log, D_param, out_proj_w, out_proj_b, norm_alpha, norm_bias, in_norm_alpha, in_norm_bias):
        import jax, jax.numpy as jnp
        import numpy as np
        from jax import lax
        B_SZ, SEQ, D_MODEL = (4, 256, 256)
        D_STATE, D_CONV, EXPAND = (16, 4, 2)
        D_INNER = EXPAND * D_MODEL
        EPS = 1e-06

        def layernorm(x, alpha, bias):
            mean = x.mean(axis=-1, keepdims=True)
            std = jnp.sqrt(jnp.var(x, axis=-1, keepdims=True, ddof=1))
            return alpha * (x - mean) / (std + EPS) + bias

        def selective_scan(x_conv, delta, A, Bm, Cm, D_param):
            L = x_conv.shape[1]

            def step(h, inp):
                xt, dt, bt, ct, t = inp
                dA = jnp.exp(jnp.clip(dt[..., None] * A, -10.0, 0.0))
                dBx = dt[..., None] * bt[:, None, :] * xt[..., None]
                h = dA * h + dBx
                hn = jnp.clip(jnp.linalg.norm(h, axis=-1, keepdims=True), 1e-06, None)
                scale = jnp.where(hn > 10.0, 10.0 / hn, jnp.ones_like(hn))
                h = jnp.where(t % 16 == 15, h * scale, h)
                y = jnp.einsum('bn,ben->be', ct, h) + D_param * xt
                return (h, y)
            h0 = jnp.zeros((x_conv.shape[0], x_conv.shape[2], A.shape[1]), x_conv.dtype)
            xs = (x_conv.swapaxes(0, 1), delta.swapaxes(0, 1), Bm.swapaxes(0, 1), Cm.swapaxes(0, 1), jnp.arange(L))
            _, ys = lax.scan(step, h0, xs)
            return ys.swapaxes(0, 1)
        residual = x
        xn = layernorm(x, in_norm_alpha, in_norm_bias)
        xz = xn @ in_proj_w.T + in_proj_b
        x_in, z = jnp.split(xz, 2, axis=-1)
        xc = lax.conv_general_dilated(x_in.swapaxes(1, 2), conv_w, window_strides=(1,), padding=[(D_CONV - 1, 0)], feature_group_count=D_INNER, dimension_numbers=('NCH', 'OIH', 'NCH')) + conv_b[None, :, None]
        x_conv = jax.nn.silu(xc.swapaxes(1, 2))
        bc = x_conv @ x_proj_w.T + x_proj_b
        Bm, Cm = jnp.split(bc, 2, axis=-1)
        delta = jax.nn.softplus(x_conv @ dt_proj_w.T + dt_proj_b)
        delta = jnp.clip(delta, 0.0001, 10.0)
        A = -jnp.exp(A_log)
        y = selective_scan(x_conv, delta, A, Bm, Cm, D_param)
        y = y * jax.nn.silu(z)
        out = y @ out_proj_w.T + out_proj_b
        return layernorm(residual + out, norm_alpha, norm_bias)

    def _L0_attn_b_ref(x, Wq, bq, Wk, bk, Wv, bv, Wo, bo):
        import jax, jax.numpy as jnp
        import numpy as np
        B, L, D_MODEL, H = (4, 512, 256, 16)
        HD = D_MODEL // H
        EPS = 1e-06
        b, l, _ = x.shape
        s = l

        def proj(W, bias):
            return (x @ W.T + bias).reshape(b, l, H, HD).transpose(0, 2, 1, 3)
        q = jax.nn.sigmoid(proj(Wq, bq))
        k = jax.nn.sigmoid(proj(Wk, bk))
        v = proj(Wv, bv)
        sink_incoming = 1.0 / jnp.einsum('nhld,nhd->nhl', q + EPS, k.sum(axis=2) + EPS)
        source_outgoing = 1.0 / jnp.einsum('nhld,nhd->nhl', k + EPS, q.sum(axis=2) + EPS)
        conserved_sink = jnp.einsum('nhld,nhd->nhl', q + EPS, (k * source_outgoing[..., None]).sum(axis=2) + EPS)
        conserved_source = jnp.einsum('nhld,nhd->nhl', k + EPS, (q * sink_incoming[..., None]).sum(axis=2) + EPS)
        conserved_source = jnp.clip(conserved_source, -1.0, 1.0)
        sink_allocation = jax.nn.sigmoid(conserved_sink * (float(l) / float(s)))
        source_competition = jax.nn.softmax(conserved_source, axis=-1) * float(s)
        kv = jnp.einsum('nhld,nhlm->nhdm', k, v * source_competition[..., None])
        out = jnp.einsum('nhld,nhdm->nhlm', q * sink_incoming[..., None], kv)
        out = out * sink_allocation[..., None]
        out = out.transpose(0, 2, 1, 3).reshape(b, l, D_MODEL)
        return out @ Wo.T + bo

    def _L0_ffn_ref(tokens, router_w, router_b, expert_w):
        import jax, jax.numpy as jnp
        import numpy as np
        HIDDEN = 256
        NUM_EXPERTS = 16
        TOP_K = 6
        EPS = 1e-10
        B, S, H = tokens.shape
        E = expert_w.shape[0]
        T = B * S
        logits = jnp.einsum('bsh,eh->bse', tokens, router_w) + router_b
        probs = jax.nn.softmax(logits, axis=-1)
        top_p, top_i = jax.lax.top_k(probs, TOP_K)
        top_p = top_p / (jnp.sum(top_p, axis=-1, keepdims=True) + EPS)
        x = tokens.reshape(T, H)
        flat_i = top_i.reshape(T, TOP_K)
        flat_p = top_p.reshape(T, TOP_K)
        gate = jnp.zeros((T, E), dtype=flat_p.dtype)
        gate = gate.at[jnp.arange(T)[:, None], flat_i].add(flat_p)
        acc = jnp.maximum(jnp.sum(gate, axis=-1), EPS)
        out = jnp.zeros_like(x)
        for e in range(E):
            out = out + x @ expert_w[e] * gate[:, e:e + 1]
        out = (out / acc[:, None]).reshape(B, S, H)
        out = out + EPS * jnp.sum(top_p, axis=-1, keepdims=True)
        return out
    x = L0_attn_a_x
    x = x + _L0_attn_a_ref(_layernorm(x, axis=-1), L0_attn_a_in_proj_w, L0_attn_a_in_proj_b, L0_attn_a_conv_w, L0_attn_a_conv_b, L0_attn_a_x_proj_w, L0_attn_a_x_proj_b, L0_attn_a_dt_proj_w, L0_attn_a_dt_proj_b, L0_attn_a_A_log, L0_attn_a_D_param, L0_attn_a_out_proj_w, L0_attn_a_out_proj_b, L0_attn_a_norm_alpha, L0_attn_a_norm_bias, L0_attn_a_in_norm_alpha, L0_attn_a_in_norm_bias)
    x = x + _L0_ffn_ref(_layernorm(x, axis=-1), L0_ffn_router_w, L0_ffn_router_b, L0_ffn_expert_w)
    x = x + _L0_attn_b_ref(_layernorm(x, axis=-1), L0_attn_b_Wq, L0_attn_b_bq, L0_attn_b_Wk, L0_attn_b_bk, L0_attn_b_Wv, L0_attn_b_bv, L0_attn_b_Wo, L0_attn_b_bo)
    x = x + _L0_ffn_ref(_layernorm(x, axis=-1), L0_ffn_router_w, L0_ffn_router_b, L0_ffn_expert_w)
    return x

_drawn_inputs = setup_inputs


def setup_inputs(seed=0):
    import zlib

    import numpy as np

    out = dict(_drawn_inputs(seed))
    spreads = {'L0_attn_a_in_proj_b': (0.0, 0.8),
     'L0_attn_a_conv_b': (0.0, 0.8),
     'L0_attn_a_x_proj_b': (0.0, 0.8),
     'L0_attn_a_dt_proj_b': (0.0, 0.8),
     'L0_attn_a_D_param': (1.0, 0.6),
     'L0_attn_a_out_proj_b': (0.0, 0.1),
     'L0_attn_a_norm_alpha': (1.0, 0.2),
     'L0_attn_a_norm_bias': (0.0, 0.1),
     'L0_attn_a_in_norm_alpha': (1.0, 0.6),
     'L0_attn_a_in_norm_bias': (0.0, 0.8)}
    factors = {'L0_attn_a_in_proj_w': 7.559,
     'L0_attn_a_conv_w': 8.0,
     'L0_attn_a_x_proj_w': 8.0,
     'L0_attn_a_dt_proj_w': 8.0,
     'L0_attn_a_A_log': 8.0,
     'L0_attn_a_out_proj_w': 7.086,
     'L0_attn_b_Wq': 8.0,
     'L0_attn_b_bq': 8.0,
     'L0_attn_b_Wk': 6.878,
     'L0_attn_b_bk': 8.0,
     'L0_attn_b_bv': 6.72,
     'L0_attn_b_bo': 7.164}
    for name, (base, spread) in spreads.items():
        noise = np.random.default_rng([zlib.crc32(name.encode()), seed]).standard_normal(out[name].shape)
        drawn = base * np.exp(spread * noise) if base else spread * noise
        out[name] = jnp.asarray(drawn.astype(out[name].dtype))
    for name, factor in factors.items():
        out[name] = (out[name] * factor).astype(out[name].dtype)
    return out
```

```python
import math
from contextlib import ExitStack

import concourse.bass as bass
from concourse import mybir

NB, L, D = 8, 1024, 256
E, N, TAPS = 512, 16, 4
P = 128
NT = L // P
NTILES = NB * NT
KD, EB = D // P, E // P
CH = 16
NC = P // CH
SL = CH + 1
ST = EB * N
HT = P // 2
HC = NC // 2
QT = P // 4
QC = NC // 4
RB = 32
X, TOPK = 16, 6
ROUTER = 16
AHEAD = 64


def build(nc, dram, out):
    f32, bf16 = mybir.dt.float32, mybir.dt.bfloat16
    ALU, ACT, AX = mybir.AluOpType, mybir.ActivationFunctionType, mybir.AxisListType
    ctx = ExitStack()
    with ctx:
        def sb(name, shape, dt=f32):
            return ctx.enter_context(nc.sbuf_tensor(name, shape, dt))

        def sig(name):
            return ctx.enter_context(nc.semaphore(name))

        w_in = sb("w_in", [P, KD, 2 * E])
        w_dt = sb("w_dt", [P, EB, E])
        w_xp = sb("w_xp", [P, EB, 3 * RB])
        w_out = sb("w_out", [P, EB, D])
        w_r = sb("w_r", [P, KD, X])
        w_x = sb("w_x", [P, KD, X * D])
        ident = sb("ident", [P, P])
        self32 = sb("self32", [3 * RB, RB])
        sel = sb("sel", [3 * RB, RB], bf16)
        hmask = sb("hmask", [P, P])
        b_in = sb("b_in", [P, 2 * EB])
        cw = sb("cw", [P, EB, TAPS])
        cb = sb("cb", [P, EB])
        b_dt = sb("b_dt", [P, EB])
        dpar = sb("dpar", [P, EB])
        aneg = sb("aneg", [P, ST])
        b_xp = sb("b_xp", [3 * RB, 1])
        ga_in = sb("ga_in", [P, KD])
        be_in = sb("be_in", [P, KD])
        ob_row = sb("ob_row", [P, D])
        ga_row = sb("ga_row", [P, D])
        be_row = sb("be_row", [P, D])
        bo_row = sb("bo_row", [P, D])
        rb_row = sb("rb_row", [P, X])
        b_qkv = sb("b_qkv", [P, 3, KD])
        resident = [(w_in, "w_in"), (w_dt, "w_dt"), (w_xp, "w_xp"), (w_out, "w_out"), (w_r, "w_r"),
                    (w_x, "w_x"), (ident, "ident"), (self32, "sel"), (hmask, "hmask"), (b_in, "b_in"),
                    (cw, "cw"), (cb, "cb"), (b_dt, "b_dt"), (dpar, "dpar"), (aneg, "A_log"),
                    (b_xp, "b_xp"), (ga_in, "ga_in"), (be_in, "be_in"), (ob_row, "ob_row"),
                    (ga_row, "ga_row"), (be_row, "be_row"), (bo_row, "bo_row"), (rb_row, "rb_row"),
                    (b_qkv, "b_qkv")]
        c_one = sb("c_one", [P, 1])
        c_eps5 = sb("c_eps5", [P, 1])
        c_ln10 = sb("c_ln10", [P, 1])
        c_eps6 = sb("c_eps6", [P, 1])

        dA = [sb(f"dA{k}", [P, NC, ST, SL]) for k in range(2)]
        hb = [sb(f"hb{k}", [P, ST, SL]) for k in range(2)]
        prod = [sb(f"prod{k}", [P, N, EB, QT]) for k in range(2)]
        bbc = [sb(f"bbc{k}", [P, N, HT]) for k in range(2)]
        cbc = [sb(f"cbc{k}", [P, N, HT]) for k in range(2)]
        xt = [sb(f"xt{k}", [P, D]) for k in range(2)]
        y1 = [sb(f"y1{k}", [P, D]) for k in range(2)]
        x1b = [sb(f"x1b{k}", [P, D]) for k in range(2)]
        xn = sb("xn", [P, D])
        xnT = sb("xnT", [P, KD, P])
        xin = sb("xin", [P, EB, P + TAPS - 1])
        zb = sb("zb", [P, EB, P])
        sg = sb("sg", [P, EB, P])
        sz = [sb(f"sz{k}", [P, EB, P]) for k in range(1)] * 2
        xc = sb("xc", [P, EB, P])
        xcv = [sb(f"xcv{k}", [P, EB, P]) for k in range(1)] * 2
        dt = sb("dt", [P, EB, P])
        u = [sb(f"u{k}", [P, EB, P]) for k in range(1)] * 2
        bcv = sb("bcv", [3 * RB, P])
        bcs = sb("bcs", [3 * RB, P], bf16)
        yg = sb("yg", [P, EB, P])
        oo = sb("oo", [P, D])
        st = sb("st", [P, 4, 6])
        mv = sb("mv", [P, 4, 2])
        sc = sb("sc", [P, 16])
        sq = sb("sq", [P, ST])
        nrm = sb("nrm", [P, EB])
        mxt = [sb(f"mxt{k}", [P, D]) for k in range(2)]
        mxn = sb("mxn", [P, D])
        mxT = [sb(f"mxT{k}", [P, KD, P]) for k in range(2)]
        macc = [sb(f"macc{k}", [P, D]) for k in range(2)]
        mst = sb("mst", [P, 6])
        mmv = sb("mmv", [P, 2])
        ms = sb("ms", [P, 16])
        lgt = sb("lgt", [P, X])
        mx8 = sb("mx8", [P, 8])
        ex = sb("ex", [P, X])
        prx = sb("prx", [P, X + 2])
        t8 = sb("t8", [P, 8])
        rest = sb("rest", [P, X + 2])
        selp = sb("selp", [P, X])
        gate = [sb(f"gate{k}", [P, X]) for k in range(2)]
        big = [t[:].rearrange("p a b c -> p (a b c)") for t in dA]
        AW = KD * L

        def half_major(h, n):
            return big[h][:, n * AW:(n + 1) * AW].rearrange("p (j l) -> p j l", j=KD)
        xTa, qa, ka, va = (half_major(0, n) for n in range(4))
        r1, r2 = (half_major(1, n) for n in range(2))
        kv = big[1][:, 2 * AW:4 * AW].rearrange("p (t d) -> p t d", t=NT)
        w_a = prod[0][:].rearrange("p a b c -> p (a b c)").rearrange("p (w k d) -> p w k d", w=4, k=KD)
        mats = prod[1][:].rearrange("p a b c -> p (a b c)").rearrange("p (m c) -> p m c", c=P)
        ac = sb("ac", [P, 50])
        TG = 512
        NG = L // TG

        F0, F1, BC, YP, G0, G1, M0, M1 = (ctx.enter_context(nc.psum_tensor(f"ps{k}", [P, 512], f32)) for k in range(8))
        G = (G0, G1)

        s_w, s_setup, s_aexp, s_zero = sig("s_w"), sig("s_setup"), sig("s_aexp"), sig("s_zero")
        s_settle = sig("s_settle")

        dve_m = ("st1", "mv1", "y1", "st2", "mv2", "vc2", "se2", "r2", "xn", "xib", "zb", "zc", "conv", "carry", "xcc",
                 "bcv", "bch", "bcr", "bcm", "bcr2", "bcl", "dtb", "dtc", "dt", "clip", "scan", "sq", "nr", "nc",
                 "nm", "st0", "hs", "prod", "yd", "o1", "o2", "st3", "mv3", "vc3", "se3", "r3", "o3")
        act_m = ("ln1", "rs1", "ln2", "sd2", "xnTs", "ez", "lz", "ss", "ex", "lx", "sx", "bbs", "edt", "ldt", "dA", "nl",
                 "ne", "ln3", "sd3")
        pool_m = ("sz", "xcv", "u", "bt", "yg", "o4", "o5", "x1")
        pe_m = ("xnT", "xi", "z", "bc", "dtp", "bb", "y", "op")
        sp_m = ("x_even", "x_odd", "x1s_even", "x1s_odd")
        dve_x = ("st", "mv", "xn", "lgb", "nm", "router", "ac")
        act_x = ("ln", "rs", "xTs", "ex")
        pe_x = ("xT", "lg", "mm")
        sp_x = ("x_even", "x_odd", "o_even", "o_odd")
        dve_a = ("st", "mv", "xn", "qk1", "qk2", "hm", "cv", "qs", "ks", "s1", "s2", "hn", "cw", "cs", "cc", "mx", "nm",
                 "rs", "rl", "v", "kvm", "og", "x2", "x3")
        act_a = ("ln", "rn", "xTs", "pjs", "l1", "r1", "l2", "r2", "sa", "e", "kvs")
        pe_a = ("xT", "pj", "cv0", "si", "so", "cw0", "ci", "co", "kvT", "kv0", "om", "om2")
        sp_a = ("x_even", "x_odd", "o_even", "o_odd")
        A = {n: sig("a_" + n) for n in dve_a + act_a + pe_a + sp_a}
        s_wa = sig("s_wa")
        M = {n: sig("m_" + n) for n in dve_m + act_m + pool_m + pe_m + sp_m}
        R = {n: sig("x_" + n) for n in dve_x + act_x + pe_x + sp_x}
        for d, names in ((M, ("x", "x1s")), (R, ("x", "o")), (A, ("x", "o"))):
            for n in names:
                d[n] = (d[n + "_even"], d[n + "_odd"])

        def head_start(eng, *groups):
            for d, names in groups:
                for n in names:
                    eng.sem_inc(d[n], AHEAD)

        def tile_of(t, b, r):
            return t[bass.ds(b, 1), bass.ds(r * P, P), :].rearrange("a p d -> p (a d)")

        def tiles(eng, body):
            with eng.Fori(0, NB) as b:
                with eng.Fori(0, NT // 2) as h:
                    for k in range(2):
                        body(b * NT + h * 2 + k, k, b * (NT // 2) + h)

        def flat(t):
            return t[:].rearrange("p a b -> p (a b)")

        block = ctx.enter_context(nc.Block())
        x1d, x2d, x3d = dram["x1d"], dram["x2d"], dram["x3d"]

        @block.sync
        def _(sp):
            for t, n in resident:
                sp.dma_start(t[:], dram[n]).then_inc(s_w, 16)
            head_start(sp, (M, sp_m), (R, sp_x), (A, sp_a))

            with sp.Fori(0, NB) as b:
                with sp.Fori(0, NT // 2) as h:
                    i = b * NT + h * 2
                    for k in range(2):
                        sp.wait_ge(M["x1"], AHEAD + i + k - 1)
                        sp.dma_start(xt[k][:], tile_of(dram["x"], b, h * 2 + k)).then_inc(M["x"][k], 16)
                    for k in range(2):
                        sp.wait_ge(M["x1"], AHEAD + i + k + 1)
                        sp.dma_start(tile_of(x1d, b, h * 2 + k), x1b[k][:]).then_inc(M["x1s"][k], 16)
            for k in range(2):
                sp.wait_ge(M["x1s"][k], AHEAD + NTILES // 2 * 16)

            def experts(src, dst, n0):
                with sp.Fori(0, NB) as b:
                    with sp.Fori(0, NT // 2) as h:
                        n = b * NT + h * 2 + n0
                        for k in range(2):
                            sp.wait_ge(R["ac"], AHEAD + (n + k - 2) * (X + 1) + 1)
                            sp.dma_start(mxt[k][:], tile_of(src, b, h * 2 + k)).then_inc(R["x"][k], 16)
                        for k in range(2):
                            sp.wait_ge(R["ac"], AHEAD + (n + k + 1) * (X + 1))
                            sp.dma_start(tile_of(dst, b, h * 2 + k), macc[k][:]).then_inc(R["o"][k], 16)
                for k in range(2):
                    sp.wait_ge(R["o"][k], AHEAD + (NTILES + n0) // 2 * 16)
            experts(x1d, x2d, 0)

            sp.dma_start(w_a, dram["w_qkvo"]).then_inc(s_wa, 16)
            with sp.Fori(0, NB) as b:
                for m in range(2 * NT):
                    if m < 2:
                        sp.wait_ge(A["x3"], AHEAD + b * NT + m - 1)
                    elif m < NT + 2:
                        sp.wait_ge(A["xn"], AHEAD + b * NT + m - 1)
                    else:
                        sp.wait_ge(A["x3"], AHEAD + b * NT + m - NT - 1)
                    sp.dma_start(xt[m % 2][:], tile_of(x2d, b, m % NT)).then_inc(A["x"][m % 2], 16)
                    if m >= NT + 1:
                        t = m - NT - 1
                        sp.wait_ge(A["x3"], AHEAD + b * NT + t + 1)
                        sp.dma_start(tile_of(x3d, b, t), x1b[t % 2][:]).then_inc(A["o"][t % 2], 16)
                sp.wait_ge(A["x3"], AHEAD + (b + 1) * NT)
                sp.dma_start(tile_of(x3d, b, NT - 1), x1b[(NT - 1) % 2][:]).then_inc(A["o"][(NT - 1) % 2], 16)
            for k in range(2):
                sp.wait_ge(A["o"][k], AHEAD + NTILES // 2 * 16)
            experts(x3d, out, NTILES)

        @block.gpsimd
        def _(g):
            head_start(g, (M, pool_m))
            TT = nc.gpsimd.tensor_tensor

            def front(i, k):
                g.wait_ge(M["zc"], AHEAD + i + 1)
                g.wait_ge(M["ss"], AHEAD + i + 1)
                TT(sz[k][:], zb[:], sg[:], ALU.mult).then_inc(M["sz"], 1)
                g.wait_ge(M["xcc"], AHEAD + i + 1)
                g.wait_ge(M["sx"], AHEAD + i + 1)
                TT(xcv[k][:], xc[:], sg[:], ALU.mult).then_inc(M["xcv"], 1)
                g.wait_ge(M["xcv"], AHEAD + i + 1)
                g.wait_ge(M["dt"], AHEAD + i + 1)
                TT(u[k][:], dt[:], xcv[k][:], ALU.mult).then_inc(M["u"], 1)

            def scan(i, k):
                g.wait_ge(M["u"], AHEAD + i + 1)
                for c in range(NC):
                    q = i * NC + c
                    half = c // HC
                    g.wait_ge(M["bbs"], AHEAD + i * NC + half * 4 + 2)
                    g.wait_ge(M["prod"], AHEAD + q - 1)
                    t0 = c * CH
                    TT(hb[c % 2][:].rearrange("p (e n) s -> p e n s", e=EB)[:, :, :, 1:SL],
                       u[k][:, :, t0:t0 + CH].rearrange("p e (n s) -> p e n s", n=1).broadcast_to([P, EB, N, CH]),
                       bbc[half][:, :, t0 - half * HT:t0 - half * HT + CH].rearrange("p (e n) s -> p e n s", e=1)
                       .broadcast_to([P, EB, N, CH]), ALU.mult).then_inc(M["bt"], 1)

            def back(i, k, j):
                g.wait_ge(M["yd"], AHEAD + (i + 1) * EB)
                TT(yg[:], yg[:], sz[k][:], ALU.mult).then_inc(M["yg"], 1)
                g.wait_ge(M["o3"], AHEAD + i + 1)
                TT(oo[:], oo[:], ga_row[:], ALU.mult).then_inc(M["o4"], 1)
                g.wait_ge(M["o4"], AHEAD + i + 1)
                TT(oo[:], oo[:], be_row[:], ALU.add).then_inc(M["o5"], 1)
                g.wait_ge(M["o5"], AHEAD + i + 1)
                g.wait_ge(M["x1s"][k], AHEAD + j * 16)
                TT(x1b[k][:], oo[:], xt[k][:], ALU.add).then_inc(M["x1"], 1)

            def tile(i, k, j):
                front(i, k)
                scan(i, k)
                back(i, k, j)
            g.wait_ge(s_w, 16 * len(resident))
            tiles(g, tile)

        @block.scalar
        def _(a):
            act = nc.scalar.activation
            nc.scalar.preload_act_table_set("natural_log_exp_and_others")
            head_start(a, (M, act_m), (R, act_x), (A, act_a))
            a.wait_ge(s_w, 16 * len(resident))
            a.wait_ge(s_setup, 1)
            act(aneg[:], aneg[:], ACT.Exp).then_inc(s_aexp, 1)
            a.wait_ge(s_setup, 3)

            def sigmoid(src, i, e, l, s):
                act(sg[:], src[:], ACT.Exp, scale=-1.0).then_inc(M[e], 1)
                a.wait_ge(M[e], AHEAD + i + 1)
                act(sg[:], sg[:], ACT.Ln, bias=c_one[:]).then_inc(M[l], 1)
                a.wait_ge(M[l], AHEAD + i + 1)
                act(sg[:], sg[:], ACT.Exp, scale=-1.0).then_inc(M[s], 1)

            def front(i, k):
                a.wait_ge(M["mv1"], AHEAD + i + 1)
                act(sc[:, 0:1], mv[:, 0, 1:2], ACT.Ln, bias=c_eps5[:]).then_inc(M["ln1"], 1)
                a.wait_ge(M["ln1"], AHEAD + i + 1)
                act(sc[:, 1:2], sc[:, 0:1], ACT.Exp, scale=-0.5).then_inc(M["rs1"], 1)
                a.wait_ge(M["vc2"], AHEAD + i + 1)
                act(sc[:, 3:4], sc[:, 2:3], ACT.Ln).then_inc(M["ln2"], 1)
                a.wait_ge(M["ln2"], AHEAD + i + 1)
                act(sc[:, 4:5], sc[:, 3:4], ACT.Exp, scale=0.5).then_inc(M["sd2"], 1)
                a.wait_ge(M["xnT"], AHEAD + i + 1)
                a.wait_ge(M["z"], AHEAD + i)
                for j in range(KD):
                    act(xnT[:, j, :], F0[:, j * P:(j + 1) * P], ACT.Identity, bias=be_in[:, j:j + 1],
                        scale=ga_in[:, j:j + 1]).then_inc(M["xnTs"], 1)
                a.wait_ge(M["zc"], AHEAD + i + 1)
                a.wait_ge(M["xcv"], AHEAD + i)
                sigmoid(zb, i, "ez", "lz", "ss")
                a.wait_ge(M["xcc"], AHEAD + i + 1)
                a.wait_ge(M["sz"], AHEAD + i + 1)
                sigmoid(xc, i, "ex", "lx", "sx")
                a.wait_ge(M["dtc"], AHEAD + i + 1)
                act(dt[:], dt[:], ACT.Exp).then_inc(M["edt"], 1)
                a.wait_ge(M["edt"], AHEAD + i + 1)
                act(dt[:], dt[:], ACT.Ln, bias=c_one[:]).then_inc(M["ldt"], 1)
                for h in range(2):
                    a.wait_ge(M["bt"], AHEAD + (i - 1) * NC + (h + 1) * HC)
                    a.wait_ge(M["prod"], AHEAD + (i - 1) * NC + (h + 1) * HC)
                    for q in range(4):
                        a.wait_ge(M["bb"], AHEAD + i * 8 + h * 4 + q + 1)
                        dst = (bbc, cbc)[q // 2][h]
                        act(dst[:, (q % 2) * 8:(q % 2) * 8 + 8, :], BC[:].rearrange("p (n t) -> p n t", n=8), ACT.Copy)\
                            .then_inc(M["bbs"], 1)
                a.wait_ge(M["dt"], AHEAD + i + 1)
                a.wait_ge(M["scan"], AHEAD + (i - 1) * NC)
                for e in range(EB):
                    for n in range(N):
                        s = e * N + n
                        last = act(dA[k][:, :, s, 1:SL], dt[:, e, :].rearrange("p (c s) -> p c s", c=NC), ACT.Exp,
                                   scale=aneg[:, s:s + 1])
                last.then_inc(M["dA"], 1)

            def scan(i, k):
                for c in range(NC):
                    q = i * NC + c
                    a.wait_ge(M["nc"], AHEAD + q + 1)
                    act(nrm[:], nrm[:], ACT.Ln).then_inc(M["nl"], 1)
                    a.wait_ge(M["nl"], AHEAD + q + 1)
                    act(nrm[:], nrm[:], ACT.Exp, scale=-0.5, bias=c_ln10[:]).then_inc(M["ne"], 1)

            def back(i, k):
                a.wait_ge(M["vc3"], AHEAD + i + 1)
                act(sc[:, 8:9], sc[:, 7:8], ACT.Ln).then_inc(M["ln3"], 1)
                a.wait_ge(M["ln3"], AHEAD + i + 1)
                act(sc[:, 9:10], sc[:, 8:9], ACT.Exp, scale=0.5).then_inc(M["sd3"], 1)

            def tile(i, k, j):
                front(i, k)
                scan(i, k)
                back(i, k)
            tiles(a, tile)

            def experts(n0):
                def tile(i, k, j):
                    n = i + n0
                    a.wait_ge(R["mv"], AHEAD + n + 1)
                    act(ms[:, 0:1], mmv[:, 1:2], ACT.Ln, bias=c_eps5[:]).then_inc(R["ln"], 1)
                    a.wait_ge(R["ln"], AHEAD + n + 1)
                    act(ms[:, 1:2], ms[:, 0:1], ACT.Exp, scale=-0.5).then_inc(R["rs"], 1)
                    a.wait_ge(R["xT"], AHEAD + n + 1)
                    a.wait_ge(R["mm"], AHEAD + (n - 1) * 8)
                    act(flat(mxT[k]), M0[:, 0:D], ACT.Copy).then_inc(R["xTs"], 1)
                    a.wait_ge(R["nm"], AHEAD + n + 1)
                    act(ex[:], lgt[:], ACT.Exp, bias=ms[:, 2:3], accum_out=ms[:, 3:4]).then_inc(R["ex"], 1)
                tiles(a, tile)
            experts(0)

            with a.Fori(0, NB) as b:
                for t in range(NT):
                    n = b * NT + t
                    a.wait_ge(A["mv"], AHEAD + n + 1)
                    act(ms[:, 0:1], mmv[:, 1:2], ACT.Ln, bias=c_eps5[:]).then_inc(A["ln"], 1)
                    a.wait_ge(A["ln"], AHEAD + n + 1)
                    act(ms[:, 1:2], ms[:, 0:1], ACT.Exp, scale=-0.5).then_inc(A["rn"], 1)
                    a.wait_ge(A["xT"], AHEAD + n + 1)
                    act(xTa[:, :, t * P:(t + 1) * P], (F0, F1)[t % 2][:, 0:D].rearrange("p (j l) -> p j l", j=KD), ACT.Copy)\
                        .then_inc(A["xTs"], 1)
                for w, dst in ((0, qa), (1, ka), (2, va)):
                    for j in range(KD):
                        for g in range(NG):
                            m = (w * KD + j) * NG + g
                            a.wait_ge(A["pj"], AHEAD + b * 12 + m + 1)
                            s = (BC, YP, G0, G1)[m % 4]
                            o = dst[:, j, g * TG:(g + 1) * TG]
                            if w < 2:
                                act(o, s[:], ACT.Sigmoid, bias=b_qkv[:, w, j:j + 1],
                                    accum_out=ac[:, m:m + 1]).then_inc(A["pjs"], 1)
                            else:
                                act(o, s[:], ACT.Identity, bias=b_qkv[:, w, j:j + 1]).then_inc(A["pjs"], 1)
                nc.scalar.preload_act_table_set("natural_log_exp_and_others")
                a.wait_ge(A["cv"], AHEAD + b + 1)
                for banks, dst, mmd, l, r, c0 in (((BC, YP, G0, G1), r1, "si", "l1", "r1", 16),
                                                  ((F0, F1, M0, M1), r2, "so", "l2", "r2", 18)):
                    for m in range(4):
                        j, g = m // NG, m % NG
                        a.wait_ge(A[mmd], AHEAD + b * 4 + m + 1)
                        act(dst[:, j, g * TG:(g + 1) * TG], banks[m][:], ACT.Ln, bias=ac[:, c0 + j:c0 + j + 1])\
                            .then_inc(A[l], 1)
                    for m in range(4):
                        j, g = m // NG, m % NG
                        a.wait_ge(A[l], AHEAD + b * 4 + m + 1)
                        o = dst[:, j, g * TG:(g + 1) * TG]
                        act(o, o, ACT.Exp, scale=-1.0).then_inc(A[r], 1)
                for j in range(KD):
                    a.wait_ge(A["nm"], AHEAD + b + 1)
                    act(xTa[:, j, :], xTa[:, j, :], ACT.Exp, bias=ac[:, 42 + j:43 + j], accum_out=ac[:, 44 + j:45 + j])\
                        .then_inc(A["e"], 1)
                for m in range(4):
                    j, g = m // NG, m % NG
                    a.wait_ge(A["ci"], AHEAD + b * 4 + m + 1)
                    act(r2[:, j, g * TG:(g + 1) * TG], (BC, YP, G0, G1)[m][:], ACT.Sigmoid, bias=ac[:, 36 + j:37 + j])\
                        .then_inc(A["sa"], 1)
                for t in range(NT):
                    a.wait_ge(A["kvT"], AHEAD + b * NT + t + 1)
                    act(kv[:, t, :], (BC, YP, G0, G1)[t % 4][:], ACT.Copy).then_inc(A["kvs"], 1)
                nc.scalar.preload_act_table_set("natural_log_exp_and_others")
            experts(NTILES)

        @block.tensor
        def _(pe):
            mm = nc.tensor.matmul
            head_start(pe, (M, pe_m), (R, pe_x), (A, pe_a))
            pe.wait_ge(s_w, 16 * len(resident))

            def front(i, k):
                pe.wait_ge(M["xn"], AHEAD + i + 1)
                pe.wait_ge(M["o1"], AHEAD + i)
                for j in range(KD):
                    last = nc.tensor.transpose(F0[:, j * P:(j + 1) * P], xn[:, j * P:(j + 1) * P], ident[:])
                last.then_inc(M["xnT"], 1)
                pe.wait_ge(M["xnTs"], AHEAD + (i + 1) * KD)
                pe.wait_ge(M["bcv"], AHEAD + i)
                for half, bank, s in ((0, F0, "xi"), (1, F1, "z")):
                    for m in range(EB):
                        for j in range(KD):
                            last = mm(bank[:, m * P:(m + 1) * P], w_in[:, j, (half * EB + m) * P:(half * EB + m + 1) * P],
                                      xnT[:, j, :], start=(j == 0), stop=(j == KD - 1))
                    last.then_inc(M[s], 1)
                pe.wait_ge(M["xcv"], AHEAD + i + 1)
                pe.wait_ge(M["zb"], AHEAD + i + 1)
                for e in range(EB):
                    last = mm(F1[0:3 * RB, 0:P], w_xp[:, e, :], xcv[k][:, e, :], start=(e == 0), stop=(e == EB - 1))
                last.then_inc(M["bc"], 1)
                pe.wait_ge(M["xib"], AHEAD + i + 1)
                for m in range(EB):
                    for e in range(EB):
                        last = mm(F0[:, m * P:(m + 1) * P], w_dt[:, e, m * P:(m + 1) * P], xcv[k][:, e, :],
                                  start=(e == 0), stop=(e == EB - 1))
                last.then_inc(M["dtp"], 1)
                pe.wait_ge(M["bcl"], AHEAD + i + 1)
                pe.wait_ge(s_setup, 3)
                for h in range(2):
                    for q in range(4):
                        pe.wait_ge(M["bbs"], AHEAD + i * 8 + h * 4 + q)
                        for n in range(8):
                            last = mm(BC[:, n * HT:(n + 1) * HT], sel[:, q * 8 + n:q * 8 + n + 1].broadcast_to([3 * RB, P]), bcs[:, h * HT:(h + 1) * HT],
                                      start=True, stop=True)
                        last.then_inc(M["bb"], 1)

            def scan(i, k):
                for h in range(4):
                    pe.wait_ge(M["prod"], AHEAD + i * NC + (h + 1) * QC)
                    pe.wait_ge(M["yd"], AHEAD + i * EB)
                    for n in range(N):
                        last = mm(YP[:, h * P:(h + 1) * P], ident[:],
                                  prod[h % 2][:, n, :, :].rearrange("p e t -> p (e t)"), start=(n == 0), stop=(n == N - 1))
                    last.then_inc(M["y"], 1)

            def back(i, k):
                pe.wait_ge(M["yg"], AHEAD + i + 1)
                pe.wait_ge(M["dtb"], AHEAD + i + 1)
                for e in range(EB):
                    last = mm(F0[:, 0:D], yg[:, e, :], w_out[:, e, :], start=(e == 0), stop=(e == EB - 1))
                last.then_inc(M["op"], 1)

            def tile(i, k, j):
                front(i, k)
                scan(i, k)
                back(i, k)
            tiles(pe, tile)

            def experts(n0):
                def tile(i, k, j):
                    n = i + n0
                    pe.wait_ge(R["xn"], AHEAD + n + 1)
                    pe.wait_ge(R["lgb"], AHEAD + n)
                    for j in range(KD):
                        last = nc.tensor.transpose(M0[:, j * P:(j + 1) * P], mxn[:, j * P:(j + 1) * P], ident[:])
                    last.then_inc(R["xT"], 1)
                    pe.wait_ge(R["xTs"], AHEAD + n + 1)
                    for j in range(KD):
                        last = mm(M0[:, D:D + X], mxT[k][:, j, :], w_r[:, j, :], start=(j == 0), stop=(j == KD - 1))
                    last.then_inc(R["lg"], 1)
                    for p in range(X // 2):
                        pe.wait_ge(R["ac"], AHEAD + n * (X + 1) + (2 * p - 1 if p >= 2 else 2 * p + 15 - (X + 1)))
                        for j in range(KD):
                            last = mm(G[p % 2][:], mxT[k][:, j, :], w_x[:, j, p * 512:(p + 1) * 512],
                                      start=(j == 0), stop=(j == KD - 1))
                        last.then_inc(R["mm"], 1)
                tiles(pe, tile)
            experts(0)

            pe.wait_ge(s_wa, 16)
            quads = ((BC, YP, G0, G1), (F0, F1, M0, M1))

            def by_group(banks, mats_, src, s, before):
                for m in range(4):
                    j, g = m // NG, m % NG
                    before(m)
                    mm(banks[m][:], mats_[j], src[:, j, g * TG:(g + 1) * TG], start=True, stop=True).then_inc(A[s], 1)

            with pe.Fori(0, NB) as b:
                for t in range(NT):
                    n = b * NT + t
                    pe.wait_ge(A["xn"], AHEAD + n + 1)
                    if t < 2:
                        pe.wait_ge(A["x3"], AHEAD + b * NT)
                    else:
                        pe.wait_ge(A["xTs"], AHEAD + n - 1)
                    for j in range(KD):
                        last = nc.tensor.transpose((F0, F1)[t % 2][:, j * P:(j + 1) * P], mxn[:, j * P:(j + 1) * P], ident[:])
                    last.then_inc(A["xT"], 1)
                pe.wait_ge(A["xTs"], AHEAD + (b + 1) * NT)
                for w in range(3):
                    for j in range(KD):
                        for g in range(NG):
                            m = (w * KD + j) * NG + g
                            if m >= 4:
                                pe.wait_ge(A["pjs"], AHEAD + b * 12 + m - 3)
                            for kk in range(KD):
                                last = mm(quads[0][m % 4][:], w_a[:, w, kk, j * P:(j + 1) * P],
                                          xTa[:, kk, g * TG:(g + 1) * TG], start=(kk == 0), stop=(kk == KD - 1))
                            last.then_inc(A["pj"], 1)
                pe.wait_ge(A["hm"], AHEAD + (b + 1) * 4)
                for m in range(4):
                    last = mm(M0[:, m:m + 1], mats[:, m, :], c_eps6[:], start=True, stop=True)
                last.then_inc(A["cv0"], 1)
                by_group(quads[0], (mats[:, 0, :], mats[:, 1, :]), qa, "si",
                         lambda m: pe.wait_ge(A["pjs"], AHEAD + (b + 1) * 12))
                by_group(quads[1], (mats[:, 2, :], mats[:, 3, :]), ka, "so",
                         lambda m: pe.wait_ge(A["cv"], AHEAD + b + 1))
                pe.wait_ge(A["hn"], AHEAD + (b + 1) * 4)
                pe.wait_ge(A["l2"], AHEAD + (b + 1) * 4)
                for m in range(4):
                    last = mm(M0[:, m:m + 1], mats[:, 4 + m, :], c_eps6[:], start=True, stop=True)
                last.then_inc(A["cw0"], 1)
                by_group(quads[0], (mats[:, 4, :], mats[:, 5, :]), qa, "ci",
                         lambda m: pe.wait_ge(A["l1"], AHEAD + (b + 1) * 4))
                by_group(quads[1], (mats[:, 6, :], mats[:, 7, :]), ka, "co",
                         lambda m: pe.wait_ge(A["cw"], AHEAD + b + 1))
                pe.wait_ge(A["v"], AHEAD + (b + 1) * KD)
                for t in range(NT):
                    if t < 4:
                        pe.wait_ge(A["sa"], AHEAD + b * 4 + t + 1)
                    else:
                        pe.wait_ge(A["kvs"], AHEAD + b * NT + t - 3)
                    for c, src in enumerate((ka, va)):
                        for j in range(KD):
                            last = nc.tensor.transpose(quads[0][t % 4][:, (c * KD + j) * P:(c * KD + j + 1) * P],
                                                       src[:, j, t * P:(t + 1) * P], ident[:])
                    last.then_inc(A["kvT"], 1)
                pe.wait_ge(A["kvs"], AHEAD + (b + 1) * NT)
                pe.wait_ge(A["cc"], AHEAD + b + 1)
                for j in range(KD):
                    for t in range(NT):
                        last = mm(M0[:, j * P:(j + 1) * P], kv[:, t, j * P:(j + 1) * P], kv[:, t, D + j * P:D + (j + 1) * P],
                                  start=(t == 0), stop=(t == NT - 1))
                last.then_inc(A["kv0"], 1)
                pe.wait_ge(A["kvm"], AHEAD + (b + 1) * KD)
                by_group((F0, F1, M1, G1), (mats[:, 8, :], mats[:, 9, :]), r1, "om",
                         lambda m: None)
                for t in range(NT):
                    if t < 2:
                        pe.wait_ge(A["og"], AHEAD + (b + 1) * 4)
                    pe.wait_ge(A["x2"], AHEAD + b * NT + t - 1)
                    for j in range(KD):
                        last = mm((BC, YP)[t % 2][:, 0:D], r2[:, j, t * P:(t + 1) * P], w_a[:, 3, j, :],
                                  start=(j == 0), stop=(j == KD - 1))
                    last.then_inc(A["om2"], 1)
            experts(NTILES)

        @block.vector
        def _(v):
            V = nc.vector
            TT, TS, STT = V.tensor_tensor, V.tensor_scalar, V.scalar_tensor_tensor
            head_start(v, (M, dve_m), (R, dve_x), (A, dve_a))
            for c, val in ((c_one, 1.0), (c_eps5, 1e-5), (c_ln10, math.log(10.0)), (c_eps6, 1e-6), (prx[:, X:X + 2], -1.0)):
                V.memset(c[:] if c is not prx else c, val)
            for k in range(2):
                last = V.memset(dA[k][:, :, :, 0:1], 0.0)
            last.then_inc(s_setup, 1)
            v.wait_ge(s_w, 16 * len(resident))
            v.wait_ge(s_aexp, 1)
            V.tensor_copy(sel[:], self32[:]).then_inc(s_setup, 1)
            TS(aneg[:], aneg[:], -1.0, None, ALU.mult).then_inc(s_setup, 1)

            def settle():
                v.sem_inc(s_settle, 1)

            def stats(src, j, s1, s2, i):
                V.bn_stats(st[:, j, :], src).then_inc(M[s1], 1)
                v.wait_ge(M[s1], AHEAD + i + 1)
                settle()
                V.bn_aggr(mv[:, j, :], st[:, j, :]).then_inc(M[s2], 1)
                v.wait_ge(M[s2], AHEAD + i + 1)

            def unbiased(j, c, vc, i):
                TS(sc[:, c:c + 1], mv[:, j, 1:2], D / (D - 1.0), 1e-19, ALU.mult, ALU.max).then_inc(M[vc], 1)

            def one_over_std(c, sd, se, r, i):
                v.wait_ge(M[sd], AHEAD + i + 1)
                TS(sc[:, c + 3:c + 4], sc[:, c + 2:c + 3], 1e-6, None, ALU.add).then_inc(M[se], 1)
                v.wait_ge(M[se], AHEAD + i + 1)
                V.reciprocal(sc[:, c + 4:c + 5], sc[:, c + 3:c + 4]).then_inc(M[r], 1)
                v.wait_ge(M[r], AHEAD + i + 1)

            def bias4(t):
                return t.rearrange("p (e t) -> p e t", t=1).broadcast_to([P, EB, P])

            def bank4(t):
                return t[:].rearrange("p (e t) -> p e t", e=EB)

            def front(i, k, j):
                v.wait_ge(M["x"][k], AHEAD + (j + 1) * 16)
                stats(xt[k][:], 0, "st1", "mv1", i)
                v.wait_ge(M["rs1"], AHEAD + i + 1)
                TS(y1[k][:], xt[k][:], mv[:, 0, 0:1], sc[:, 1:2], ALU.subtract, ALU.mult).then_inc(M["y1"], 1)
                v.wait_ge(M["y1"], AHEAD + i + 1)
                stats(y1[k][:], 1, "st2", "mv2", i)
                unbiased(1, 2, "vc2", i)
                one_over_std(2, "sd2", "se2", "r2", i)
                v.wait_ge(M["xnT"], AHEAD + i)
                TS(xn[:], y1[k][:], mv[:, 1, 0:1], sc[:, 6:7], ALU.subtract, ALU.mult).then_inc(M["xn"], 1)
                v.wait_ge(M["xi"], AHEAD + i + 1)
                v.wait_ge(M["carry"], AHEAD + i)
                TT(xin[:, :, TAPS - 1:], bank4(F0), bias4(b_in[:, 0:EB]), ALU.add).then_inc(M["xib"], 1)
                v.wait_ge(M["z"], AHEAD + i + 1)
                v.wait_ge(M["sz"], AHEAD + i)
                TT(zb[:], bank4(F1), bias4(b_in[:, EB:]), ALU.add).then_inc(M["zb"], 1)
                v.wait_ge(M["zb"], AHEAD + i + 1)
                TS(zb[:], zb[:], -40.0, None, ALU.max).then_inc(M["zc"], 1)
                v.wait_ge(M["xib"], AHEAD + i + 1)
                v.wait_ge(M["xcv"], AHEAD + i)
                for j in range(TAPS):
                    for e in range(EB):
                        if j == 0:
                            ins = TS(xc[:, e, :], xin[:, e, 0:P], cw[:, e, 0:1], cb[:, e:e + 1], ALU.mult, ALU.add)
                        else:
                            v.wait_ge(M["conv"], AHEAD + (i * TAPS + j - 1) * EB + e + 1)
                            ins = STT(xc[:, e, :], xin[:, e, j:j + P], cw[:, e, j:j + 1], xc[:, e, :], ALU.mult, ALU.add)
                        ins.then_inc(M["conv"], 1)
                V.tensor_copy(xin[:, :, 0:TAPS - 1], xin[:, :, P:]).then_inc(M["carry"], 1)
                v.wait_ge(M["conv"], AHEAD + (i + 1) * TAPS * EB)
                TS(xc[:], xc[:], -40.0, None, ALU.max).then_inc(M["xcc"], 1)
                v.wait_ge(M["bc"], AHEAD + i + 1)
                TS(bcv[:], F1[0:3 * RB, 0:P], b_xp[:], None, ALU.add).then_inc(M["bcv"], 1)
                v.wait_ge(M["bcv"], AHEAD + i + 1)
                v.wait_ge(M["bb"], AHEAD + i * 8)
                V.tensor_copy(bcs[:], bcv[:]).then_inc(M["bch"], 1)
                v.wait_ge(M["bch"], AHEAD + i + 1)
                TT(bcv[:], bcv[:], bcs[:], ALU.subtract).then_inc(M["bcr"], 1)
                v.wait_ge(M["bcr"], AHEAD + i + 1)
                V.tensor_copy(bcs[RB:2 * RB, :], bcv[RB:2 * RB, :]).then_inc(M["bcm"], 1)
                V.tensor_copy(bcs[2 * RB:, :], bcv[2 * RB:, :]).then_inc(M["bcm"], 1)
                v.wait_ge(M["bcm"], AHEAD + (i + 1) * 2)
                TT(bcv[2 * RB:, :], bcv[2 * RB:, :], bcs[2 * RB:, :], ALU.subtract).then_inc(M["bcr2"], 1)
                v.wait_ge(M["bcr2"], AHEAD + i + 1)
                V.tensor_copy(bcs[2 * RB:, :], bcv[2 * RB:, :]).then_inc(M["bcl"], 1)
                v.wait_ge(M["dtp"], AHEAD + i + 1)
                v.wait_ge(M["dA"], AHEAD + i)
                v.wait_ge(M["u"], AHEAD + i)
                TT(dt[:], bank4(F0), bias4(b_dt[:]), ALU.add).then_inc(M["dtb"], 1)
                v.wait_ge(M["dtb"], AHEAD + i + 1)
                TS(dt[:], dt[:], 40.0, None, ALU.min).then_inc(M["dtc"], 1)
                v.wait_ge(M["ldt"], AHEAD + i + 1)
                TS(dt[:], dt[:], 1e-4, 10.0, ALU.max, ALU.min).then_inc(M["dt"], 1)

            def scan(i, k):
                v.wait_ge(M["dA"], AHEAD + i + 1)
                for c in range(NC):
                    q = i * NC + c
                    h = c // HC
                    cur, nxt = hb[c % 2], hb[(c + 1) % 2]
                    TS(dA[k][:, c, :, 1:SL], dA[k][:, c, :, 1:SL], math.exp(-10.0), None, ALU.max).then_inc(M["clip"], 1)
                    v.wait_ge(M["clip"], AHEAD + q + 1)
                    v.wait_ge(M["bt"], AHEAD + q + 1)
                    v.wait_ge(M["st0"], AHEAD + q)
                    hf = cur[:].rearrange("p a b -> p (a b)")
                    V.tensor_tensor_scan(hf, dA[k][:, c, :, :].rearrange("p a b -> p (a b)"), hf, 0.0, ALU.mult,
                                             ALU.add).then_inc(M["scan"], 1)
                    v.wait_ge(M["scan"], AHEAD + q + 1)
                    end = cur[:, :, CH:SL].rearrange("p a b -> p (a b)")
                    TT(sq[:], end, end, ALU.mult).then_inc(M["sq"], 1)
                    v.wait_ge(M["sq"], AHEAD + q + 1)
                    V.tensor_reduce(nrm[:], sq[:].rearrange("p (e n) -> p e n", e=EB), AX.X, ALU.add).then_inc(M["nr"], 1)
                    v.wait_ge(M["nr"], AHEAD + q + 1)
                    TS(nrm[:], nrm[:], 1e-12, None, ALU.max).then_inc(M["nc"], 1)
                    v.wait_ge(M["ne"], AHEAD + q + 1)
                    TS(nrm[:], nrm[:], 1.0, None, ALU.min).then_inc(M["nm"], 1)
                    v.wait_ge(M["nm"], AHEAD + q + 1)
                    e3 = cur[:, :, CH:SL].rearrange("p (e n) s -> p e (n s)", e=EB)
                    s3 = nrm[:].rearrange("p (e t) -> p e t", t=1).broadcast_to([P, EB, N])
                    TT(nxt[:, :, 0:1].rearrange("p (e n) s -> p e (n s)", e=EB), e3, s3, ALU.mult).then_inc(M["st0"], 1)
                    TT(e3, e3, s3, ALU.mult).then_inc(M["hs"], 1)
                    v.wait_ge(M["hs"], AHEAD + q + 1)
                    v.wait_ge(M["bbs"], AHEAD + i * 8 + h * 4 + 4)
                    v.wait_ge(M["y"], AHEAD + i * 4 + c // QC - 1)
                    t0, tq = (c % HC) * CH, (c % QC) * CH
                    TT(prod[(c // QC) % 2][:].rearrange("p n e t -> p e n t")[:, :, :, tq:tq + CH],
                           cur[:].rearrange("p (e n) s -> p e n s", e=EB)[:, :, :, 1:SL],
                           cbc[h][:, :, t0:t0 + CH].rearrange("p (e n) s -> p e n s", e=1).broadcast_to([P, EB, N, CH]),
                           ALU.mult).then_inc(M["prod"], 1)

            def back(i, k):
                v.wait_ge(M["y"], AHEAD + (i + 1) * 4)
                v.wait_ge(M["op"], AHEAD + i)
                for e in range(EB):
                    STT(yg[:, e, :].rearrange("p (h t) -> p h t", h=4),
                            xcv[k][:, e, :].rearrange("p (h t) -> p h t", h=4), dpar[:, e:e + 1],
                            YP[:].rearrange("p (h e t) -> p h e t", h=4, e=EB)[:, :, e, :], ALU.mult, ALU.add).then_inc(M["yd"], 1)
                v.wait_ge(M["op"], AHEAD + i + 1)
                v.wait_ge(M["x1"], AHEAD + i)
                TT(oo[:], F0[:, 0:D], ob_row[:], ALU.add).then_inc(M["o1"], 1)
                v.wait_ge(M["o1"], AHEAD + i + 1)
                TT(oo[:], oo[:], y1[k][:], ALU.add).then_inc(M["o2"], 1)
                v.wait_ge(M["o2"], AHEAD + i + 1)
                stats(oo[:], 2, "st3", "mv3", i)
                unbiased(2, 7, "vc3", i)
                one_over_std(7, "sd3", "se3", "r3", i)
                TS(oo[:], oo[:], mv[:, 2, 0:1], sc[:, 11:12], ALU.subtract, ALU.mult).then_inc(M["o3"], 1)

            with v.Fori(0, NB) as b:
                V.memset(xin[:, :, 0:TAPS - 1], 0.0)
                V.memset(hb[0][:, :, 0:1], 0.0).then_inc(s_zero, 1)
                with v.Fori(0, NT // 2) as h:
                    v.wait_ge(s_zero, b + 1)
                    for k in range(2):
                        i = b * NT + h * 2 + k
                        front(i, k, b * (NT // 2) + h)
                        scan(i, k)
                        back(i, k)

            def experts(n0):
                def tile(i, k, j):
                    n = i + n0

                    v.wait_ge(R["x"][k], AHEAD + (j + 1 + n0 // 2) * 16)
                    V.bn_stats(mst[:], mxt[k][:]).then_inc(R["st"], 1)
                    v.wait_ge(R["st"], AHEAD + n + 1)
                    settle()
                    V.bn_aggr(mmv[:], mst[:]).then_inc(R["mv"], 1)
                    v.wait_ge(R["mv"], AHEAD + n + 1)
                    v.wait_ge(R["rs"], AHEAD + n + 1)
                    v.wait_ge(R["xT"], AHEAD + n)
                    TS(mxn[:], mxt[k][:], mmv[:, 0:1], ms[:, 1:2], ALU.subtract, ALU.mult).then_inc(R["xn"], 1)
                    v.wait_ge(R["xn"], AHEAD + n + 1)
                    v.wait_ge(R["lg"], AHEAD + n + 1)
                    TT(lgt[:], M0[:, D:D + X], rb_row[:], ALU.add).then_inc(R["lgb"], 1)
                    v.wait_ge(R["lgb"], AHEAD + n + 1)
                    settle()
                    V.max(mx8[:], lgt[:]).then_inc(R["router"], 1)
                    v.wait_ge(R["router"], AHEAD + n * ROUTER + 1)
                    TS(ms[:, 2:3], mx8[:, 0:1], -1.0, None, ALU.mult).then_inc(R["nm"], 1)
                    v.wait_ge(R["nm"], AHEAD + n + 1)
                    v.wait_ge(R["ex"], AHEAD + n + 1)
                    V.reciprocal(ms[:, 4:5], ms[:, 3:4]).then_inc(R["router"], 1)
                    v.wait_ge(R["router"], AHEAD + n * ROUTER + 2)
                    TS(prx[:, 0:X], ex[:], ms[:, 4:5], None, ALU.mult).then_inc(R["router"], 1)
                    v.wait_ge(R["router"], AHEAD + n * ROUTER + 3)
                    settle()
                    V.max(t8[:], prx[:, 0:X]).then_inc(R["router"], 1)
                    v.wait_ge(R["router"], AHEAD + n * ROUTER + 4)
                    V.memset(t8[:, TOPK:8], -1.0).then_inc(R["router"], 1)
                    v.wait_ge(R["router"], AHEAD + n * ROUTER + 5)
                    settle()
                    V.match_replace(rest[:], t8[:], prx[:], 0.0).then_inc(R["router"], 1)
                    v.wait_ge(R["router"], AHEAD + n * ROUTER + 6)
                    TT(selp[:], prx[:, 0:X], rest[:, 0:X], ALU.subtract).then_inc(R["router"], 1)
                    v.wait_ge(R["router"], AHEAD + n * ROUTER + 7)
                    V.tensor_reduce(ms[:, 5:6], selp[:], AX.X, ALU.add).then_inc(R["router"], 1)
                    v.wait_ge(R["router"], AHEAD + n * ROUTER + 8)
                    TS(ms[:, 6:7], ms[:, 5:6], 1e-10, None, ALU.add).then_inc(R["router"], 1)
                    v.wait_ge(R["router"], AHEAD + n * ROUTER + 9)
                    V.reciprocal(ms[:, 7:8], ms[:, 6:7]).then_inc(R["router"], 1)
                    v.wait_ge(R["router"], AHEAD + n * ROUTER + 10)
                    TT(ms[:, 8:9], ms[:, 5:6], ms[:, 7:8], ALU.mult).then_inc(R["router"], 1)
                    v.wait_ge(R["router"], AHEAD + n * ROUTER + 11)
                    TS(ms[:, 9:10], ms[:, 8:9], 1e-10, None, ALU.max).then_inc(R["router"], 1)
                    v.wait_ge(R["router"], AHEAD + n * ROUTER + 12)
                    V.reciprocal(ms[:, 10:11], ms[:, 9:10]).then_inc(R["router"], 1)
                    v.wait_ge(R["router"], AHEAD + n * ROUTER + 13)
                    TT(ms[:, 11:12], ms[:, 7:8], ms[:, 10:11], ALU.mult).then_inc(R["router"], 1)
                    v.wait_ge(R["router"], AHEAD + n * ROUTER + 14)
                    TS(gate[k][:], selp[:], ms[:, 11:12], None, ALU.mult).then_inc(R["router"], 1)
                    v.wait_ge(R["router"], AHEAD + n * ROUTER + 15)
                    TS(ms[:, 12:13], ms[:, 8:9], 1e-10, None, ALU.mult).then_inc(R["router"], 1)
                    v.wait_ge(R["router"], AHEAD + n * ROUTER + 16)
                    v.wait_ge(R["o"][k], AHEAD + (j + n0 // 2) * 16)
                    TS(macc[k][:], mxt[k][:], ms[:, 12:13], None, ALU.add).then_inc(R["ac"], 1)
                    for e in range(X):
                        v.wait_ge(R["mm"], AHEAD + n * 8 + e // 2 + 1)
                        v.wait_ge(R["ac"], AHEAD + n * (X + 1) + 1 + e)
                        STT(macc[k][:], G[(e // 2) % 2][:, (e % 2) * D:(e % 2 + 1) * D], gate[k][:, e:e + 1], macc[k][:],
                            ALU.mult, ALU.add).then_inc(R["ac"], 1)
                tiles(v, tile)
            experts(0)

            def columns(first, last):
                return ac[:, first:last]

            with v.Fori(0, NB) as b:
                for t in range(NT):
                    n = b * NT + t
                    v.wait_ge(A["x"][t % 2], AHEAD + (b * NT + t // 2 + 1) * 16)
                    V.bn_stats(mst[:], xt[t % 2][:]).then_inc(A["st"], 1)
                    v.wait_ge(A["st"], AHEAD + n + 1)
                    settle()
                    V.bn_aggr(mmv[:], mst[:]).then_inc(A["mv"], 1)
                    v.wait_ge(A["rn"], AHEAD + n + 1)
                    v.wait_ge(A["xT"], AHEAD + n)
                    TS(mxn[:], xt[t % 2][:], mmv[:, 0:1], ms[:, 1:2], ALU.subtract, ALU.mult).then_inc(A["xn"], 1)
                v.wait_ge(A["pjs"], AHEAD + b * 12 + 8)
                V.tensor_reduce(columns(8, 12), columns(0, 8).rearrange("p (a g) -> p a g", g=NG), AX.X, ALU.add).then_inc(A["qk1"], 1)
                v.wait_ge(A["qk1"], AHEAD + b + 1)
                TS(columns(12, 16), columns(8, 12), 1e-6, None, ALU.add).then_inc(A["qk2"], 1)
                v.wait_ge(A["qk2"], AHEAD + b + 1)
                for m, c in enumerate((14, 15, 12, 13)):
                    TS(mats[:, m, :], hmask[:], columns(c, c + 1), None, ALU.mult).then_inc(A["hm"], 1)
                v.wait_ge(A["cv0"], AHEAD + b + 1)
                V.tensor_copy(columns(16, 20), M0[:, 0:4]).then_inc(A["cv"], 1)
                for src, dst, r, s, c0 in ((qa, r1, "r1", "qs", 20), (ka, r2, "r2", "ks", 24)):
                    for m in range(4):
                        j, g = m // NG, m % NG
                        v.wait_ge(A[r], AHEAD + b * 4 + m + 1)
                        o = dst[:, j, g * TG:(g + 1) * TG]
                        STT(o, src[:, j, g * TG:(g + 1) * TG], 1.0, o, ALU.mult, ALU.mult,
                                accum_out=columns(c0 + m, c0 + m + 1)).then_inc(A[s], 1)
                v.wait_ge(A["qs"], AHEAD + (b + 1) * 4)
                v.wait_ge(A["ks"], AHEAD + (b + 1) * 4)
                V.tensor_reduce(columns(28, 32), columns(20, 28).rearrange("p (a g) -> p a g", g=NG), AX.X, ALU.add).then_inc(A["s1"], 1)
                v.wait_ge(A["s1"], AHEAD + b + 1)
                TS(columns(32, 36), columns(28, 32), 1e-6, None, ALU.add).then_inc(A["s2"], 1)
                v.wait_ge(A["s2"], AHEAD + b + 1)
                for m, c in enumerate((34, 35, 32, 33)):
                    TS(mats[:, 4 + m, :], hmask[:], columns(c, c + 1), None, ALU.mult).then_inc(A["hn"], 1)
                v.wait_ge(A["cw0"], AHEAD + b + 1)
                V.tensor_copy(columns(36, 40), M0[:, 0:4]).then_inc(A["cw"], 1)
                v.wait_ge(A["cw"], AHEAD + b + 1)
                for m in range(4):
                    j, g = m // NG, m % NG
                    v.wait_ge(A["co"], AHEAD + b * 4 + m + 1)
                    TS(xTa[:, j, g * TG:(g + 1) * TG], (F0, F1, M0, M1)[m][:], columns(38 + j, 39 + j), 1.0, ALU.add, ALU.min).then_inc(A["cs"], 1)
                v.wait_ge(A["cs"], AHEAD + (b + 1) * 4)
                TS(xTa, xTa, -1.0, None, ALU.max).then_inc(A["cc"], 1)
                v.wait_ge(A["cc"], AHEAD + b + 1)
                V.tensor_reduce(columns(40, 42), xTa, AX.X, ALU.max).then_inc(A["mx"], 1)
                v.wait_ge(A["mx"], AHEAD + b + 1)
                TS(columns(42, 44), columns(40, 42), -1.0, None, ALU.mult).then_inc(A["nm"], 1)
                v.wait_ge(A["e"], AHEAD + (b + 1) * KD)
                V.reciprocal(columns(46, 48), columns(44, 46)).then_inc(A["rs"], 1)
                v.wait_ge(A["rs"], AHEAD + b + 1)
                TS(columns(48, 50), columns(46, 48), float(L), None, ALU.mult).then_inc(A["rl"], 1)
                v.wait_ge(A["rl"], AHEAD + b + 1)
                for j in range(KD):
                    STT(va[:, j, :], xTa[:, j, :], columns(48 + j, 49 + j), va[:, j, :], ALU.mult, ALU.mult).then_inc(A["v"], 1)
                v.wait_ge(A["kv0"], AHEAD + b + 1)
                for j in range(KD):
                    TT(mats[:, 8 + j, :], M0[:, j * P:(j + 1) * P], hmask[:], ALU.mult).then_inc(A["kvm"], 1)
                for m in range(4):
                    j, g = m // NG, m % NG
                    v.wait_ge(A["om"], AHEAD + b * 4 + m + 1)
                    o = r2[:, j, g * TG:(g + 1) * TG]
                    TT(o, (F0, F1, M1, G1)[m][:], o, ALU.mult).then_inc(A["og"], 1)
                for t in range(NT):
                    n = b * NT + t
                    v.wait_ge(A["om2"], AHEAD + n + 1)
                    v.wait_ge(A["x"][t % 2], AHEAD + (b * NT + NT // 2 + t // 2 + 1) * 16)
                    v.wait_ge(A["o"][t % 2], AHEAD + (b * (NT // 2) + t // 2) * 16)
                    TT(x1b[t % 2][:], (BC, YP)[t % 2][:, 0:D], bo_row[:], ALU.add).then_inc(A["x2"], 1)
                    v.wait_ge(A["x2"], AHEAD + n + 1)
                    TT(x1b[t % 2][:], x1b[t % 2][:], xt[t % 2][:], ALU.add).then_inc(A["x3"], 1)
            experts(NTILES)


def _param(a, blocks):
    import numpy as np
    return np.ascontiguousarray(a.reshape(blocks, P, -1).transpose(1, 0, 2))


def layout(i):
    import numpy as np
    g = {k.replace("L0_", ""): np.asarray(v) for k, v in i.items()}
    row = lambda a: np.ascontiguousarray(np.broadcast_to(a, (P, a.shape[0])))
    col = lambda a: np.ascontiguousarray(a.reshape(-1, P).T)
    sel = np.tile(np.eye(RB, dtype=np.float32), (3, 1))
    hmask = np.kron(np.eye(P // 16), np.ones((16, 16))).astype(np.float32)
    xw = g["ffn_expert_w"]
    return {
        "x": g["attn_a_x"],
        "w_in": _param(g["attn_a_in_proj_w"].T, KD), "w_dt": _param(g["attn_a_dt_proj_w"].T, EB),
        "w_xp": _param(np.tile(g["attn_a_x_proj_w"].T, (1, 3)), EB), "w_out": _param(g["attn_a_out_proj_w"].T, EB),
        "w_r": _param(g["ffn_router_w"].T, KD),
        "w_x": np.ascontiguousarray(xw.reshape(X, KD, P, D).transpose(2, 1, 0, 3)).reshape(P, KD, X * D),
        "ident": np.eye(P, dtype=np.float32), "sel": sel, "hmask": hmask,
        "b_in": col(g["attn_a_in_proj_b"]), "cw": _param(g["attn_a_conv_w"].reshape(E, TAPS), EB),
        "cb": col(g["attn_a_conv_b"]), "b_dt": col(g["attn_a_dt_proj_b"]), "dpar": col(g["attn_a_D_param"]),
        "A_log": _param(g["attn_a_A_log"], EB).reshape(P, ST),
        "b_xp": np.tile(g["attn_a_x_proj_b"], 3).reshape(3 * RB, 1),
        "ga_in": col(g["attn_a_in_norm_alpha"]), "be_in": col(g["attn_a_in_norm_bias"]),
        "ob_row": row(g["attn_a_out_proj_b"]), "ga_row": row(g["attn_a_norm_alpha"]), "be_row": row(g["attn_a_norm_bias"]),
        "bo_row": row(g["attn_b_bo"]), "rb_row": row(g["ffn_router_b"]),
        "b_qkv": np.ascontiguousarray(np.stack([col(g[f"attn_b_b{c}"]) for c in "qkv"], 1)),
        "w_qkvo": np.ascontiguousarray(np.stack([_param(g[f"attn_b_W{c}"].T, KD) for c in "qkvo"], 1)),
    }


def kernel(**inputs):
    import numpy as _np
    import concourse.bacc as _bacc
    from concourse import mybir as _mybir
    from concourse.bass_utils import run_bass_kernel_spmd as _run

    nc = _bacc.Bacc("TRN2", target_bir_lowering=False, num_devices=1)
    arrays, dram = {}, {}
    for name, a in layout(inputs).items():
        a = _np.ascontiguousarray(a)
        arrays[f"in_{name}"] = a
        dram[name] = nc.dram_tensor(f"in_{name}", a.shape, _mybir.dt.from_np(a.dtype), kind="ExternalInput").ap()
    for name in ("x1d", "x2d", "x3d"):
        dram[name] = nc.dram_tensor(name, (NB, L, D), _mybir.dt.float32, kind="Internal").ap()
    out = nc.dram_tensor("out_dram", (NB, L, D), _mybir.dt.float32, kind="ExternalOutput").ap()
    build(nc, dram, out)
    r = _run(nc, [arrays], core_ids=[0])
    return r.results[0]["out_dram"]
```

```python
import math
from contextlib import ExitStack

import concourse.bass as bass
from concourse import mybir

NB, L, D = 8, 1024, 256
E, N, TAPS = 512, 16, 4
P = 128
NT = L // P
NTILES = NB * NT
KD, EB = D // P, E // P
CH = 16
NC = P // CH
SL = CH + 1
ST = EB * N
HT = P // 2
HC = NC // 2
QT = P // 4
QC = NC // 4
RB = 32
X, TOPK = 16, 6
ROUTER = 16
PV = (3, 7)
PP = (0, 1, 2, 4, 5, 6)
DECAYS = (0, 0, 0, 0, 12, 28, 42, 54, 64)
EARLY = (0, 2)
AHEAD = 64


def build(nc, dram, out):
    f32, bf16 = mybir.dt.float32, mybir.dt.bfloat16
    ALU, ACT, AX = mybir.AluOpType, mybir.ActivationFunctionType, mybir.AxisListType
    ctx = ExitStack()
    with ctx:
        def sb(name, shape, dt=f32):
            return ctx.enter_context(nc.sbuf_tensor(name, shape, dt))

        def sig(name):
            return ctx.enter_context(nc.semaphore(name))

        w_in = sb("w_in", [P, KD, 2 * E])
        w_dt = sb("w_dt", [P, EB, E])
        w_xp = sb("w_xp", [P, EB, 3 * RB])
        w_out = sb("w_out", [P, EB, D])
        w_r = sb("w_r", [P, KD, X])
        w_x = sb("w_x", [P, KD, X * D])
        ident = sb("ident", [P, P])
        self32 = sb("self32", [3 * RB, RB])
        sel = sb("sel", [3 * RB, RB], bf16)
        hmask = sb("hmask", [P, P])
        b_in = sb("b_in", [P, 2 * EB])
        cw = sb("cw", [P, EB, TAPS])
        cb = sb("cb", [P, EB])
        b_dt = sb("b_dt", [P, EB])
        dpar = sb("dpar", [P, EB])
        aneg = sb("aneg", [P, ST])
        b_xp = sb("b_xp", [3 * RB, 1])
        ga_in = sb("ga_in", [P, KD])
        be_in = sb("be_in", [P, KD])
        ob_row = sb("ob_row", [P, D])
        ga_row = sb("ga_row", [P, D])
        be_row = sb("be_row", [P, D])
        bo_row = sb("bo_row", [P, D])
        rb_row = sb("rb_row", [P, X])
        b_qkv = sb("b_qkv", [P, 3, KD])
        resident = [(w_in, "w_in"), (w_dt, "w_dt"), (w_xp, "w_xp"), (w_out, "w_out"), (w_r, "w_r"),
                    (w_x, "w_x"), (ident, "ident"), (self32, "sel"), (hmask, "hmask"), (b_in, "b_in"),
                    (cw, "cw"), (cb, "cb"), (b_dt, "b_dt"), (dpar, "dpar"), (aneg, "A_log"),
                    (b_xp, "b_xp"), (ga_in, "ga_in"), (be_in, "be_in"), (ob_row, "ob_row"),
                    (ga_row, "ga_row"), (be_row, "be_row"), (bo_row, "bo_row"), (rb_row, "rb_row"),
                    (b_qkv, "b_qkv")]
        c_one = sb("c_one", [P, 1])
        c_eps5 = sb("c_eps5", [P, 1])
        c_ln10 = sb("c_ln10", [P, 1])
        c_eps6 = sb("c_eps6", [P, 1])
        c_tiny = sb("c_tiny", [P, 1])

        dA = [sb(f"dA{k}", [P, NC, ST, SL]) for k in range(2)]
        hb = [sb(f"hb{k}", [P, ST, SL]) for k in range(2)]
        prod = [sb(f"prod{k}", [P, N, EB, QT]) for k in range(2)]
        bbc = [sb(f"bbc{k}", [P, N, HT]) for k in range(2)]
        cbc = [sb(f"cbc{k}", [P, N, HT]) for k in range(2)]
        xt = [sb(f"xt{k}", [P, D]) for k in range(2)]
        y1 = sb("y1", [P, D])
        yr = sb("yr", [P, D])
        x1b = [sb(f"x1b{k}", [P, D]) for k in range(2)]
        xn = sb("xn", [P, D])
        xnT = sb("xnT", [P, KD, P])
        xin = sb("xin", [P, EB, P + TAPS - 1])
        sg = sb("sg", [P, EB, P])
        sz = [sb(f"sz{k}", [P, EB, P]) for k in range(2)]
        xcv = sb("xcv", [P, EB, P])
        xd = [sb(f"xd{k}", [P, EB, P]) for k in range(2)]
        dt = sb("dt", [P, EB, P])
        u = [sb(f"u{k}", [P, EB, P]) for k in range(2)]
        bcv = sb("bcv", [3 * RB, P])
        bcs = sb("bcs", [3 * RB, P], bf16)
        oo = sb("oo", [P, D])
        st = sb("st", [P, 4, 6])
        mv = sb("mv", [P, 4, 2])
        ln1 = [sb(f"ln1{k}", [P, 2]) for k in range(2)]
        ln1r = [sb(f"ln1r{k}", [P, 2]) for k in range(2)]
        carry = sb("carry", [P, NT // 2])
        sc = sb("sc", [P, 16])
        sq = sb("sq", [P, ST])
        nrm = sb("nrm", [P, EB])
        mxt = x1b
        mxn = sb("mxn", [P, D])
        mxT = [sb(f"mxT{k}", [P, KD, P]) for k in range(2)]
        macc = [sb(f"macc{k}", [P, D]) for k in range(2)]
        mst = sb("mst", [P, 6])
        mmv = sb("mmv", [P, 2])
        ms = sb("ms", [P, 16])
        lgt = sb("lgt", [P, X])
        mx8 = sb("mx8", [P, 8])
        ex = sb("ex", [P, X])
        prx = sb("prx", [P, X + 2])
        t8 = sb("t8", [P, 8])
        rest = sb("rest", [P, X + 2])
        selp = sb("selp", [P, X])
        gate = [sb(f"gate{k}", [P, X]) for k in range(2)]
        big = [t[:].rearrange("p a b c -> p (a b c)") for t in dA]
        AW = KD * L

        def half_major(h, n):
            return big[h][:, n * AW:(n + 1) * AW].rearrange("p (j l) -> p j l", j=KD)
        xTa, qa, ka, va = (half_major(0, n) for n in range(4))
        r1, r2 = (half_major(1, n) for n in range(2))
        kv = big[1][:, 2 * AW:4 * AW].rearrange("p (t d) -> p t d", t=NT)
        w_a = prod[0][:].rearrange("p a b c -> p (a b c)").rearrange("p (w k d) -> p w k d", w=4, k=KD)
        mats = prod[1][:].rearrange("p a b c -> p (a b c)").rearrange("p (m c) -> p m c", c=P)
        ac = sb("ac", [P, 50])
        TG = 512
        NG = L // TG

        F0, F1, BC, YP, G0, G1, M0, M1 = (ctx.enter_context(nc.psum_tensor(f"ps{k}", [P, 512], f32)) for k in range(8))
        G = (G0, G1)
        XP = 512 - P

        s_w, s_setup, s_aexp, s_zero = sig("s_w"), sig("s_setup"), sig("s_aexp"), sig("s_zero")
        s_settle = sig("s_settle")
        s_zero2 = sig("s_zero2")

        dve_m = ("st1", "mv1", "y1", "st2", "mv2", "vc2", "se2", "r2", "xn", "keep", "xib", "zb", "zc", "conv", "carry",
                 "xcc", "bcv", "bch", "bcr", "bcm", "bcr2", "bcl", "dtb", "dtc", "dt", "xd", "clip", "scan", "sq", "nr",
                 "st0", "hs", "prodv", "yd", "yr", "o1", "o2", "st3", "mv3", "vc3", "se3", "r3", "o3")
        act_m = ("ln1", "rs1", "ln2", "sd2", "xnTs", "ez", "lz", "ss", "ex", "lx", "sx", "bbs", "edt", "ldt", "dA", "nl",
                 "ne", "ln3", "sd3")
        pool_m = ("sz", "xcv", "u", "bt", "prodp", "yg", "o4", "o5", "x1")
        pe_m = ("xnT", "xi", "z", "bc", "dtp", "bb", "y", "op")
        sp_m = ("x", "xr")
        dve_x = ("st", "mv", "xn", "lgb", "nm", "router", "ac")
        act_x = ("ln", "rs", "xTs", "ex")
        pe_x = ("xT", "lg", "mm")
        sp_x = ("x_even", "x_odd", "o_even", "o_odd")
        dve_a = ("st", "mv", "xn", "qk1", "qk2", "hm", "cv", "qs", "ks", "s1", "s2", "hn", "cw", "cs", "cc", "mx", "nm",
                 "rs", "rl", "v", "kvm", "og", "x2", "x3")
        act_a = ("ln", "rn", "xTs", "pjs", "l1", "r1", "l2", "r2", "sa", "e", "kvs")
        pe_a = ("xT", "pj", "cv0", "si", "so", "cw0", "ci", "co", "kvT", "kv0", "om", "om2")
        sp_a = ("x_even", "x_odd", "o_even", "o_odd")
        A = {n: sig("a_" + n) for n in dve_a + act_a + pe_a + sp_a}
        s_wa = sig("s_wa")
        M = {n: sig("m_" + n) for n in dve_m + act_m + pool_m + pe_m + sp_m}
        R = {n: sig("x_" + n) for n in dve_x + act_x + pe_x + sp_x}
        for d, names in ((R, ("x", "o")), (A, ("x", "o"))):
            for n in names:
                d[n] = (d[n + "_even"], d[n + "_odd"])

        def head_start(eng, *groups):
            for d, names in groups:
                for n in names:
                    eng.sem_inc(d[n], AHEAD)

        def tile_of(t, b, r):
            return t[bass.ds(b, 1), bass.ds(r * P, P), :].rearrange("a p d -> p (a d)")

        def flat_tile(t, i):
            v = t.rearrange("b (t p) d -> (b t) p d", p=P)
            return v[bass.ds(i, 1), :, :].rearrange("a p d -> p (a d)")

        def pipeline(eng, step):
            for i, stages in ((-2, "L"), (-1, "LF"), (0, "LFS"), (1, "LFSB"), (2, "LFSBX"), (3, "LFSBXY")):
                step(i, i % 2, stages)
            with eng.Fori(2, NTILES // 2 - 1) as j:
                for k in range(2):
                    step(j * 2 + k, k, "LFSBXY")
            for i, stages in ((NTILES - 2, "FSBXY"), (NTILES - 1, "SBXY"), (NTILES, "BXY"), (NTILES + 1, "XY"),
                              (NTILES + 2, "Y")):
                step(i, i % 2, stages)

        def products_done(eng, i, c):
            eng.wait_ge(M["prodv"], AHEAD + i * len(PV) + len([x for x in PV if x <= c]))
            eng.wait_ge(M["prodp"], AHEAD + i * len(PP) + len([x for x in PP if x <= c]))

        def tiles(eng, body):
            with eng.Fori(0, NB) as b:
                with eng.Fori(0, NT // 2) as h:
                    for k in range(2):
                        body(b * NT + h * 2 + k, k, b * (NT // 2) + h)

        def flat(t):
            return t[:].rearrange("p a b -> p (a b)")

        def chunk_product(i, c):
            t0, tq = (c % HC) * CH, (c % QC) * CH
            return (prod[(c // QC) % 2][:].rearrange("p n e t -> p e n t")[:, :, :, tq:tq + CH],
                    hb[c % 2][:].rearrange("p (e n) s -> p e n s", e=EB)[:, :, :, 1:SL],
                    cbc[c // HC][:, :, t0:t0 + CH].rearrange("p (e n) s -> p e n s", e=1).broadcast_to([P, EB, N, CH]))

        block = ctx.enter_context(nc.Block())
        x1d, x2d, x3d = dram["x1d"], dram["x2d"], dram["x3d"]

        @block.sync
        def _(sp):
            for t, n in resident:
                sp.dma_start(t[:], dram[n]).then_inc(s_w, 16)
            head_start(sp, (M, sp_m), (R, sp_x), (A, sp_a))

            def step(i, k, stages):
                if "L" in stages:
                    sp.wait_ge(M["y1"], AHEAD + i + 2)
                    sp.dma_start(xt[0][:], flat_tile(dram["x"], i + 2)).then_inc(M["x"], 16)
                if "B" in stages:
                    sp.wait_ge(M["x1"], AHEAD + i - 1)
                    sp.dma_start(xt[1][:], flat_tile(dram["x"], i - 1)).then_inc(M["xr"], 16)
                if "Y" in stages:
                    sp.wait_ge(R["ac"], AHEAD + (i - 2) * (X + 1))
                    sp.dma_start(flat_tile(x2d, i - 3), macc[1 - k][:]).then_inc(R["o"][1 - k], 16)
            pipeline(sp, step)
            for k in range(2):
                sp.wait_ge(R["o"][k], AHEAD + NTILES // 2 * 16)

            def experts(src, dst, n0):
                with sp.Fori(0, NB) as b:
                    with sp.Fori(0, NT // 2) as h:
                        n = b * NT + h * 2 + n0
                        for k in range(2):
                            sp.wait_ge(R["ac"], AHEAD + (n + k - 2) * (X + 1) + 1)
                            sp.dma_start(mxt[k][:], tile_of(src, b, h * 2 + k)).then_inc(R["x"][k], 16)
                        for k in range(2):
                            sp.wait_ge(R["ac"], AHEAD + (n + k + 1) * (X + 1))
                            sp.dma_start(tile_of(dst, b, h * 2 + k), macc[k][:]).then_inc(R["o"][k], 16)
                for k in range(2):
                    sp.wait_ge(R["o"][k], AHEAD + (NTILES + n0) // 2 * 16)
            sp.dma_start(w_a, dram["w_qkvo"]).then_inc(s_wa, 16)
            with sp.Fori(0, NB) as b:
                for m in range(2 * NT):
                    if m < 2:
                        sp.wait_ge(A["x3"], AHEAD + b * NT + m - 1)
                    elif m < NT + 2:
                        sp.wait_ge(A["xn"], AHEAD + b * NT + m - 1)
                    else:
                        sp.wait_ge(A["x3"], AHEAD + b * NT + m - NT - 1)
                    sp.dma_start(xt[m % 2][:], tile_of(x2d, b, m % NT)).then_inc(A["x"][m % 2], 16)
                    if m >= NT + 1:
                        t = m - NT - 1
                        sp.wait_ge(A["x3"], AHEAD + b * NT + t + 1)
                        sp.dma_start(tile_of(x3d, b, t), x1b[t % 2][:]).then_inc(A["o"][t % 2], 16)
                sp.wait_ge(A["x3"], AHEAD + (b + 1) * NT)
                sp.dma_start(tile_of(x3d, b, NT - 1), x1b[(NT - 1) % 2][:]).then_inc(A["o"][(NT - 1) % 2], 16)
            for k in range(2):
                sp.wait_ge(A["o"][k], AHEAD + NTILES // 2 * 16)
            experts(x3d, out, NTILES)

        @block.gpsimd
        def _(g):
            head_start(g, (M, pool_m))
            TT = nc.gpsimd.tensor_tensor

            def product(i, k, c):
                g.wait_ge(M["hs"], AHEAD + i * NC + c + 1)
                g.wait_ge(M["bbs"], AHEAD + i * 8 + (c // HC) * 4 + 4)
                g.wait_ge(M["y"], AHEAD + i * 4 + c // QC - 1)
                dst, states, cc = chunk_product(i, c)
                TT(dst, states, cc, ALU.mult).then_inc(M["prodp"], 1)

            def inputs(i, k, c):
                g.wait_ge(M["u"], AHEAD + i + 1)
                g.wait_ge(M["bbs"], AHEAD + i * 8 + (c // HC) * 4 + 2)
                products_done(g, i if c >= 2 else i - 1, (c - 2) % NC)
                t0, half = c * CH, c // HC
                TT(hb[c % 2][:].rearrange("p (e n) s -> p e n s", e=EB)[:, :, :, 1:SL],
                   u[k][:, :, t0:t0 + CH].rearrange("p e (n s) -> p e n s", n=1).broadcast_to([P, EB, N, CH]),
                   bbc[half][:, :, t0 - half * HT:t0 - half * HT + CH].rearrange("p (e n) s -> p e n s", e=1)
                   .broadcast_to([P, EB, N, CH]), ALU.mult).then_inc(M["bt"], 1)

            def extra(i, k, c, stages):
                if c == 1 and "F" in stages:
                    g.wait_ge(M["xcc"], AHEAD + i + 2)
                    g.wait_ge(M["sx"], AHEAD + i + 2)
                    TT(xcv[:], xcv[:], sg[:], ALU.mult).then_inc(M["xcv"], 1)
                if c == 2 and "B" in stages:
                    g.wait_ge(M["yd"], AHEAD + i)
                    TT(xd[1 - k][:], xd[1 - k][:], sz[1 - k][:], ALU.mult).then_inc(M["yg"], 1)
                if c == 4 and "F" in stages:
                    g.wait_ge(M["xcv"], AHEAD + i + 2)
                    g.wait_ge(M["dt"], AHEAD + i + 2)
                    TT(u[1 - k][:], dt[:], xcv[:], ALU.mult).then_inc(M["u"], 1)
                if c == 4 and "S" in stages:
                    g.wait_ge(M["zc"], AHEAD + i + 1)
                    g.wait_ge(M["ss"], AHEAD + i + 1)
                    TT(sz[k][:], sz[k][:], sg[:], ALU.mult).then_inc(M["sz"], 1)
                if c == 0 and "X" in stages:
                    g.wait_ge(M["o3"], AHEAD + i - 1)
                    TT(oo[:], oo[:], ga_row[:], ALU.mult).then_inc(M["o4"], 1)
                    g.wait_ge(M["o4"], AHEAD + i - 1)
                    TT(oo[:], oo[:], be_row[:], ALU.add).then_inc(M["o5"], 1)
                    g.wait_ge(M["o5"], AHEAD + i - 1)
                    g.wait_ge(M["xr"], AHEAD + (i - 1) * 16)
                    g.wait_ge(R["ac"], AHEAD + (i - 4) * (X + 1) + 1)
                    TT(x1b[k][:], oo[:], xt[1][:], ALU.add).then_inc(M["x1"], 1)

            def step(i, k, stages):
                for c in range(NC):
                    if c == 0 and "B" in stages and NC - 1 in PP:
                        product(i - 1, 1 - k, NC - 1)
                    if c > 0 and "S" in stages and c - 1 in PP:
                        product(i, k, c - 1)
                    if c == 1:
                        extra(i, k, c, stages)
                    if c < NC - 1 and "S" in stages:
                        inputs(i, k, c + 1)
                    if c != 1:
                        extra(i, k, c, stages)
                if "F" in stages:
                    inputs(i + 1, 1 - k, 0)
            g.wait_ge(s_w, 16 * len(resident))
            pipeline(g, step)

        @block.scalar
        def _(a):
            act = nc.scalar.activation
            nc.scalar.preload_act_table_set("natural_log_exp_and_others")
            head_start(a, (M, act_m), (R, act_x), (A, act_a))
            a.wait_ge(s_w, 16 * len(resident))
            a.wait_ge(s_setup, 1)
            act(aneg[:], aneg[:], ACT.Exp).then_inc(s_aexp, 1)
            a.wait_ge(s_setup, 3)

            def spread(i, h, w):
                if w == 0:
                    a.wait_ge(M["bt"], AHEAD + (i - 1) * NC + (h + 1) * HC)
                else:
                    products_done(a, i - 1, (h + 1) * HC - 1)
                for q in range(2):
                    a.wait_ge(M["bb"], AHEAD + i * 8 + h * 4 + w * 2 + q + 1)
                    act((bbc, cbc)[w][h][:, q * 8:q * 8 + 8, :], (BC, M1)[q][:].rearrange("p (n t) -> p n t", n=8), ACT.Copy)\
                        .then_inc(M["bbs"], 1)

            def decays(i, k, lo, hi):
                if lo == 0:
                    a.wait_ge(M["dt"], AHEAD + i + 1)
                    a.wait_ge(M["scan"], AHEAD + (i - 1) * NC)
                for s in range(lo, hi):
                    last = act(dA[k][:, :, s, 1:SL], dt[:, s // N, :].rearrange("p (c s) -> p c s", c=NC), ACT.Exp,
                               scale=aneg[:, s:s + 1])
                if hi == ST:
                    last.then_inc(M["dA"], 1)

            def norms(i, c):
                q = i * NC + c
                a.wait_ge(M["nr"], AHEAD + q + 1)
                act(nrm[:], nrm[:], ACT.Ln, bias=c_tiny[:]).then_inc(M["nl"], 1)
                a.wait_ge(M["nl"], AHEAD + q + 1)
                act(nrm[:], nrm[:], ACT.Exp, scale=-0.5, bias=c_ln10[:]).then_inc(M["ne"], 1)

            def route_norm(n):
                a.wait_ge(R["mv"], AHEAD + n + 1)
                act(ms[:, 0:1], mmv[:, 1:2], ACT.Ln, bias=c_eps5[:]).then_inc(R["ln"], 1)
                a.wait_ge(R["ln"], AHEAD + n + 1)
                act(ms[:, 1:2], ms[:, 0:1], ACT.Exp, scale=-0.5).then_inc(R["rs"], 1)

            def route_copy(n, k):
                a.wait_ge(R["xT"], AHEAD + n + 1)
                a.wait_ge(R["mm"], AHEAD + (n - 1) * 8)
                act(flat(mxT[k]), M0[:, 0:D], ACT.Copy).then_inc(R["xTs"], 1)

            def route_exp(n):
                a.wait_ge(R["nm"], AHEAD + n + 1)
                act(ex[:], lgt[:], ACT.Exp, bias=ms[:, 2:3], accum_out=ms[:, 3:4]).then_inc(R["ex"], 1)

            def step(i, k, stages):
                for c in range(NC):
                    if "S" in stages:
                        norms(i, c)
                    if c == 0 and "S" in stages:
                        spread(i, 0, 1)
                        spread(i, 1, 0)
                    if c == 1 and "S" in stages:
                        spread(i, 1, 1)
                    if c == 0 and "F" in stages:
                        a.wait_ge(M["xcc"], AHEAD + i + 2)
                        a.wait_ge(M["sz"], AHEAD + i)
                        act(sg[:], xcv[:], ACT.Exp, scale=-1.0).then_inc(M["ex"], 1)
                        a.wait_ge(M["ex"], AHEAD + i + 2)
                        act(sg[:], sg[:], ACT.Ln, bias=c_one[:]).then_inc(M["lx"], 1)
                        a.wait_ge(M["lx"], AHEAD + i + 2)
                        act(sg[:], sg[:], ACT.Exp, scale=-1.0).then_inc(M["sx"], 1)
                    if c == 1 and "X" in stages:
                        route_norm(i - 2)
                    if c == 2:
                        if "S" in stages:
                            a.wait_ge(M["zc"], AHEAD + i + 1)
                            a.wait_ge(M["xcv"], AHEAD + (i + 2 if "F" in stages else NTILES))
                            act(sg[:], sz[k][:], ACT.Exp, scale=-1.0).then_inc(M["ez"], 1)
                            a.wait_ge(M["ez"], AHEAD + i + 1)
                            act(sg[:], sg[:], ACT.Ln, bias=c_one[:]).then_inc(M["lz"], 1)
                            a.wait_ge(M["lz"], AHEAD + i + 1)
                            act(sg[:], sg[:], ACT.Exp, scale=-1.0).then_inc(M["ss"], 1)
                        if "F" in stages:
                            a.wait_ge(M["dtc"], AHEAD + i + 2)
                            act(dt[:], dt[:], ACT.Exp).then_inc(M["edt"], 1)
                            a.wait_ge(M["edt"], AHEAD + i + 2)
                            act(dt[:], dt[:], ACT.Ln, bias=c_one[:]).then_inc(M["ldt"], 1)
                    if c == 3:
                        if "X" in stages:
                            route_copy(i - 2, k)
                    if c == 6:
                        if "B" in stages:
                            a.wait_ge(M["vc3"], AHEAD + i)
                            act(sc[:, 8:9], sc[:, 7:8], ACT.Ln).then_inc(M["ln3"], 1)
                            a.wait_ge(M["ln3"], AHEAD + i)
                            act(sc[:, 9:10], sc[:, 8:9], ACT.Exp, scale=0.5).then_inc(M["sd3"], 1)
                    if c == 4:
                        if "X" in stages:
                            route_exp(i - 2)
                    if c == 4 and "L" in stages:
                        a.wait_ge(M["mv1"], AHEAD + i + 3)
                        act(sc[:, 0:1], mv[:, 0, 1:2], ACT.Ln, bias=c_eps5[:]).then_inc(M["ln1"], 1)
                        a.wait_ge(M["ln1"], AHEAD + i + 3)
                        a.wait_ge(M["keep"], AHEAD + i + 1)
                        act(ln1[k][:, 1:2], sc[:, 0:1], ACT.Exp, scale=-0.5).then_inc(M["rs1"], 1)
                    if c == 5 and "F" in stages:
                        spread(i + 1, 0, 0)
                    if c == 5 and "L" in stages:
                        a.wait_ge(M["vc2"], AHEAD + i + 3)
                        act(sc[:, 3:4], sc[:, 2:3], ACT.Ln).then_inc(M["ln2"], 1)
                        a.wait_ge(M["ln2"], AHEAD + i + 3)
                        act(sc[:, 4:5], sc[:, 3:4], ACT.Exp, scale=0.5).then_inc(M["sd2"], 1)
                    if c == 7 and "L" in stages:
                        a.wait_ge(M["xnT"], AHEAD + i + 3)
                        a.wait_ge(M["z"], AHEAD + i + 2)
                        for j in range(KD):
                            act(xnT[:, j, :], F0[:, j * P:(j + 1) * P], ACT.Identity, bias=be_in[:, j:j + 1],
                                scale=ga_in[:, j:j + 1]).then_inc(M["xnTs"], 1)
                    if "F" in stages and DECAYS[c] < DECAYS[c + 1]:
                        decays(i + 1, 1 - k, DECAYS[c], DECAYS[c + 1])
            pipeline(a, step)

            def experts(n0):
                def tile(i, k, j):
                    n = i + n0
                    route_norm(n)
                    route_copy(n, k)
                    route_exp(n)
                tiles(a, tile)

            with a.Fori(0, NB) as b:
                for t in range(NT):
                    n = b * NT + t
                    a.wait_ge(A["mv"], AHEAD + n + 1)
                    act(ms[:, 0:1], mmv[:, 1:2], ACT.Ln, bias=c_eps5[:]).then_inc(A["ln"], 1)
                    a.wait_ge(A["ln"], AHEAD + n + 1)
                    act(ms[:, 1:2], ms[:, 0:1], ACT.Exp, scale=-0.5).then_inc(A["rn"], 1)
                    a.wait_ge(A["xT"], AHEAD + n + 1)
                    act(xTa[:, :, t * P:(t + 1) * P], (F0, F1)[t % 2][:, 0:D].rearrange("p (j l) -> p j l", j=KD), ACT.Copy)\
                        .then_inc(A["xTs"], 1)
                for w, dst in ((0, qa), (1, ka), (2, va)):
                    for j in range(KD):
                        for g in range(NG):
                            m = (w * KD + j) * NG + g
                            a.wait_ge(A["pj"], AHEAD + b * 12 + m + 1)
                            s = (BC, YP, G0, G1)[m % 4]
                            o = dst[:, j, g * TG:(g + 1) * TG]
                            if w < 2:
                                act(o, s[:], ACT.Sigmoid, bias=b_qkv[:, w, j:j + 1],
                                    accum_out=ac[:, m:m + 1]).then_inc(A["pjs"], 1)
                            else:
                                act(o, s[:], ACT.Identity, bias=b_qkv[:, w, j:j + 1]).then_inc(A["pjs"], 1)
                nc.scalar.preload_act_table_set("natural_log_exp_and_others")
                a.wait_ge(A["cv"], AHEAD + b + 1)
                for banks, dst, mmd, l, r, c0 in (((BC, YP, G0, G1), r1, "si", "l1", "r1", 16),
                                                  ((F0, F1, M0, M1), r2, "so", "l2", "r2", 18)):
                    for m in range(4):
                        j, g = m // NG, m % NG
                        a.wait_ge(A[mmd], AHEAD + b * 4 + m + 1)
                        act(dst[:, j, g * TG:(g + 1) * TG], banks[m][:], ACT.Ln, bias=ac[:, c0 + j:c0 + j + 1])\
                            .then_inc(A[l], 1)
                    for m in range(4):
                        j, g = m // NG, m % NG
                        a.wait_ge(A[l], AHEAD + b * 4 + m + 1)
                        o = dst[:, j, g * TG:(g + 1) * TG]
                        act(o, o, ACT.Exp, scale=-1.0).then_inc(A[r], 1)
                for j in range(KD):
                    a.wait_ge(A["nm"], AHEAD + b + 1)
                    act(xTa[:, j, :], xTa[:, j, :], ACT.Exp, bias=ac[:, 42 + j:43 + j], accum_out=ac[:, 44 + j:45 + j])\
                        .then_inc(A["e"], 1)
                for m in range(4):
                    j, g = m // NG, m % NG
                    a.wait_ge(A["ci"], AHEAD + b * 4 + m + 1)
                    act(r2[:, j, g * TG:(g + 1) * TG], (BC, YP, G0, G1)[m][:], ACT.Sigmoid, bias=ac[:, 36 + j:37 + j])\
                        .then_inc(A["sa"], 1)
                for t in range(NT):
                    a.wait_ge(A["kvT"], AHEAD + b * NT + t + 1)
                    act(kv[:, t, :], (BC, YP, G0, G1)[t % 4][:], ACT.Copy).then_inc(A["kvs"], 1)
                nc.scalar.preload_act_table_set("natural_log_exp_and_others")
            experts(NTILES)

        @block.tensor
        def _(pe):
            mm = nc.tensor.matmul
            head_start(pe, (M, pe_m), (R, pe_x), (A, pe_a))
            pe.wait_ge(s_w, 16 * len(resident))

            def sum_states(i, h):
                products_done(pe, i, (h + 1) * QC - 1)
                pe.wait_ge(M["yd"], AHEAD + i)
                for n in range(N):
                    last = mm(YP[:, h * P:(h + 1) * P], ident[:],
                              prod[h % 2][:, n, :, :].rearrange("p e t -> p (e t)"), start=(n == 0), stop=(n == N - 1))
                last.then_inc(M["y"], 1)

            def spread(i, h, w):
                pe.wait_ge(M["bcl"], AHEAD + i + 1)
                for q in range(2):
                    pe.wait_ge(M["bbs"], AHEAD + i * 8 + h * 4 + w * 2 + q - 1)
                    for n in range(8):
                        r = (w * 2 + q) * 8 + n
                        last = mm((BC, M1)[q][:, n * HT:(n + 1) * HT], sel[:, r:r + 1].broadcast_to([3 * RB, P]),
                                  bcs[:, h * HT:(h + 1) * HT], start=True, stop=True)
                    last.then_inc(M["bb"], 1)

            def route(n, k):
                pe.wait_ge(R["xn"], AHEAD + n + 1)
                pe.wait_ge(R["lgb"], AHEAD + n)
                for j in range(KD):
                    last = nc.tensor.transpose(M0[:, j * P:(j + 1) * P], mxn[:, j * P:(j + 1) * P], ident[:])
                last.then_inc(R["xT"], 1)

            def logits(n, k):
                pe.wait_ge(R["xTs"], AHEAD + n + 1)
                for j in range(KD):
                    last = mm(M0[:, D:D + X], mxT[k][:, j, :], w_r[:, j, :], start=(j == 0), stop=(j == KD - 1))
                last.then_inc(R["lg"], 1)

            def experts_mm(n, k, lo, hi):
                for p in range(lo, hi):
                    pe.wait_ge(R["ac"], AHEAD + n * (X + 1) + (2 * p - 1 if p >= 2 else 2 * p + 15 - (X + 1)))
                    for j in range(KD):
                        last = mm(G[p % 2][:], mxT[k][:, j, :], w_x[:, j, p * 512:(p + 1) * 512],
                                  start=(j == 0), stop=(j == KD - 1))
                    last.then_inc(R["mm"], 1)

            def step(i, k, stages):
                for c in range(NC):
                    if c == 0 and "S" in stages:
                        spread(i, 0, 1)
                        spread(i, 1, 0)
                    if c == 0 and "B" in stages:
                        sum_states(i - 1, 3)
                    if c == 7 and "X" in stages:
                        experts_mm(i - 2, k, 0, 1)
                    if c < 7 and "Y" in stages:
                        experts_mm(i - 3, 1 - k, c + 1, c + 2)
                    if c == 1:
                        if "S" in stages:
                            spread(i, 1, 1)
                        if "F" in stages:
                            pe.wait_ge(M["xcv"], AHEAD + i + 2)
                            pe.wait_ge(R["lgb"], AHEAD + i - 2)
                            for e in range(EB):
                                last = mm(M0[0:3 * RB, XP:XP + P], w_xp[:, e, :], xcv[:, e, :], start=(e == 0),
                                          stop=(e == EB - 1))
                            last.then_inc(M["bc"], 1)
                            pe.wait_ge(M["xib"], AHEAD + i + 2)
                            for m in range(EB):
                                for e in range(EB):
                                    last = mm(F0[:, m * P:(m + 1) * P], w_dt[:, e, m * P:(m + 1) * P], xcv[:, e, :],
                                              start=(e == 0), stop=(e == EB - 1))
                            last.then_inc(M["dtp"], 1)
                    if c == 3 and "X" in stages:
                        if "F" in stages:
                            pe.wait_ge(M["bcv"], AHEAD + i + 2)
                        route(i - 2, k)
                    if c in (3, 5, 7) and "S" in stages:
                        sum_states(i, (c - 3) // 2)
                    if c == 4 and "X" in stages:
                        logits(i - 2, k)
                    if c == 4:
                        if "B" in stages:
                            pe.wait_ge(M["yg"], AHEAD + i)
                            pe.wait_ge(M["dtb"], AHEAD + (i + 2 if "F" in stages else NTILES))
                            for e in range(EB):
                                last = mm(F0[:, 0:D], xd[1 - k][:, e, :], w_out[:, e, :], start=(e == 0), stop=(e == EB - 1))
                            last.then_inc(M["op"], 1)
                        if "F" in stages:
                            pe.wait_ge(s_setup, 3)
                            spread(i + 1, 0, 0)
                    if c == 6 and "L" in stages:
                        pe.wait_ge(M["xn"], AHEAD + i + 3)
                        pe.wait_ge(M["o1"], AHEAD + (i if "B" in stages else 0))
                        for j in range(KD):
                            last = nc.tensor.transpose(F0[:, j * P:(j + 1) * P], xn[:, j * P:(j + 1) * P], ident[:])
                        last.then_inc(M["xnT"], 1)
                    if c == 7 and "L" in stages:
                        pe.wait_ge(M["xnTs"], AHEAD + (i + 3) * KD)
                        pe.wait_ge(M["zb"], AHEAD + i + 2)
                        for half, bank, s in ((0, F0, "xi"), (1, F1, "z")):
                            for m in range(EB):
                                for j in range(KD):
                                    last = mm(bank[:, m * P:(m + 1) * P],
                                              w_in[:, j, (half * EB + m) * P:(half * EB + m + 1) * P],
                                              xnT[:, j, :], start=(j == 0), stop=(j == KD - 1))
                            last.then_inc(M[s], 1)
            pipeline(pe, step)

            def experts(n0):
                def tile(i, k, j):
                    n = i + n0
                    route(n, k)
                    logits(n, k)
                    experts_mm(n, k, 0, X // 2)
                tiles(pe, tile)

            pe.wait_ge(s_wa, 16)
            quads = ((BC, YP, G0, G1), (F0, F1, M0, M1))

            def by_group(banks, mats_, src, s, before):
                for m in range(4):
                    j, g = m // NG, m % NG
                    before(m)
                    mm(banks[m][:], mats_[j], src[:, j, g * TG:(g + 1) * TG], start=True, stop=True).then_inc(A[s], 1)

            with pe.Fori(0, NB) as b:
                for t in range(NT):
                    n = b * NT + t
                    pe.wait_ge(A["xn"], AHEAD + n + 1)
                    if t < 2:
                        pe.wait_ge(A["x3"], AHEAD + b * NT)
                    else:
                        pe.wait_ge(A["xTs"], AHEAD + n - 1)
                    for j in range(KD):
                        last = nc.tensor.transpose((F0, F1)[t % 2][:, j * P:(j + 1) * P], mxn[:, j * P:(j + 1) * P], ident[:])
                    last.then_inc(A["xT"], 1)
                pe.wait_ge(A["xTs"], AHEAD + (b + 1) * NT)
                for w in range(3):
                    for j in range(KD):
                        for g in range(NG):
                            m = (w * KD + j) * NG + g
                            if m >= 4:
                                pe.wait_ge(A["pjs"], AHEAD + b * 12 + m - 3)
                            for kk in range(KD):
                                last = mm(quads[0][m % 4][:], w_a[:, w, kk, j * P:(j + 1) * P],
                                          xTa[:, kk, g * TG:(g + 1) * TG], start=(kk == 0), stop=(kk == KD - 1))
                            last.then_inc(A["pj"], 1)
                pe.wait_ge(A["hm"], AHEAD + (b + 1) * 4)
                for m in range(4):
                    last = mm(M0[:, m:m + 1], mats[:, m, :], c_eps6[:], start=True, stop=True)
                last.then_inc(A["cv0"], 1)
                by_group(quads[0], (mats[:, 0, :], mats[:, 1, :]), qa, "si",
                         lambda m: pe.wait_ge(A["pjs"], AHEAD + (b + 1) * 12))
                by_group(quads[1], (mats[:, 2, :], mats[:, 3, :]), ka, "so",
                         lambda m: pe.wait_ge(A["cv"], AHEAD + b + 1))
                pe.wait_ge(A["hn"], AHEAD + (b + 1) * 4)
                pe.wait_ge(A["l2"], AHEAD + (b + 1) * 4)
                for m in range(4):
                    last = mm(M0[:, m:m + 1], mats[:, 4 + m, :], c_eps6[:], start=True, stop=True)
                last.then_inc(A["cw0"], 1)
                by_group(quads[0], (mats[:, 4, :], mats[:, 5, :]), qa, "ci",
                         lambda m: pe.wait_ge(A["l1"], AHEAD + (b + 1) * 4))
                by_group(quads[1], (mats[:, 6, :], mats[:, 7, :]), ka, "co",
                         lambda m: pe.wait_ge(A["cw"], AHEAD + b + 1))
                pe.wait_ge(A["v"], AHEAD + (b + 1) * KD)
                for t in range(NT):
                    if t < 4:
                        pe.wait_ge(A["sa"], AHEAD + b * 4 + t + 1)
                    else:
                        pe.wait_ge(A["kvs"], AHEAD + b * NT + t - 3)
                    for c, src in enumerate((ka, va)):
                        for j in range(KD):
                            last = nc.tensor.transpose(quads[0][t % 4][:, (c * KD + j) * P:(c * KD + j + 1) * P],
                                                       src[:, j, t * P:(t + 1) * P], ident[:])
                    last.then_inc(A["kvT"], 1)
                pe.wait_ge(A["kvs"], AHEAD + (b + 1) * NT)
                pe.wait_ge(A["cc"], AHEAD + b + 1)
                for j in range(KD):
                    for t in range(NT):
                        last = mm(M0[:, j * P:(j + 1) * P], kv[:, t, j * P:(j + 1) * P], kv[:, t, D + j * P:D + (j + 1) * P],
                                  start=(t == 0), stop=(t == NT - 1))
                last.then_inc(A["kv0"], 1)
                pe.wait_ge(A["kvm"], AHEAD + (b + 1) * KD)
                by_group((F0, F1, M1, G1), (mats[:, 8, :], mats[:, 9, :]), r1, "om",
                         lambda m: None)
                for t in range(NT):
                    if t < 2:
                        pe.wait_ge(A["og"], AHEAD + (b + 1) * 4)
                    pe.wait_ge(A["x2"], AHEAD + b * NT + t - 1)
                    for j in range(KD):
                        last = mm((BC, YP)[t % 2][:, 0:D], r2[:, j, t * P:(t + 1) * P], w_a[:, 3, j, :],
                                  start=(j == 0), stop=(j == KD - 1))
                    last.then_inc(A["om2"], 1)
            experts(NTILES)

        @block.vector
        def _(v):
            V = nc.vector
            TT, TS, STT = V.tensor_tensor, V.tensor_scalar, V.scalar_tensor_tensor
            head_start(v, (M, dve_m), (R, dve_x), (A, dve_a))
            for c, val in ((c_one, 1.0), (c_eps5, 1e-5), (c_ln10, math.log(10.0)), (c_eps6, 1e-6), (c_tiny, 1e-12), (prx[:, X:X + 2], -1.0)):
                V.memset(c[:] if c is not prx else c, val)
            for k in range(2):
                last = V.memset(dA[k][:, :, :, 0:1], 0.0)
            last.then_inc(s_setup, 1)
            v.wait_ge(s_w, 16 * len(resident))
            v.wait_ge(s_aexp, 1)
            V.tensor_copy(sel[:], self32[:]).then_inc(s_setup, 1)
            TS(aneg[:], aneg[:], -1.0, None, ALU.mult).then_inc(s_setup, 1)

            def settle():
                v.sem_inc(s_settle, 1)

            def bias4(t):
                return t.rearrange("p (e t) -> p e t", t=1).broadcast_to([P, EB, P])

            def bank4(t):
                return t[:].rearrange("p (e t) -> p e t", e=EB)

            def convolve(i, k, j, also):
                v.wait_ge(M["conv"], AHEAD + i * TAPS * EB)
                if j is None:
                    V.tensor_copy(xin[:, :, 0:TAPS - 1], xin[:, :, P:]).then_inc(M["carry"], 1)
                else:
                    TS(xin[:, :, 0:TAPS - 1], xin[:, :, P:], carry[:, bass.ds(j, 1)], None, ALU.mult).then_inc(M["carry"], 1)
                v.wait_ge(M["xi"], AHEAD + i + 1)
                v.wait_ge(M["carry"], AHEAD + i + 1)
                TT(xin[:, :, TAPS - 1:], bank4(F0), bias4(b_in[:, 0:EB]), ALU.add).then_inc(M["xib"], 1)
                v.wait_ge(M["xib"], AHEAD + i + 1)
                v.wait_ge(M["u"], AHEAD + i)
                v.wait_ge(M["dtp"], AHEAD + i)
                for t in range(TAPS):
                    for e in range(EB):
                        if t == 0:
                            TS(xcv[:, e, :], xin[:, e, 0:P], cw[:, e, 0:1], cb[:, e:e + 1], ALU.mult, ALU.add)\
                                .then_inc(M["conv"], 1)
                        else:
                            v.wait_ge(M["conv"], AHEAD + (i * TAPS + t - 1) * EB + e + 1)
                            STT(xcv[:, e, :], xin[:, e, t:t + P], cw[:, e, t:t + 1], xcv[:, e, :], ALU.mult, ALU.add)\
                                .then_inc(M["conv"], 1)
                        also(t * EB + e)
                v.wait_ge(M["conv"], AHEAD + (i + 1) * TAPS * EB)
                TS(xcv[:], xcv[:], -40.0, None, ALU.max).then_inc(M["xcc"], 1)

            def split_bc(i):
                v.wait_ge(M["bcv"], AHEAD + i + 1)
                v.wait_ge(M["bb"], AHEAD + i * 8)
                V.tensor_copy(bcs[:], bcv[:]).then_inc(M["bch"], 1)
                v.wait_ge(M["bch"], AHEAD + i + 1)
                TT(bcv[:], bcv[:], bcs[:], ALU.subtract).then_inc(M["bcr"], 1)
                v.wait_ge(M["bcr"], AHEAD + i + 1)
                V.tensor_copy(bcs[RB:2 * RB, :], bcv[RB:2 * RB, :]).then_inc(M["bcm"], 1)
                V.tensor_copy(bcs[2 * RB:, :], bcv[2 * RB:, :]).then_inc(M["bcm"], 1)
                v.wait_ge(M["bcm"], AHEAD + (i + 1) * 2)
                TT(bcv[2 * RB:, :], bcv[2 * RB:, :], bcs[2 * RB:, :], ALU.subtract).then_inc(M["bcr2"], 1)
                v.wait_ge(M["bcr2"], AHEAD + i + 1)
                V.tensor_copy(bcs[2 * RB:, :], bcv[2 * RB:, :]).then_inc(M["bcl"], 1)

            def clip(i, k, c):
                TS(dA[k][:, c, :, 1:SL], dA[k][:, c, :, 1:SL], math.exp(-10.0), None, ALU.max).then_inc(M["clip"], 1)

            def scan(i, k, c, also):
                q = i * NC + c
                cur = hb[c % 2]
                v.wait_ge(M["clip"], AHEAD + q + 1)
                v.wait_ge(M["bt"], AHEAD + q + 1)
                v.wait_ge(M["st0"], AHEAD + q)
                states = cur[:].rearrange("p a b -> p (a b)")
                V.tensor_tensor_scan(states, dA[k][:, c, :, :].rearrange("p a b -> p (a b)"), states, 0.0, ALU.mult,
                                     ALU.add).then_inc(M["scan"], 1)
                also(0)
                v.wait_ge(M["scan"], AHEAD + q + 1)
                end = cur[:, :, CH:SL].rearrange("p a b -> p (a b)")
                TT(sq[:], end, end, ALU.mult).then_inc(M["sq"], 1)
                also(1)
                v.wait_ge(M["sq"], AHEAD + q + 1)
                v.wait_ge(M["ne"], AHEAD + q)
                V.tensor_reduce(nrm[:], sq[:].rearrange("p (e n) -> p e n", e=EB), AX.X, ALU.add).then_inc(M["nr"], 1)

            def bound(i, c):
                q = i * NC + c
                cur, nxt = hb[c % 2], hb[(c + 1) % 2]
                v.wait_ge(M["ne"], AHEAD + q + 1)
                last = cur[:, :, CH:SL].rearrange("p (e n) s -> p e (n s)", e=EB)
                factor = nrm[:].rearrange("p (e t) -> p e t", t=1).broadcast_to([P, EB, N])
                STT(nxt[:, :, 0:1].rearrange("p (e n) s -> p e (n s)", e=EB), factor, 1.0, last, ALU.min, ALU.mult)\
                    .then_inc(M["st0"], 1)
                STT(last, factor, 1.0, last, ALU.min, ALU.mult).then_inc(M["hs"], 1)

            def product(i, c):
                v.wait_ge(M["hs"], AHEAD + i * NC + c + 1)
                v.wait_ge(M["bbs"], AHEAD + i * 8 + (c // HC) * 4 + 4)
                v.wait_ge(M["y"], AHEAD + i * 4 + c // QC - 1)
                dst, states, cc = chunk_product(i, c)
                TT(dst, states, cc, ALU.mult).then_inc(M["prodv"], 1)

            def route_norm1(n, k, ready):
                ready()
                V.bn_stats(mst[:], mxt[k][:]).then_inc(R["st"], 1)
                v.wait_ge(R["st"], AHEAD + n + 1)
                settle()
                V.bn_aggr(mmv[:], mst[:]).then_inc(R["mv"], 1)

            def route_norm2(n, k):
                v.wait_ge(R["rs"], AHEAD + n + 1)
                v.wait_ge(R["xT"], AHEAD + n)
                TS(mxn[:], mxt[k][:], mmv[:, 0:1], ms[:, 1:2], ALU.subtract, ALU.mult).then_inc(R["xn"], 1)

            def route_scores(n, k):
                v.wait_ge(R["lg"], AHEAD + n + 1)
                TT(lgt[:], M0[:, D:D + X], rb_row[:], ALU.add).then_inc(R["lgb"], 1)
                v.wait_ge(R["lgb"], AHEAD + n + 1)
                settle()
                V.max(mx8[:], lgt[:]).then_inc(R["router"], 1)
                v.wait_ge(R["router"], AHEAD + n * ROUTER + 1)
                TS(ms[:, 2:3], mx8[:, 0:1], -1.0, None, ALU.mult).then_inc(R["nm"], 1)

            def route_step(n, k, step, stored):
                if step == 0:
                    v.wait_ge(R["ex"], AHEAD + n + 1)
                    V.reciprocal(ms[:, 4:5], ms[:, 3:4]).then_inc(R["router"], 1)
                elif step == 1:
                    v.wait_ge(R["router"], AHEAD + n * ROUTER + 2)
                    TS(prx[:, 0:X], ex[:], ms[:, 4:5], None, ALU.mult).then_inc(R["router"], 1)
                elif step == 2:
                    v.wait_ge(R["router"], AHEAD + n * ROUTER + 3)
                    settle()
                    V.max(t8[:], prx[:, 0:X]).then_inc(R["router"], 1)
                elif step == 3:
                    v.wait_ge(R["router"], AHEAD + n * ROUTER + 4)
                    V.memset(t8[:, TOPK:8], -1.0).then_inc(R["router"], 1)
                elif step == 4:
                    v.wait_ge(R["router"], AHEAD + n * ROUTER + 5)
                    settle()
                    V.match_replace(rest[:], t8[:], prx[:], 0.0).then_inc(R["router"], 1)
                elif step == 5:
                    v.wait_ge(R["router"], AHEAD + n * ROUTER + 6)
                    TT(selp[:], prx[:, 0:X], rest[:, 0:X], ALU.subtract).then_inc(R["router"], 1)
                elif step == 6:
                    v.wait_ge(R["router"], AHEAD + n * ROUTER + 7)
                    V.tensor_reduce(ms[:, 5:6], selp[:], AX.X, ALU.add).then_inc(R["router"], 1)
                elif step == 7:
                    v.wait_ge(R["router"], AHEAD + n * ROUTER + 8)
                    TS(ms[:, 6:7], ms[:, 5:6], 1e-10, None, ALU.add).then_inc(R["router"], 1)
                elif step == 8:
                    v.wait_ge(R["router"], AHEAD + n * ROUTER + 9)
                    V.reciprocal(ms[:, 7:8], ms[:, 6:7]).then_inc(R["router"], 1)
                elif step == 9:
                    v.wait_ge(R["router"], AHEAD + n * ROUTER + 10)
                    TT(ms[:, 8:9], ms[:, 5:6], ms[:, 7:8], ALU.mult).then_inc(R["router"], 1)
                elif step == 10:
                    v.wait_ge(R["router"], AHEAD + n * ROUTER + 11)
                    TS(ms[:, 9:10], ms[:, 8:9], 1e-10, None, ALU.max).then_inc(R["router"], 1)
                    TS(ms[:, 12:13], ms[:, 8:9], 1e-10, None, ALU.mult).then_inc(R["router"], 1)
                elif step == 11:
                    v.wait_ge(R["router"], AHEAD + n * ROUTER + 12)
                    V.reciprocal(ms[:, 10:11], ms[:, 9:10]).then_inc(R["router"], 1)
                elif step == 12:
                    v.wait_ge(R["router"], AHEAD + n * ROUTER + 14)
                    TT(ms[:, 11:12], ms[:, 7:8], ms[:, 10:11], ALU.mult).then_inc(R["router"], 1)
                elif step == 13:
                    stored()
                    TS(macc[k][:], mxt[k][:], ms[:, 12:13], None, ALU.add).then_inc(R["ac"], 1)
                elif step == 14:
                    v.wait_ge(R["router"], AHEAD + n * ROUTER + 15)
                    TS(gate[k][:], selp[:], ms[:, 11:12], None, ALU.mult).then_inc(R["router"], 1)
                elif step == 15:
                    v.wait_ge(R["router"], AHEAD + n * ROUTER + 16)

            def route_top(n, k, stored):
                for step in range(16):
                    route_step(n, k, step, stored)

            def expert_sums(n, k, lo, hi):
                for e in range(lo, hi):
                    v.wait_ge(R["mm"], AHEAD + n * 8 + e // 2 + 1)
                    v.wait_ge(R["ac"], AHEAD + n * (X + 1) + 1 + e)
                    STT(macc[k][:], G[(e // 2) % 2][:, (e % 2) * D:(e % 2 + 1) * D], gate[k][:, e:e + 1], macc[k][:],
                        ALU.mult, ALU.add).then_inc(R["ac"], 1)

            def between(i, k, c, stages, j, stored):
                L_, F, B, X_ = ("L" in stages, "F" in stages, "B" in stages, "X" in stages)
                if c == 0:
                    if "S" in stages:
                        V.tensor_copy(ln1r[k][:], ln1[k][:]).then_inc(M["keep"], 1)
                    if F:
                        convolve(i + 1, 1 - k, j, lambda s: route_step(i - 3, 1 - k, s, stored) if "Y" in stages else None)
                    elif "Y" in stages:
                        route_top(i - 3, 1 - k, stored)
                if c == 1 and B:
                    v.wait_ge(M["y"], AHEAD + i * 4)
                    v.wait_ge(M["xd"], AHEAD + i * EB)
                    x4 = xd[1 - k][:].rearrange("p e (h t) -> p h e t", h=4)
                    TT(x4, x4, YP[:].rearrange("p (h e t) -> p h e t", h=4, e=EB), ALU.add).then_inc(M["yd"], 1)
                if c == 1 and X_:
                    route_norm1(i - 2, k, lambda: v.wait_ge(M["x1"], AHEAD + i - 1))
                if c == 2:
                    if X_:
                        route_norm2(i - 2, k)
                    if F:
                        v.wait_ge(M["bc"], AHEAD + i + 2)
                        TS(bcv[:], M0[0:3 * RB, XP:XP + P], b_xp[:], None, ALU.add).then_inc(M["bcv"], 1)
                        v.wait_ge(M["dtp"], AHEAD + i + 2)
                        v.wait_ge(M["dA"], AHEAD + i + 1)
                        v.wait_ge(M["u"], AHEAD + i + 1)
                        TT(dt[:], bank4(F0), bias4(b_dt[:]), ALU.add).then_inc(M["dtb"], 1)
                        v.wait_ge(M["dtb"], AHEAD + i + 2)
                        TS(dt[:], dt[:], 40.0, None, ALU.min).then_inc(M["dtc"], 1)
                        split_bc(i + 1)
                if c == 3:
                    if F:
                        v.wait_ge(M["ldt"], AHEAD + i + 2)
                        TS(dt[:], dt[:], 1e-4, 10.0, ALU.max, ALU.min).then_inc(M["dt"], 1)
                if c == 4:
                    if X_:
                        route_scores(i - 2, k)
                    if F:
                        v.wait_ge(M["z"], AHEAD + i + 2)
                        v.wait_ge(M["yg"], AHEAD + i)
                        TT(sz[1 - k][:], bank4(F1), bias4(b_in[:, EB:]), ALU.add).then_inc(M["zb"], 1)
                        v.wait_ge(M["zb"], AHEAD + i + 2)
                        TS(sz[1 - k][:], sz[1 - k][:], -40.0, None, ALU.max).then_inc(M["zc"], 1)
                    if L_:
                        v.wait_ge(M["x"], AHEAD + (i + 3) * 16)
                        V.bn_stats(st[:, 0, :], xt[0][:]).then_inc(M["st1"], 1)
                        v.wait_ge(M["st1"], AHEAD + i + 3)
                        settle()
                        V.bn_aggr(mv[:, 0, :], st[:, 0, :]).then_inc(M["mv1"], 1)
                if c == 5:
                    if L_:
                        v.wait_ge(M["rs1"], AHEAD + i + 3)
                        V.tensor_copy(ln1[k][:, 0:1], mv[:, 0, 0:1])
                        TS(y1[:], xt[0][:], mv[:, 0, 0:1], ln1[k][:, 1:2], ALU.subtract, ALU.mult).then_inc(M["y1"], 1)
                        v.wait_ge(M["y1"], AHEAD + i + 3)
                        V.bn_stats(st[:, 1, :], y1[:]).then_inc(M["st2"], 1)
                        v.wait_ge(M["st2"], AHEAD + i + 3)
                        settle()
                        V.bn_aggr(mv[:, 1, :], st[:, 1, :]).then_inc(M["mv2"], 1)
                        v.wait_ge(M["mv2"], AHEAD + i + 3)
                        TS(sc[:, 2:3], mv[:, 1, 1:2], D / (D - 1.0), 1e-19, ALU.mult, ALU.max).then_inc(M["vc2"], 1)
                    if B:
                        v.wait_ge(M["xr"], AHEAD + i * 16)
                        TS(yr[:], xt[1][:], ln1r[1 - k][:, 0:1], ln1r[1 - k][:, 1:2], ALU.subtract, ALU.mult).then_inc(M["yr"], 1)
                        v.wait_ge(M["op"], AHEAD + i)
                        v.wait_ge(M["x1"], AHEAD + i - 1)
                        TT(oo[:], F0[:, 0:D], ob_row[:], ALU.add).then_inc(M["o1"], 1)
                        v.wait_ge(M["o1"], AHEAD + i)
                        TT(oo[:], oo[:], yr[:], ALU.add).then_inc(M["o2"], 1)
                        v.wait_ge(M["o2"], AHEAD + i)
                        V.bn_stats(st[:, 2, :], oo[:]).then_inc(M["st3"], 1)
                        v.wait_ge(M["st3"], AHEAD + i)
                        settle()
                        V.bn_aggr(mv[:, 2, :], st[:, 2, :]).then_inc(M["mv3"], 1)
                        v.wait_ge(M["mv3"], AHEAD + i)
                        TS(sc[:, 7:8], mv[:, 2, 1:2], D / (D - 1.0), 1e-19, ALU.mult, ALU.max).then_inc(M["vc3"], 1)
                if c == 6:
                    if L_:
                        v.wait_ge(M["sd2"], AHEAD + i + 3)
                        TS(sc[:, 5:6], sc[:, 4:5], 1e-6, None, ALU.add).then_inc(M["se2"], 1)
                        v.wait_ge(M["se2"], AHEAD + i + 3)
                        V.reciprocal(sc[:, 6:7], sc[:, 5:6]).then_inc(M["r2"], 1)
                        v.wait_ge(M["r2"], AHEAD + i + 3)
                        v.wait_ge(M["xnT"], AHEAD + i + 2)
                        TS(xn[:], y1[:], mv[:, 1, 0:1], sc[:, 6:7], ALU.subtract, ALU.mult).then_inc(M["xn"], 1)
                    if F:
                        v.wait_ge(M["xcv"], AHEAD + i + 2)
                        v.wait_ge(M["op"], AHEAD + i)
                        for e in range(EB):
                            TS(xd[1 - k][:, e, :], xcv[:, e, :], dpar[:, e:e + 1], None, ALU.mult).then_inc(M["xd"], 1)
                if c == 7 and B:
                    v.wait_ge(M["sd3"], AHEAD + i)
                    TS(sc[:, 10:11], sc[:, 9:10], 1e-6, None, ALU.add).then_inc(M["se3"], 1)
                    v.wait_ge(M["se3"], AHEAD + i)
                    V.reciprocal(sc[:, 11:12], sc[:, 10:11]).then_inc(M["r3"], 1)
                    v.wait_ge(M["r3"], AHEAD + i)
                    TS(oo[:], oo[:], mv[:, 2, 0:1], sc[:, 11:12], ALU.subtract, ALU.mult).then_inc(M["o3"], 1)
            def step(i, k, stages):
                if isinstance(i, int):
                    j = (NT // 2 - 1 if (i + 1) % NT == 0 else 0) if (i + 1) % 2 == 0 else None
                    fresh = (NT // 2 - 1 if i % NT == 0 else 0) if i % 2 == 0 else None
                else:
                    pair = i // 2
                    j = pair % (NT // 2) if k == 1 else None
                    fresh = (pair + NT // 2 - 1) % (NT // 2) if k == 0 else None
                if "S" in stages:
                    clip_wait = v.wait_ge(M["dA"], AHEAD + i + 1)
                    clip(i, k, 0)
                    if fresh is not None:
                        v.wait_ge(M["st0"], AHEAD + i * NC)
                        first = hb[0][:, :, 0:1].rearrange("p a b -> p (a b)")
                        TS(first, first, carry[:, bass.ds(fresh, 1)], None, ALU.mult).then_inc(s_zero, 1)
                        v.wait_ge(s_zero, i // 2 + 1)
                def expert(e):
                    if "Y" in stages:
                        expert_sums(i - 3, 1 - k, e, e + 1)

                for c in range(NC):
                    if "S" in stages:
                        scan(i, k, c, lambda m: expert(2 * c + m) if c > 0 else None)
                        if c < NC - 1:
                            clip(i, k, c + 1)
                    elif c > 0:
                        expert(2 * c)
                        expert(2 * c + 1)
                    if "S" in stages and c in EARLY:
                        bound(i, c)
                        if c in PV:
                            product(i, c)
                    between(i, k, c, stages, j, lambda: v.wait_ge(R["o"][1 - k], AHEAD + (i - 4 + k) * 8))
                    if c == 0:
                        expert(0)
                        expert(1)
                    if "S" in stages and c not in EARLY:
                        bound(i, c)
                        if c in PV:
                            product(i, c)
            V.memset(hb[0][:, :, 0:1], 0.0)
            V.memset(xin[:], 0.0)
            V.memset(carry[:, 0:NT // 2 - 1], 1.0)
            V.memset(carry[:, NT // 2 - 1:], 0.0).then_inc(s_zero2, 1)
            v.wait_ge(s_zero2, 1)
            pipeline(v, step)

            def experts(n0):
                def tile(i, k, j):
                    n = i + n0
                    route_norm1(n, k, lambda: v.wait_ge(R["x"][k], AHEAD + (j + 1) * 16))
                    route_norm2(n, k)
                    route_scores(n, k)
                    route_top(n, k, lambda: v.wait_ge(R["o"][k], AHEAD + (j + n0 // 2) * 16))
                    expert_sums(n, k, 0, X)
                tiles(v, tile)

            def columns(first, last):
                return ac[:, first:last]

            with v.Fori(0, NB) as b:
                for t in range(NT):
                    n = b * NT + t
                    v.wait_ge(A["x"][t % 2], AHEAD + (b * NT + t // 2 + 1) * 16)
                    V.bn_stats(mst[:], xt[t % 2][:]).then_inc(A["st"], 1)
                    v.wait_ge(A["st"], AHEAD + n + 1)
                    settle()
                    V.bn_aggr(mmv[:], mst[:]).then_inc(A["mv"], 1)
                    v.wait_ge(A["rn"], AHEAD + n + 1)
                    v.wait_ge(A["xT"], AHEAD + n)
                    TS(mxn[:], xt[t % 2][:], mmv[:, 0:1], ms[:, 1:2], ALU.subtract, ALU.mult).then_inc(A["xn"], 1)
                v.wait_ge(A["pjs"], AHEAD + b * 12 + 8)
                V.tensor_reduce(columns(8, 12), columns(0, 8).rearrange("p (a g) -> p a g", g=NG), AX.X, ALU.add).then_inc(A["qk1"], 1)
                v.wait_ge(A["qk1"], AHEAD + b + 1)
                TS(columns(12, 16), columns(8, 12), 1e-6, None, ALU.add).then_inc(A["qk2"], 1)
                v.wait_ge(A["qk2"], AHEAD + b + 1)
                for m, c in enumerate((14, 15, 12, 13)):
                    TS(mats[:, m, :], hmask[:], columns(c, c + 1), None, ALU.mult).then_inc(A["hm"], 1)
                v.wait_ge(A["cv0"], AHEAD + b + 1)
                V.tensor_copy(columns(16, 20), M0[:, 0:4]).then_inc(A["cv"], 1)
                for src, dst, r, s, c0 in ((qa, r1, "r1", "qs", 20), (ka, r2, "r2", "ks", 24)):
                    for m in range(4):
                        j, g = m // NG, m % NG
                        v.wait_ge(A[r], AHEAD + b * 4 + m + 1)
                        o = dst[:, j, g * TG:(g + 1) * TG]
                        STT(o, src[:, j, g * TG:(g + 1) * TG], 1.0, o, ALU.mult, ALU.mult,
                                accum_out=columns(c0 + m, c0 + m + 1)).then_inc(A[s], 1)
                v.wait_ge(A["qs"], AHEAD + (b + 1) * 4)
                v.wait_ge(A["ks"], AHEAD + (b + 1) * 4)
                V.tensor_reduce(columns(28, 32), columns(20, 28).rearrange("p (a g) -> p a g", g=NG), AX.X, ALU.add).then_inc(A["s1"], 1)
                v.wait_ge(A["s1"], AHEAD + b + 1)
                TS(columns(32, 36), columns(28, 32), 1e-6, None, ALU.add).then_inc(A["s2"], 1)
                v.wait_ge(A["s2"], AHEAD + b + 1)
                for m, c in enumerate((34, 35, 32, 33)):
                    TS(mats[:, 4 + m, :], hmask[:], columns(c, c + 1), None, ALU.mult).then_inc(A["hn"], 1)
                v.wait_ge(A["cw0"], AHEAD + b + 1)
                V.tensor_copy(columns(36, 40), M0[:, 0:4]).then_inc(A["cw"], 1)
                v.wait_ge(A["cw"], AHEAD + b + 1)
                for m in range(4):
                    j, g = m // NG, m % NG
                    v.wait_ge(A["co"], AHEAD + b * 4 + m + 1)
                    TS(xTa[:, j, g * TG:(g + 1) * TG], (F0, F1, M0, M1)[m][:], columns(38 + j, 39 + j), 1.0, ALU.add, ALU.min).then_inc(A["cs"], 1)
                v.wait_ge(A["cs"], AHEAD + (b + 1) * 4)
                TS(xTa, xTa, -1.0, None, ALU.max).then_inc(A["cc"], 1)
                v.wait_ge(A["cc"], AHEAD + b + 1)
                V.tensor_reduce(columns(40, 42), xTa, AX.X, ALU.max).then_inc(A["mx"], 1)
                v.wait_ge(A["mx"], AHEAD + b + 1)
                TS(columns(42, 44), columns(40, 42), -1.0, None, ALU.mult).then_inc(A["nm"], 1)
                v.wait_ge(A["e"], AHEAD + (b + 1) * KD)
                V.reciprocal(columns(46, 48), columns(44, 46)).then_inc(A["rs"], 1)
                v.wait_ge(A["rs"], AHEAD + b + 1)
                TS(columns(48, 50), columns(46, 48), float(L), None, ALU.mult).then_inc(A["rl"], 1)
                v.wait_ge(A["rl"], AHEAD + b + 1)
                for j in range(KD):
                    STT(va[:, j, :], xTa[:, j, :], columns(48 + j, 49 + j), va[:, j, :], ALU.mult, ALU.mult).then_inc(A["v"], 1)
                v.wait_ge(A["kv0"], AHEAD + b + 1)
                for j in range(KD):
                    TT(mats[:, 8 + j, :], M0[:, j * P:(j + 1) * P], hmask[:], ALU.mult).then_inc(A["kvm"], 1)
                for m in range(4):
                    j, g = m // NG, m % NG
                    v.wait_ge(A["om"], AHEAD + b * 4 + m + 1)
                    o = r2[:, j, g * TG:(g + 1) * TG]
                    TT(o, (F0, F1, M1, G1)[m][:], o, ALU.mult).then_inc(A["og"], 1)
                for t in range(NT):
                    n = b * NT + t
                    v.wait_ge(A["om2"], AHEAD + n + 1)
                    v.wait_ge(A["x"][t % 2], AHEAD + (b * NT + NT // 2 + t // 2 + 1) * 16)
                    v.wait_ge(A["o"][t % 2], AHEAD + (b * (NT // 2) + t // 2) * 16)
                    TT(x1b[t % 2][:], (BC, YP)[t % 2][:, 0:D], bo_row[:], ALU.add).then_inc(A["x2"], 1)
                    v.wait_ge(A["x2"], AHEAD + n + 1)
                    TT(x1b[t % 2][:], x1b[t % 2][:], xt[t % 2][:], ALU.add).then_inc(A["x3"], 1)
            experts(NTILES)


def _param(a, blocks):
    import numpy as np
    return np.ascontiguousarray(a.reshape(blocks, P, -1).transpose(1, 0, 2))


def layout(i):
    import numpy as np
    g = {k.replace("L0_", ""): np.asarray(v) for k, v in i.items()}
    row = lambda a: np.ascontiguousarray(np.broadcast_to(a, (P, a.shape[0])))
    col = lambda a: np.ascontiguousarray(a.reshape(-1, P).T)
    sel = np.tile(np.eye(RB, dtype=np.float32), (3, 1))
    hmask = np.kron(np.eye(P // 16), np.ones((16, 16))).astype(np.float32)
    xw = g["ffn_expert_w"]
    return {
        "x": g["attn_a_x"],
        "w_in": _param(g["attn_a_in_proj_w"].T, KD), "w_dt": _param(g["attn_a_dt_proj_w"].T, EB),
        "w_xp": _param(np.tile(g["attn_a_x_proj_w"].T, (1, 3)), EB), "w_out": _param(g["attn_a_out_proj_w"].T, EB),
        "w_r": _param(g["ffn_router_w"].T, KD),
        "w_x": np.ascontiguousarray(xw.reshape(X, KD, P, D).transpose(2, 1, 0, 3)).reshape(P, KD, X * D),
        "ident": np.eye(P, dtype=np.float32), "sel": sel, "hmask": hmask,
        "b_in": col(g["attn_a_in_proj_b"]), "cw": _param(g["attn_a_conv_w"].reshape(E, TAPS), EB),
        "cb": col(g["attn_a_conv_b"]), "b_dt": col(g["attn_a_dt_proj_b"]), "dpar": col(g["attn_a_D_param"]),
        "A_log": _param(g["attn_a_A_log"], EB).reshape(P, ST),
        "b_xp": np.tile(g["attn_a_x_proj_b"], 3).reshape(3 * RB, 1),
        "ga_in": col(g["attn_a_in_norm_alpha"]), "be_in": col(g["attn_a_in_norm_bias"]),
        "ob_row": row(g["attn_a_out_proj_b"]), "ga_row": row(g["attn_a_norm_alpha"]), "be_row": row(g["attn_a_norm_bias"]),
        "bo_row": row(g["attn_b_bo"]), "rb_row": row(g["ffn_router_b"]),
        "b_qkv": np.ascontiguousarray(np.stack([col(g[f"attn_b_b{c}"]) for c in "qkv"], 1)),
        "w_qkvo": np.ascontiguousarray(np.stack([_param(g[f"attn_b_W{c}"].T, KD) for c in "qkvo"], 1)),
    }


def kernel(**inputs):
    import numpy as _np
    import concourse.bacc as _bacc
    from concourse import mybir as _mybir
    from concourse.bass_utils import run_bass_kernel_spmd as _run

    nc = _bacc.Bacc("TRN2", target_bir_lowering=False, num_devices=1)
    arrays, dram = {}, {}
    for name, a in layout(inputs).items():
        a = _np.ascontiguousarray(a)
        arrays[f"in_{name}"] = a
        dram[name] = nc.dram_tensor(f"in_{name}", a.shape, _mybir.dt.from_np(a.dtype), kind="ExternalInput").ap()
    for name in ("x1d", "x2d", "x3d"):
        dram[name] = nc.dram_tensor(name, (NB, L, D), _mybir.dt.float32, kind="Internal").ap()
    out = nc.dram_tensor("out_dram", (NB, L, D), _mybir.dt.float32, kind="ExternalOutput").ap()
    build(nc, dram, out)
    r = _run(nc, [arrays], core_ids=[0])
    return r.results[0]["out_dram"]
```

```python
import math
from contextlib import ExitStack

import concourse.bass as bass
from concourse import mybir

NB, L, D = 8, 1024, 256
E, N, TAPS = 512, 16, 4
P = 128
NT = L // P
NTILES = NB * NT
KD, EB = D // P, E // P
CH = 16
NC = P // CH
SL = CH + 1
ST = EB * N
HT = P // 2
HC = NC // 2
QT = P // 4
QC = NC // 4
RB = 32
X, TOPK = 16, 6
ROUTER = 16
PV = (3,)
PP = (0, 1, 2, 4, 5, 6, 7)
DECAYS = (0, 0, 0, 8, 26, 42, 52, 62, 64)
EARLY = (0, 2)
AHEAD = 64


def build(nc, dram, out):
    f32, bf16 = mybir.dt.float32, mybir.dt.bfloat16
    ALU, ACT, AX = mybir.AluOpType, mybir.ActivationFunctionType, mybir.AxisListType
    ctx = ExitStack()
    with ctx:
        def sb(name, shape, dt=f32):
            return ctx.enter_context(nc.sbuf_tensor(name, shape, dt))

        def sig(name):
            return ctx.enter_context(nc.semaphore(name))

        w_in = sb("w_in", [P, KD, 2 * E])
        w_dt = sb("w_dt", [P, EB, E])
        w_xp = sb("w_xp", [P, EB, 3 * RB])
        w_out = sb("w_out", [P, EB, D])
        w_r = sb("w_r", [P, KD, X])
        w_x = sb("w_x", [P, KD, X * D])
        ident = sb("ident", [P, P])
        self32 = sb("self32", [3 * RB, RB])
        sel = sb("sel", [3 * RB, RB], bf16)
        hmask = sb("hmask", [P, P])
        b_in = sb("b_in", [P, 2 * EB])
        cw = sb("cw", [P, EB, TAPS])
        cb = sb("cb", [P, EB])
        b_dt = sb("b_dt", [P, EB])
        dpar = sb("dpar", [P, EB])
        aneg = sb("aneg", [P, ST])
        b_xp = sb("b_xp", [3 * RB, 1])
        ga_in = sb("ga_in", [P, KD])
        be_in = sb("be_in", [P, KD])
        ob_row = sb("ob_row", [P, D])
        ga_row = sb("ga_row", [P, D])
        be_row = sb("be_row", [P, D])
        bo_row = sb("bo_row", [P, D])
        rb_row = sb("rb_row", [P, X])
        b_qkv = sb("b_qkv", [P, 3, KD])
        resident = [(w_in, "w_in"), (w_dt, "w_dt"), (w_xp, "w_xp"), (w_out, "w_out"), (w_r, "w_r"),
                    (w_x, "w_x"), (ident, "ident"), (self32, "sel"), (hmask, "hmask"), (b_in, "b_in"),
                    (cw, "cw"), (cb, "cb"), (b_dt, "b_dt"), (dpar, "dpar"), (aneg, "A_log"),
                    (b_xp, "b_xp"), (ga_in, "ga_in"), (be_in, "be_in"), (ob_row, "ob_row"),
                    (ga_row, "ga_row"), (be_row, "be_row"), (bo_row, "bo_row"), (rb_row, "rb_row"),
                    (b_qkv, "b_qkv")]
        c_one = sb("c_one", [P, 1])
        c_eps5 = sb("c_eps5", [P, 1])
        c_ln10 = sb("c_ln10", [P, 1])
        c_eps6 = sb("c_eps6", [P, 1])
        c_tiny = sb("c_tiny", [P, 1])

        dA = [sb(f"dA{k}", [P, NC, ST, SL]) for k in range(2)]
        hb = [sb(f"hb{k}", [P, ST, SL]) for k in range(2)]
        prod = [sb(f"prod{k}", [P, N, EB, QT]) for k in range(2)]
        bbc = [sb(f"bbc{k}", [P, N, HT]) for k in range(2)]
        cbc = [sb(f"cbc{k}", [P, N, HT]) for k in range(2)]
        xt = [sb(f"xt{k}", [P, D]) for k in range(2)]
        xq = [sb(f"xq{k}", [P, D]) for k in range(2)]
        y1 = sb("y1", [P, D])
        yr = sb("yr", [P, D])
        x1b = [sb(f"x1b{k}", [P, D]) for k in range(2)]
        xn = sb("xn", [P, D])
        xnT = sb("xnT", [P, KD, P])
        xin = sb("xin", [P, EB, P + TAPS - 1])
        sg = sb("sg", [P, EB, P])
        sz = [sb(f"sz{k}", [P, EB, P]) for k in range(2)]
        xcv = sb("xcv", [P, EB, P])
        xd = [sb(f"xd{k}", [P, EB, P]) for k in range(2)]
        dt = sb("dt", [P, EB, P])
        u = [sb(f"u{k}", [P, EB, P]) for k in range(2)]
        bcv = sb("bcv", [3 * RB, P])
        bcs = sb("bcs", [3 * RB, P], bf16)
        oo = sb("oo", [P, D])
        st = sb("st", [P, 4, 6])
        mv = sb("mv", [P, 4, 2])
        ln1 = [sb(f"ln1{k}", [P, 2]) for k in range(2)]
        ln1r = [sb(f"ln1r{k}", [P, 2]) for k in range(2)]
        carry = sb("carry", [P, NT // 2])
        sc = sb("sc", [P, 16])
        sq = sb("sq", [P, ST])
        nrm = sb("nrm", [P, EB])
        mxt = x1b
        mxn = sb("mxn", [P, D])
        mxT = [sb(f"mxT{k}", [P, KD, P]) for k in range(2)]
        macc = [sb(f"macc{k}", [P, D]) for k in range(2)]
        mst = sb("mst", [P, 6])
        mmv = sb("mmv", [P, 2])
        ms = sb("ms", [P, 16])
        lgt = sb("lgt", [P, X])
        mx8 = sb("mx8", [P, 8])
        ex = sb("ex", [P, X])
        prx = sb("prx", [P, X + 2])
        t8 = sb("t8", [P, 8])
        rest = sb("rest", [P, X + 2])
        selp = sb("selp", [P, X])
        gate = [sb(f"gate{k}", [P, X]) for k in range(2)]
        big = [t[:].rearrange("p a b c -> p (a b c)") for t in dA]
        AW = KD * L

        def half_major(h, n):
            return big[h][:, n * AW:(n + 1) * AW].rearrange("p (j l) -> p j l", j=KD)
        xTa, qa, ka, va = (half_major(0, n) for n in range(4))
        r1, r2 = (half_major(1, n) for n in range(2))
        kv = big[1][:, 2 * AW:4 * AW].rearrange("p (t d) -> p t d", t=NT)
        w_a = prod[0][:].rearrange("p a b c -> p (a b c)").rearrange("p (w k d) -> p w k d", w=4, k=KD)
        mats = prod[1][:].rearrange("p a b c -> p (a b c)").rearrange("p (m c) -> p m c", c=P)
        ac = sb("ac", [P, 50])
        TG = 512
        NG = L // TG

        F0, F1, BC, YP, G0, G1, M0, M1 = (ctx.enter_context(nc.psum_tensor(f"ps{k}", [P, 512], f32)) for k in range(8))
        G = (G0, G1)
        G4 = (G0, G1, F0, F1)
        XP = 512 - P

        s_w, s_setup, s_aexp, s_zero = sig("s_w"), sig("s_setup"), sig("s_aexp"), sig("s_zero")
        s_settle = sig("s_settle")

        dve_m = ("st1", "mv1", "y1", "st2", "mv2", "vc2", "se2", "r2", "xn", "keep", "xib", "zb", "zc", "conv", "carry",
                 "xcc", "bcv", "bch", "bcr", "bcm", "bcr2", "bcl", "dtb", "dtc", "dt", "xd", "clip", "scan", "sq", "nr",
                 "st0", "hs", "prodv", "yd", "o1", "o2", "st3", "mv3", "vc3", "se3", "r3", "o3")
        act_m = ("ln1", "rs1", "ln2", "sd2", "xnTs", "ez", "lz", "ss", "ex", "lx", "sx", "bbs", "edt", "ldt", "dA", "nl",
                 "ne", "ln3", "sd3")
        pool_m = ("sz", "xcv", "u", "bt", "prodp", "yg", "o4", "o5", "x1")
        pe_m = ("xnT", "xi", "z", "bc", "dtp", "bb", "y", "op")
        sp_m = ("x", "xr")
        dve_x = ("st", "mv", "xn", "lgb", "nm", "router", "ac")
        act_x = ("ln", "rs", "xTs", "ex")
        pe_x = ("xT", "lg", "mm")
        sp_x = ("x_even", "x_odd", "o_even", "o_odd")
        dve_a = ("st", "mv", "xn", "qk1", "qk2", "hm", "cv", "qs", "ks", "s1", "s2", "hn", "cw", "cs", "cc", "mx", "nm",
                 "rs", "rl", "v", "kvm", "og", "x2", "x3")
        act_a = ("ln", "rn", "xTs", "pjs", "l1", "r1", "l2", "r2", "sa", "e", "kvs")
        pe_a = ("xT", "pj", "cv0", "si", "so", "cw0", "ci", "co", "kvT", "kv0", "om", "om2")
        sp_a = ("x_even", "x_odd", "q_even", "q_odd", "o_even", "o_odd")
        A = {n: sig("a_" + n) for n in dve_a + act_a + pe_a + sp_a}
        s_wa = sig("s_wa")
        M = {n: sig("m_" + n) for n in dve_m + act_m + pool_m + pe_m + sp_m}
        R = {n: sig("x_" + n) for n in dve_x + act_x + pe_x + sp_x}
        for d, names in ((R, ("x", "o")), (A, ("x", "o"))):
            for n in names:
                d[n] = (d[n + "_even"], d[n + "_odd"])
        A["q"] = (A["q_even"], A["q_odd"])
        inputs_a = ((xt[0], A["x"][0], 0), (xt[1], A["x"][1], 0), (y1, M["x"], NTILES * 16), (yr, M["xr"], NTILES * 16))

        def head_start(eng, *groups):
            for d, names in groups:
                for n in names:
                    eng.sem_inc(d[n], AHEAD)

        def tile_of(t, b, r):
            return t[bass.ds(b, 1), bass.ds(r * P, P), :].rearrange("a p d -> p (a d)")

        def flat_tile(t, i):
            v = t.rearrange("b (t p) d -> (b t) p d", p=P)
            return v[bass.ds(i, 1), :, :].rearrange("a p d -> p (a d)")

        def pipeline(eng, step):
            for i, stages in ((-2, "L"), (-1, "LF"), (0, "LFS"), (1, "LFSB"), (2, "LFSBX"), (3, "LFSBXY")):
                step(i, i % 2, stages)
            with eng.Fori(2, NTILES // 2 - 1) as j:
                for k in range(2):
                    step(j * 2 + k, k, "LFSBXY")
            for i, stages in ((NTILES - 2, "FSBXY"), (NTILES - 1, "SBXY"), (NTILES, "BXY"), (NTILES + 1, "XY"),
                              (NTILES + 2, "Y")):
                step(i, i % 2, stages)

        def products_done(eng, i, c):
            eng.wait_ge(M["prodv"], AHEAD + i * len(PV) + len([x for x in PV if x <= c]))
            eng.wait_ge(M["prodp"], AHEAD + i * len(PP) + len([x for x in PP if x <= c]))

        def tiles(eng, body):
            with eng.Fori(0, NTILES // 2 - 1) as j:
                for k in range(2):
                    body(j * 2 + k, k, True)
            body(NTILES - 2, 0, True)
            body(NTILES - 1, 1, False)

        def flat(t):
            return t[:].rearrange("p a b -> p (a b)")

        def chunk_product(i, c):
            t0, tq = (c % HC) * CH, (c % QC) * CH
            return (prod[(c // QC) % 2][:].rearrange("p n e t -> p e n t")[:, :, :, tq:tq + CH],
                    hb[c % 2][:].rearrange("p (e n) s -> p e n s", e=EB)[:, :, :, 1:SL],
                    cbc[c // HC][:, :, t0:t0 + CH].rearrange("p (e n) s -> p e n s", e=1).broadcast_to([P, EB, N, CH]))

        block = ctx.enter_context(nc.Block())
        x1d, x2d, x3d = dram["x1d"], dram["x2d"], dram["x3d"]

        @block.sync
        def _(sp):
            for t, n in resident:
                sp.dma_start(t[:], dram[n]).then_inc(s_w, 16)
            head_start(sp, (M, sp_m), (R, sp_x), (A, sp_a))

            def step(i, k, stages):
                if "L" in stages:
                    sp.wait_ge(M["y1"], AHEAD + i + 2)
                    sp.dma_start(xt[0][:], flat_tile(dram["x"], i + 2)).then_inc(M["x"], 16)
                if "B" in stages:
                    sp.wait_ge(M["x1"], AHEAD + i - 1)
                    sp.dma_start(xt[1][:], flat_tile(dram["x"], i - 1)).then_inc(M["xr"], 16)
                if "Y" in stages:
                    sp.wait_ge(R["ac"], AHEAD + (i - 2) * (X + 1))
                    sp.dma_start(flat_tile(x2d, i - 3), macc[1 - k][:]).then_inc(R["o"][1 - k], 16)
            pipeline(sp, step)
            for k in range(2):
                sp.wait_ge(R["o"][k], AHEAD + NTILES // 2 * 16)

            def experts(src, dst, n0):
                def load(i, k):
                    sp.dma_start(mxt[k][:], flat_tile(src, i)).then_inc(R["x"][k], 16)

                def store(i, k):
                    sp.wait_ge(R["ac"], AHEAD + (i + n0 + 1) * (X + 1))
                    sp.dma_start(flat_tile(dst, i), macc[k][:]).then_inc(R["o"][k], 16)

                for k in range(2):
                    load(k, k)
                with sp.Fori(0, NTILES // 2 - 1) as j:
                    for k in range(2):
                        sp.wait_ge(R["ac"], AHEAD + (j * 2 + k + n0) * (X + 1) + 1)
                        load(j * 2 + k + 2, k)
                        store(j * 2 + k, k)
                for k in range(2):
                    store(NTILES - 2 + k, k)
                for k in range(2):
                    sp.wait_ge(R["o"][k], AHEAD + (NTILES + n0) // 2 * 16)
            sp.dma_start(w_a, dram["w_qkvo"]).then_inc(s_wa, 16)

            def load(b, t):
                buf, sem, _ = inputs_a[t % 4]
                sp.wait_ge(A["xn"], AHEAD + b * NT + t - 3)
                sp.dma_start(buf[:], flat_tile(x2d, b * NT + t)).then_inc(sem, 16)

            def residual(n, k):
                sp.wait_ge(A["x3"], AHEAD + n - 1)
                sp.dma_start(xq[k][:], flat_tile(x2d, n)).then_inc(A["q"][k], 16)

            def outputs(b, more):
                for t in range(NT):
                    if more and 2 <= t < NT - 2:
                        load(b + 1, t + 2)
                    sp.wait_ge(A["x3"], AHEAD + b * NT + t + 1)
                    sp.dma_start(flat_tile(x3d, b * NT + t), x1b[t % 2][:]).then_inc(A["o"][t % 2], 16)
                    if more or t < NT - 2:
                        residual(b * NT + t + 2, t % 2)

            for t in range(NT):
                load(0, t)
            for t in range(2):
                residual(t, t)
            with sp.Fori(0, NB - 1) as b:
                for t in range(4):
                    load(b + 1, t)
                outputs(b, True)
            outputs(NB - 1, False)
            for k in range(2):
                sp.wait_ge(A["o"][k], AHEAD + NTILES // 2 * 16)
            experts(x3d, out, NTILES)

        @block.gpsimd
        def _(g):
            head_start(g, (M, pool_m))
            TT = nc.gpsimd.tensor_tensor

            def product(i, k, c):
                g.wait_ge(M["hs"], AHEAD + i * NC + c + 1)
                g.wait_ge(M["bbs"], AHEAD + i * 8 + (c // HC) * 4 + 4)
                g.wait_ge(M["y"], AHEAD + i * 4 + c // QC - 1)
                dst, states, cc = chunk_product(i, c)
                TT(dst, states, cc, ALU.mult).then_inc(M["prodp"], 1)

            def inputs(i, k, c):
                g.wait_ge(M["u"], AHEAD + i + 1)
                g.wait_ge(M["bbs"], AHEAD + i * 8 + (c // HC) * 4 + 2)
                products_done(g, i if c >= 2 else i - 1, (c - 2) % NC)
                t0, half = c * CH, c // HC
                TT(hb[c % 2][:].rearrange("p (e n) s -> p e n s", e=EB)[:, :, :, 1:SL],
                   u[k][:, :, t0:t0 + CH].rearrange("p e (n s) -> p e n s", n=1).broadcast_to([P, EB, N, CH]),
                   bbc[half][:, :, t0 - half * HT:t0 - half * HT + CH].rearrange("p (e n) s -> p e n s", e=1)
                   .broadcast_to([P, EB, N, CH]), ALU.mult).then_inc(M["bt"], 1)

            def extra(i, k, c, stages):
                if c == 1 and "F" in stages:
                    g.wait_ge(M["xcc"], AHEAD + i + 2)
                    g.wait_ge(M["sx"], AHEAD + i + 2)
                    TT(xcv[:], xcv[:], sg[:], ALU.mult).then_inc(M["xcv"], 1)
                if c == 2 and "B" in stages:
                    g.wait_ge(M["yd"], AHEAD + i)
                    TT(xd[1 - k][:], xd[1 - k][:], sz[1 - k][:], ALU.mult).then_inc(M["yg"], 1)
                if c == 4 and "F" in stages:
                    g.wait_ge(M["xcv"], AHEAD + i + 2)
                    g.wait_ge(M["dt"], AHEAD + i + 2)
                    TT(u[1 - k][:], dt[:], xcv[:], ALU.mult).then_inc(M["u"], 1)
                if c == 4 and "S" in stages:
                    g.wait_ge(M["zc"], AHEAD + i + 1)
                    g.wait_ge(M["ss"], AHEAD + i + 1)
                    TT(sz[k][:], sz[k][:], sg[:], ALU.mult).then_inc(M["sz"], 1)
                if c == 0 and "X" in stages:
                    g.wait_ge(M["o3"], AHEAD + i - 1)
                    TT(oo[:], oo[:], ga_row[:], ALU.mult).then_inc(M["o4"], 1)
                    g.wait_ge(M["o4"], AHEAD + i - 1)
                    TT(oo[:], oo[:], be_row[:], ALU.add).then_inc(M["o5"], 1)
                    g.wait_ge(M["o5"], AHEAD + i - 1)
                    g.wait_ge(M["xr"], AHEAD + (i - 1) * 16)
                    g.wait_ge(R["ac"], AHEAD + (i - 4) * (X + 1) + 1)
                    TT(x1b[k][:], oo[:], xt[1][:], ALU.add).then_inc(M["x1"], 1)

            def step(i, k, stages):
                for c in range(NC):
                    if c == 0 and "B" in stages and NC - 1 in PP:
                        product(i - 1, 1 - k, NC - 1)
                    if c > 0 and "S" in stages and c - 1 in PP:
                        product(i, k, c - 1)
                    if c < NC - 1 and "S" in stages:
                        inputs(i, k, c + 1)
                    extra(i, k, c, stages)
                if "F" in stages:
                    inputs(i + 1, 1 - k, 0)
            g.wait_ge(s_w, 16 * len(resident))
            pipeline(g, step)

        @block.scalar
        def _(a):
            act = nc.scalar.activation
            nc.scalar.preload_act_table_set("natural_log_exp_and_others")
            head_start(a, (M, act_m), (R, act_x), (A, act_a))
            a.wait_ge(s_w, 16 * len(resident))
            a.wait_ge(s_setup, 1)
            act(aneg[:], aneg[:], ACT.Exp).then_inc(s_aexp, 1)
            a.wait_ge(s_setup, 3)

            def spread(i, h, w):
                if w == 0:
                    a.wait_ge(M["bt"], AHEAD + (i - 1) * NC + (h + 1) * HC)
                else:
                    products_done(a, i - 1, (h + 1) * HC - 1)
                for q in range(2):
                    a.wait_ge(M["bb"], AHEAD + i * 8 + h * 4 + w * 2 + q + 1)
                    act((bbc, cbc)[w][h][:, q * 8:q * 8 + 8, :], (BC, M1)[q][:].rearrange("p (n t) -> p n t", n=8), ACT.Copy)\
                        .then_inc(M["bbs"], 1)

            def decays(i, k, lo, hi):
                if lo == 0:
                    a.wait_ge(M["dt"], AHEAD + i + 1)
                    a.wait_ge(M["scan"], AHEAD + (i - 1) * NC)
                for s in range(lo, hi):
                    last = act(dA[k][:, :, s, 1:SL], dt[:, s // N, :].rearrange("p (c s) -> p c s", c=NC), ACT.Exp,
                               scale=aneg[:, s:s + 1])
                if hi == ST:
                    last.then_inc(M["dA"], 1)

            def norms(i, c):
                q = i * NC + c
                a.wait_ge(M["nr"], AHEAD + q + 1)
                act(nrm[:], nrm[:], ACT.Ln, bias=c_tiny[:]).then_inc(M["nl"], 1)
                a.wait_ge(M["nl"], AHEAD + q + 1)
                act(nrm[:], nrm[:], ACT.Exp, scale=-0.5, bias=c_ln10[:]).then_inc(M["ne"], 1)

            def route_norm(n):
                a.wait_ge(R["mv"], AHEAD + n + 1)
                act(ms[:, 0:1], mmv[:, 1:2], ACT.Ln, bias=c_eps5[:]).then_inc(R["ln"], 1)
                a.wait_ge(R["ln"], AHEAD + n + 1)
                act(ms[:, 1:2], ms[:, 0:1], ACT.Exp, scale=-0.5).then_inc(R["rs"], 1)

            def route_copy(n, k):
                a.wait_ge(R["xT"], AHEAD + n + 1)
                a.wait_ge(R["mm"], AHEAD + (n - 1) * 8)
                act(flat(mxT[k]), M0[:, 0:D], ACT.Copy).then_inc(R["xTs"], 1)

            def route_exp(n):
                a.wait_ge(R["nm"], AHEAD + n + 1)
                act(ex[:], lgt[:], ACT.Exp, bias=ms[:, 2:3], accum_out=ms[:, 3:4]).then_inc(R["ex"], 1)

            def step(i, k, stages):
                for c in range(NC):
                    if "S" in stages:
                        norms(i, c)
                    if c == 0 and "S" in stages:
                        spread(i, 0, 1)
                        spread(i, 1, 0)
                    if c == 1 and "S" in stages:
                        spread(i, 1, 1)
                    if c == 0 and "F" in stages:
                        a.wait_ge(M["xcc"], AHEAD + i + 2)
                        a.wait_ge(M["sz"], AHEAD + i)
                        act(sg[:], xcv[:], ACT.Exp, scale=-1.0).then_inc(M["ex"], 1)
                        a.wait_ge(M["ex"], AHEAD + i + 2)
                        act(sg[:], sg[:], ACT.Ln, bias=c_one[:]).then_inc(M["lx"], 1)
                        a.wait_ge(M["lx"], AHEAD + i + 2)
                        act(sg[:], sg[:], ACT.Exp, scale=-1.0).then_inc(M["sx"], 1)
                    if c == 1 and "X" in stages:
                        route_norm(i - 2)
                    if c == 2:
                        if "S" in stages:
                            a.wait_ge(M["zc"], AHEAD + i + 1)
                            a.wait_ge(M["xcv"], AHEAD + (i + 2 if "F" in stages else NTILES))
                            act(sg[:], sz[k][:], ACT.Exp, scale=-1.0).then_inc(M["ez"], 1)
                            a.wait_ge(M["ez"], AHEAD + i + 1)
                            act(sg[:], sg[:], ACT.Ln, bias=c_one[:]).then_inc(M["lz"], 1)
                            a.wait_ge(M["lz"], AHEAD + i + 1)
                            act(sg[:], sg[:], ACT.Exp, scale=-1.0).then_inc(M["ss"], 1)
                        if "F" in stages:
                            a.wait_ge(M["dtc"], AHEAD + i + 2)
                            act(dt[:], dt[:], ACT.Exp).then_inc(M["edt"], 1)
                            a.wait_ge(M["edt"], AHEAD + i + 2)
                            act(dt[:], dt[:], ACT.Ln, bias=c_one[:]).then_inc(M["ldt"], 1)
                    if c == 3:
                        if "X" in stages:
                            route_copy(i - 2, k)
                    if c == 6:
                        if "B" in stages:
                            a.wait_ge(M["vc3"], AHEAD + i)
                            act(sc[:, 8:9], sc[:, 7:8], ACT.Ln).then_inc(M["ln3"], 1)
                            a.wait_ge(M["ln3"], AHEAD + i)
                            act(sc[:, 9:10], sc[:, 8:9], ACT.Exp, scale=0.5).then_inc(M["sd3"], 1)
                    if c == 4:
                        if "X" in stages:
                            route_exp(i - 2)
                    if c == 4 and "L" in stages:
                        a.wait_ge(M["mv1"], AHEAD + i + 3)
                        act(sc[:, 0:1], mv[:, 0, 1:2], ACT.Ln, bias=c_eps5[:]).then_inc(M["ln1"], 1)
                        a.wait_ge(M["ln1"], AHEAD + i + 3)
                        a.wait_ge(M["keep"], AHEAD + i + 1)
                        act(ln1[k][:, 1:2], sc[:, 0:1], ACT.Exp, scale=-0.5).then_inc(M["rs1"], 1)
                    if c == 5 and "F" in stages:
                        spread(i + 1, 0, 0)
                    if c == 5 and "L" in stages:
                        a.wait_ge(M["vc2"], AHEAD + i + 3)
                        act(sc[:, 3:4], sc[:, 2:3], ACT.Ln).then_inc(M["ln2"], 1)
                        a.wait_ge(M["ln2"], AHEAD + i + 3)
                        act(sc[:, 4:5], sc[:, 3:4], ACT.Exp, scale=0.5).then_inc(M["sd2"], 1)
                    if c == 7 and "L" in stages:
                        a.wait_ge(M["xnT"], AHEAD + i + 3)
                        a.wait_ge(M["z"], AHEAD + i + 2)
                        for j in range(KD):
                            act(xnT[:, j, :], F0[:, j * P:(j + 1) * P], ACT.Identity, bias=be_in[:, j:j + 1],
                                scale=ga_in[:, j:j + 1]).then_inc(M["xnTs"], 1)
                    if "F" in stages and DECAYS[c] < DECAYS[c + 1]:
                        decays(i + 1, 1 - k, DECAYS[c], DECAYS[c + 1])
            pipeline(a, step)

            def experts(n0):
                def route_tile(n, k):
                    route_norm(n)
                    route_copy(n, k)
                    route_exp(n)
                route_tile(n0, 0)
                tiles(a, lambda i, k, more: route_tile(i + n0 + 1, 1 - k) if more else None)

            def norm(b, t):
                n, k = b * NT + t, t % 2
                if t < NT:
                    a.wait_ge(A["mv"], AHEAD + n + 1)
                    act(sc[:, 2 * k:2 * k + 1], mv[:, k, 1:2], ACT.Ln, bias=c_eps5[:]).then_inc(A["ln"], 1)
                    a.wait_ge(A["ln"], AHEAD + n + 1)
                    act(sc[:, 2 * k + 1:2 * k + 2], sc[:, 2 * k:2 * k + 1], ACT.Exp, scale=-0.5).then_inc(A["rn"], 1)
                if t > 0:
                    a.wait_ge(A["xT"], AHEAD + n)
                    act(xTa[:, :, (t - 1) * P:t * P], (F0, F1)[(t - 1) % 2][:, 0:D].rearrange("p (j l) -> p j l", j=KD),
                        ACT.Copy).then_inc(A["xTs"], 1)

            def attend(b, more):
                for w, dst in ((0, qa), (1, ka), (2, va)):
                    for j in range(KD):
                        for g in range(NG):
                            m = (w * KD + j) * NG + g
                            a.wait_ge(A["pj"], AHEAD + b * 12 + m + 1)
                            s = (BC, YP, G0, G1)[m % 4]
                            o = dst[:, j, g * TG:(g + 1) * TG]
                            if w < 2:
                                act(o, s[:], ACT.Sigmoid, bias=b_qkv[:, w, j:j + 1],
                                    accum_out=ac[:, m:m + 1]).then_inc(A["pjs"], 1)
                            else:
                                act(o, s[:], ACT.Identity, bias=b_qkv[:, w, j:j + 1]).then_inc(A["pjs"], 1)
                nc.scalar.preload_act_table_set("natural_log_exp_and_others")
                a.wait_ge(A["cv"], AHEAD + b + 1)
                for banks, dst, mmd, l, r, c0 in (((BC, YP, G0, G1), r1, "si", "l1", "r1", 16),
                                                  ((F0, F1, M0, M1), r2, "so", "l2", "r2", 18)):
                    for m in range(4):
                        j, g = m // NG, m % NG
                        a.wait_ge(A[mmd], AHEAD + b * 4 + m + 1)
                        act(dst[:, j, g * TG:(g + 1) * TG], banks[m][:], ACT.Ln, bias=ac[:, c0 + j:c0 + j + 1])\
                            .then_inc(A[l], 1)
                    for m in range(4):
                        j, g = m // NG, m % NG
                        a.wait_ge(A[l], AHEAD + b * 4 + m + 1)
                        o = dst[:, j, g * TG:(g + 1) * TG]
                        act(o, o, ACT.Exp, scale=-1.0).then_inc(A[r], 1)
                for j in range(KD):
                    a.wait_ge(A["nm"], AHEAD + b + 1)
                    act(xTa[:, j, :], xTa[:, j, :], ACT.Exp, bias=ac[:, 42 + j:43 + j], accum_out=ac[:, 44 + j:45 + j])\
                        .then_inc(A["e"], 1)
                for m in range(4):
                    j, g = m // NG, m % NG
                    a.wait_ge(A["ci"], AHEAD + b * 4 + m + 1)
                    act(r2[:, j, g * TG:(g + 1) * TG], (BC, YP, G0, G1)[m][:], ACT.Sigmoid, bias=ac[:, 36 + j:37 + j])\
                        .then_inc(A["sa"], 1)
                for t in range(NT):
                    a.wait_ge(A["kvT"], AHEAD + b * NT + t + 1)
                    act(kv[:, t, :], (BC, YP, G0, G1)[t % 4][:], ACT.Copy).then_inc(A["kvs"], 1)
                nc.scalar.preload_act_table_set("natural_log_exp_and_others")
                if more:
                    for t in range(NT + 1):
                        norm(b + 1, t)

            for t in range(NT + 1):
                norm(0, t)
            with a.Fori(0, NB - 1) as b:
                attend(b, True)
            attend(NB - 1, False)
            experts(NTILES)

        @block.tensor
        def _(pe):
            mm = nc.tensor.matmul
            head_start(pe, (M, pe_m), (R, pe_x), (A, pe_a))
            pe.wait_ge(s_w, 16 * len(resident))

            def sum_states(i, h):
                products_done(pe, i, (h + 1) * QC - 1)
                pe.wait_ge(M["yd"], AHEAD + i)
                for n in range(N):
                    last = mm(YP[:, h * P:(h + 1) * P], ident[:],
                              prod[h % 2][:, n, :, :].rearrange("p e t -> p (e t)"), start=(n == 0), stop=(n == N - 1))
                last.then_inc(M["y"], 1)

            def spread(i, h, w):
                pe.wait_ge(M["bcl"], AHEAD + i + 1)
                for q in range(2):
                    pe.wait_ge(M["bbs"], AHEAD + i * 8 + h * 4 + w * 2 + q - 1)
                    for n in range(8):
                        r = (w * 2 + q) * 8 + n
                        last = mm((BC, M1)[q][:, n * HT:(n + 1) * HT], sel[:, r:r + 1].broadcast_to([3 * RB, P]),
                                  bcs[:, h * HT:(h + 1) * HT], start=True, stop=True)
                    last.then_inc(M["bb"], 1)

            def route(n, k):
                pe.wait_ge(R["xn"], AHEAD + n + 1)
                pe.wait_ge(R["lgb"], AHEAD + n)
                for j in range(KD):
                    last = nc.tensor.transpose(M0[:, j * P:(j + 1) * P], mxn[:, j * P:(j + 1) * P], ident[:])
                last.then_inc(R["xT"], 1)

            def logits(n, k):
                pe.wait_ge(R["xTs"], AHEAD + n + 1)
                for j in range(KD):
                    last = mm(M0[:, D:D + X], mxT[k][:, j, :], w_r[:, j, :], start=(j == 0), stop=(j == KD - 1))
                last.then_inc(R["lg"], 1)

            def experts_mm(n, k, lo, hi, banks=G):
                for p in range(lo, hi):
                    r = p - len(banks) + (0 if p >= len(banks) else X // 2)
                    pe.wait_ge(R["ac"], AHEAD + n * (X + 1) + 2 * r + 3 - (0 if p >= len(banks) else X + 1))
                    for j in range(KD):
                        last = mm(banks[p % len(banks)][:], mxT[k][:, j, :], w_x[:, j, p * 512:(p + 1) * 512],
                                  start=(j == 0), stop=(j == KD - 1))
                    last.then_inc(R["mm"], 1)

            def step(i, k, stages):
                for c in range(NC):
                    if c == 0 and "S" in stages:
                        spread(i, 0, 1)
                        spread(i, 1, 0)
                    if c == 0 and "B" in stages:
                        sum_states(i - 1, 3)
                    if c == 7 and "X" in stages:
                        experts_mm(i - 2, k, 0, 1)
                    if c < 7 and "Y" in stages:
                        experts_mm(i - 3, 1 - k, c + 1, c + 2)
                    if c == 1:
                        if "S" in stages:
                            spread(i, 1, 1)
                        if "F" in stages:
                            pe.wait_ge(M["xcv"], AHEAD + i + 2)
                            pe.wait_ge(R["lgb"], AHEAD + i - 2)
                            for e in range(EB):
                                last = mm(M0[0:3 * RB, XP:XP + P], w_xp[:, e, :], xcv[:, e, :], start=(e == 0),
                                          stop=(e == EB - 1))
                            last.then_inc(M["bc"], 1)
                            pe.wait_ge(M["xib"], AHEAD + i + 2)
                            for m in range(EB):
                                for e in range(EB):
                                    last = mm(F0[:, m * P:(m + 1) * P], w_dt[:, e, m * P:(m + 1) * P], xcv[:, e, :],
                                              start=(e == 0), stop=(e == EB - 1))
                            last.then_inc(M["dtp"], 1)
                    if c == 3 and "X" in stages:
                        if "F" in stages:
                            pe.wait_ge(M["bcv"], AHEAD + i + 2)
                        route(i - 2, k)
                    if c in (3, 5, 7) and "S" in stages:
                        sum_states(i, (c - 3) // 2)
                    if c == 4 and "X" in stages:
                        logits(i - 2, k)
                    if c == 4:
                        if "B" in stages:
                            pe.wait_ge(M["yg"], AHEAD + i)
                            pe.wait_ge(M["dtb"], AHEAD + (i + 2 if "F" in stages else NTILES))
                            for e in range(EB):
                                last = mm(F0[:, 0:D], xd[1 - k][:, e, :], w_out[:, e, :], start=(e == 0), stop=(e == EB - 1))
                            last.then_inc(M["op"], 1)
                        if "F" in stages:
                            pe.wait_ge(s_setup, 3)
                            spread(i + 1, 0, 0)
                    if c == 6 and "L" in stages:
                        pe.wait_ge(M["xn"], AHEAD + i + 3)
                        pe.wait_ge(M["o1"], AHEAD + (i if "B" in stages else 0))
                        for j in range(KD):
                            last = nc.tensor.transpose(F0[:, j * P:(j + 1) * P], xn[:, j * P:(j + 1) * P], ident[:])
                        last.then_inc(M["xnT"], 1)
                    if c == 7 and "L" in stages:
                        pe.wait_ge(M["xnTs"], AHEAD + (i + 3) * KD)
                        pe.wait_ge(M["zb"], AHEAD + i + 2)
                        for half, bank, s in ((0, F0, "xi"), (1, F1, "z")):
                            for m in range(EB):
                                for j in range(KD):
                                    last = mm(bank[:, m * P:(m + 1) * P],
                                              w_in[:, j, (half * EB + m) * P:(half * EB + m + 1) * P],
                                              xnT[:, j, :], start=(j == 0), stop=(j == KD - 1))
                            last.then_inc(M[s], 1)
            pipeline(pe, step)

            def experts(n0):
                def tile(i, k, more):
                    n = i + n0
                    experts_mm(n, k, 0, 3, G4)
                    if more:
                        route(n + 1, 1 - k)
                    experts_mm(n, k, 3, 4, G4)
                    if more:
                        logits(n + 1, 1 - k)
                    experts_mm(n, k, 4, X // 2, G4)
                route(n0, 0)
                logits(n0, 0)
                tiles(pe, tile)

            pe.wait_ge(s_wa, 16)
            quads = ((BC, YP, G0, G1), (F0, F1, M0, M1))

            def by_group(banks, mats_, src, s, before):
                for m in range(4):
                    j, g = m // NG, m % NG
                    before(m)
                    mm(banks[m][:], mats_[j], src[:, j, g * TG:(g + 1) * TG], start=True, stop=True).then_inc(A[s], 1)

            def transposes(b, t):
                n = b * NT + t
                pe.wait_ge(A["xn"], AHEAD + n + 1)
                pe.wait_ge(A["xTs"], AHEAD + n - 1)
                for j in range(KD):
                    last = nc.tensor.transpose((F0, F1)[t % 2][:, j * P:(j + 1) * P], mxn[:, j * P:(j + 1) * P], ident[:])
                last.then_inc(A["xT"], 1)

            def attend(b, more):
                pe.wait_ge(A["xTs"], AHEAD + (b + 1) * NT)
                pe.wait_ge(A["x2"], AHEAD + b * NT)
                for w in range(3):
                    for j in range(KD):
                        for g in range(NG):
                            m = (w * KD + j) * NG + g
                            if m >= 4:
                                pe.wait_ge(A["pjs"], AHEAD + b * 12 + m - 3)
                            for kk in range(KD):
                                last = mm(quads[0][m % 4][:], w_a[:, w, kk, j * P:(j + 1) * P],
                                          xTa[:, kk, g * TG:(g + 1) * TG], start=(kk == 0), stop=(kk == KD - 1))
                            last.then_inc(A["pj"], 1)
                pe.wait_ge(A["hm"], AHEAD + (b + 1) * 4)
                for m in range(4):
                    last = mm(M0[:, m:m + 1], mats[:, m, :], c_eps6[:], start=True, stop=True)
                last.then_inc(A["cv0"], 1)
                by_group(quads[0], (mats[:, 0, :], mats[:, 1, :]), qa, "si",
                         lambda m: pe.wait_ge(A["pjs"], AHEAD + (b + 1) * 12))
                by_group(quads[1], (mats[:, 2, :], mats[:, 3, :]), ka, "so",
                         lambda m: pe.wait_ge(A["cv"], AHEAD + b + 1))
                pe.wait_ge(A["hn"], AHEAD + (b + 1) * 4)
                pe.wait_ge(A["l2"], AHEAD + (b + 1) * 4)
                for m in range(4):
                    last = mm(M0[:, m:m + 1], mats[:, 4 + m, :], c_eps6[:], start=True, stop=True)
                last.then_inc(A["cw0"], 1)
                by_group(quads[0], (mats[:, 4, :], mats[:, 5, :]), qa, "ci",
                         lambda m: pe.wait_ge(A["l1"], AHEAD + (b + 1) * 4))
                by_group(quads[1], (mats[:, 6, :], mats[:, 7, :]), ka, "co",
                         lambda m: pe.wait_ge(A["cw"], AHEAD + b + 1))
                pe.wait_ge(A["v"], AHEAD + (b + 1) * KD)
                for t in range(NT):
                    if t < 4:
                        pe.wait_ge(A["sa"], AHEAD + b * 4 + t + 1)
                    else:
                        pe.wait_ge(A["kvs"], AHEAD + b * NT + t - 3)
                    for c, src in enumerate((ka, va)):
                        for j in range(KD):
                            last = nc.tensor.transpose(quads[0][t % 4][:, (c * KD + j) * P:(c * KD + j + 1) * P],
                                                       src[:, j, t * P:(t + 1) * P], ident[:])
                    last.then_inc(A["kvT"], 1)
                pe.wait_ge(A["kvs"], AHEAD + (b + 1) * NT)
                pe.wait_ge(A["cc"], AHEAD + b + 1)
                for j in range(KD):
                    for t in range(NT):
                        last = mm(M0[:, j * P:(j + 1) * P], kv[:, t, j * P:(j + 1) * P], kv[:, t, D + j * P:D + (j + 1) * P],
                                  start=(t == 0), stop=(t == NT - 1))
                last.then_inc(A["kv0"], 1)
                pe.wait_ge(A["kvm"], AHEAD + (b + 1) * KD)
                by_group((F0, F1, M1, G1), (mats[:, 8, :], mats[:, 9, :]), r1, "om",
                         lambda m: None)
                for t in range(NT):
                    if t == 0:
                        pe.wait_ge(A["og"], AHEAD + (b + 1) * 4)
                    pe.wait_ge(A["x2"], AHEAD + b * NT + t - 1)
                    for j in range(KD):
                        last = mm((BC, YP)[t % 2][:, 0:D], r2[:, j, t * P:(t + 1) * P], w_a[:, 3, j, :],
                                  start=(j == 0), stop=(j == KD - 1))
                    last.then_inc(A["om2"], 1)
                    if more and t > 1:
                        transposes(b + 1, t - 2)
                if more:
                    transposes(b + 1, NT - 2)
                    transposes(b + 1, NT - 1)

            for t in range(NT):
                transposes(0, t)
            with pe.Fori(0, NB - 1) as b:
                attend(b, True)
            attend(NB - 1, False)
            experts(NTILES)

        @block.vector
        def _(v):
            V = nc.vector
            TT, TS, STT = V.tensor_tensor, V.tensor_scalar, V.scalar_tensor_tensor
            head_start(v, (M, dve_m), (R, dve_x), (A, dve_a))
            for c, val in ((c_one, 1.0), (c_eps5, 1e-5), (c_ln10, math.log(10.0)), (c_eps6, 1e-6), (c_tiny, 1e-12), (prx[:, X:X + 2], -1.0)):
                V.memset(c[:] if c is not prx else c, val)
            for k in range(2):
                last = V.memset(dA[k][:, :, :, 0:1], 0.0)
            last.then_inc(s_setup, 1)
            v.wait_ge(s_w, 16 * len(resident))
            v.wait_ge(s_aexp, 1)
            V.tensor_copy(sel[:], self32[:]).then_inc(s_setup, 1)
            TS(aneg[:], aneg[:], -1.0, None, ALU.mult).then_inc(s_setup, 1)

            def settle():
                v.sem_inc(s_settle, 1)

            def bias4(t):
                return t.rearrange("p (e t) -> p e t", t=1).broadcast_to([P, EB, P])

            def bank4(t):
                return t[:].rearrange("p (e t) -> p e t", e=EB)

            def convolve(i, k, j, also):
                v.wait_ge(M["conv"], AHEAD + i * TAPS * EB)
                if j is None:
                    V.tensor_copy(xin[:, :, 0:TAPS - 1], xin[:, :, P:]).then_inc(M["carry"], 1)
                else:
                    TS(xin[:, :, 0:TAPS - 1], xin[:, :, P:], carry[:, bass.ds(j, 1)], None, ALU.mult).then_inc(M["carry"], 1)
                v.wait_ge(M["xi"], AHEAD + i + 1)
                v.wait_ge(M["carry"], AHEAD + i + 1)
                TT(xin[:, :, TAPS - 1:], bank4(F0), bias4(b_in[:, 0:EB]), ALU.add).then_inc(M["xib"], 1)
                v.wait_ge(M["xib"], AHEAD + i + 1)
                v.wait_ge(M["u"], AHEAD + i)
                v.wait_ge(M["dtp"], AHEAD + i)
                for t in range(TAPS):
                    for e in range(EB):
                        if t == 0:
                            TS(xcv[:, e, :], xin[:, e, 0:P], cw[:, e, 0:1], cb[:, e:e + 1], ALU.mult, ALU.add)\
                                .then_inc(M["conv"], 1)
                        else:
                            v.wait_ge(M["conv"], AHEAD + (i * TAPS + t - 1) * EB + e + 1)
                            STT(xcv[:, e, :], xin[:, e, t:t + P], cw[:, e, t:t + 1], xcv[:, e, :], ALU.mult, ALU.add)\
                                .then_inc(M["conv"], 1)
                        also(t * EB + e)
                v.wait_ge(M["conv"], AHEAD + (i + 1) * TAPS * EB)
                TS(xcv[:], xcv[:], -40.0, None, ALU.max).then_inc(M["xcc"], 1)

            def split_high(i):
                v.wait_ge(M["bcv"], AHEAD + i + 1)
                v.wait_ge(M["bb"], AHEAD + i * 8)
                V.tensor_copy(bcs[:], bcv[:]).then_inc(M["bch"], 1)

            def split_rest(i):
                v.wait_ge(M["bch"], AHEAD + i + 1)
                TT(bcv[:], bcv[:], bcs[:], ALU.subtract).then_inc(M["bcr"], 1)
                v.wait_ge(M["bcr"], AHEAD + i + 1)
                V.tensor_copy(bcs[RB:2 * RB, :], bcv[RB:2 * RB, :]).then_inc(M["bcm"], 1)
                V.tensor_copy(bcs[2 * RB:, :], bcv[2 * RB:, :]).then_inc(M["bcm"], 1)
                v.wait_ge(M["bcm"], AHEAD + (i + 1) * 2)
                TT(bcv[2 * RB:, :], bcv[2 * RB:, :], bcs[2 * RB:, :], ALU.subtract).then_inc(M["bcr2"], 1)
                v.wait_ge(M["bcr2"], AHEAD + i + 1)
                V.tensor_copy(bcs[2 * RB:, :], bcv[2 * RB:, :]).then_inc(M["bcl"], 1)

            def clip(i, k, c):
                TS(dA[k][:, c, :, 1:SL], dA[k][:, c, :, 1:SL], math.exp(-10.0), None, ALU.max).then_inc(M["clip"], 1)

            def scan(i, k, c, also):
                q = i * NC + c
                cur = hb[c % 2]
                v.wait_ge(M["clip"], AHEAD + q + 1)
                v.wait_ge(M["bt"], AHEAD + q + 1)
                v.wait_ge(M["st0"], AHEAD + q)
                states = cur[:].rearrange("p a b -> p (a b)")
                V.tensor_tensor_scan(states, dA[k][:, c, :, :].rearrange("p a b -> p (a b)"), states, 0.0, ALU.mult,
                                     ALU.add).then_inc(M["scan"], 1)
                also(0)
                v.wait_ge(M["scan"], AHEAD + q + 1)
                end = cur[:, :, CH:SL].rearrange("p a b -> p (a b)")
                TT(sq[:], end, end, ALU.mult).then_inc(M["sq"], 1)
                also(1)
                v.wait_ge(M["sq"], AHEAD + q + 1)
                v.wait_ge(M["ne"], AHEAD + q)
                V.tensor_reduce(nrm[:], sq[:].rearrange("p (e n) -> p e n", e=EB), AX.X, ALU.add).then_inc(M["nr"], 1)

            def bound(i, c):
                q = i * NC + c
                cur, nxt = hb[c % 2], hb[(c + 1) % 2]
                v.wait_ge(M["ne"], AHEAD + q + 1)
                last = cur[:, :, CH:SL].rearrange("p (e n) s -> p e (n s)", e=EB)
                factor = nrm[:].rearrange("p (e t) -> p e t", t=1).broadcast_to([P, EB, N])
                STT(nxt[:, :, 0:1].rearrange("p (e n) s -> p e (n s)", e=EB), factor, 1.0, last, ALU.min, ALU.mult)\
                    .then_inc(M["st0"], 1)
                STT(last, factor, 1.0, last, ALU.min, ALU.mult).then_inc(M["hs"], 1)

            def product(i, c):
                v.wait_ge(M["hs"], AHEAD + i * NC + c + 1)
                v.wait_ge(M["bbs"], AHEAD + i * 8 + (c // HC) * 4 + 4)
                v.wait_ge(M["y"], AHEAD + i * 4 + c // QC - 1)
                dst, states, cc = chunk_product(i, c)
                TT(dst, states, cc, ALU.mult).then_inc(M["prodv"], 1)

            def route_norm1(n, k, ready):
                ready()
                V.bn_stats(mst[:], mxt[k][:]).then_inc(R["st"], 1)
                v.wait_ge(R["st"], AHEAD + n + 1)
                settle()
                V.bn_aggr(mmv[:], mst[:]).then_inc(R["mv"], 1)

            def route_norm2(n, k):
                v.wait_ge(R["rs"], AHEAD + n + 1)
                v.wait_ge(R["xT"], AHEAD + n)
                TS(mxn[:], mxt[k][:], mmv[:, 0:1], ms[:, 1:2], ALU.subtract, ALU.mult).then_inc(R["xn"], 1)

            def route_scores(n, k):
                v.wait_ge(R["lg"], AHEAD + n + 1)
                TT(lgt[:], M0[:, D:D + X], rb_row[:], ALU.add).then_inc(R["lgb"], 1)
                v.wait_ge(R["lgb"], AHEAD + n + 1)
                settle()
                V.max(mx8[:], lgt[:]).then_inc(R["router"], 1)
                v.wait_ge(R["router"], AHEAD + n * ROUTER + 1)
                TS(ms[:, 2:3], mx8[:, 0:1], -1.0, None, ALU.mult).then_inc(R["nm"], 1)

            def route_step(n, k, step, stored):
                if step == 0:
                    v.wait_ge(R["ex"], AHEAD + n + 1)
                    V.reciprocal(ms[:, 4:5], ms[:, 3:4]).then_inc(R["router"], 1)
                elif step == 1:
                    v.wait_ge(R["router"], AHEAD + n * ROUTER + 2)
                    TS(prx[:, 0:X], ex[:], ms[:, 4:5], None, ALU.mult).then_inc(R["router"], 1)
                elif step == 2:
                    v.wait_ge(R["router"], AHEAD + n * ROUTER + 3)
                    settle()
                    V.max(t8[:], prx[:, 0:X]).then_inc(R["router"], 1)
                elif step == 3:
                    v.wait_ge(R["router"], AHEAD + n * ROUTER + 4)
                    V.memset(t8[:, TOPK:8], -1.0).then_inc(R["router"], 1)
                elif step == 4:
                    v.wait_ge(R["router"], AHEAD + n * ROUTER + 5)
                    settle()
                    V.match_replace(rest[:], t8[:], prx[:], 0.0).then_inc(R["router"], 1)
                elif step == 5:
                    v.wait_ge(R["router"], AHEAD + n * ROUTER + 6)
                    TT(selp[:], prx[:, 0:X], rest[:, 0:X], ALU.subtract).then_inc(R["router"], 1)
                elif step == 6:
                    v.wait_ge(R["router"], AHEAD + n * ROUTER + 7)
                    V.tensor_reduce(ms[:, 5:6], selp[:], AX.X, ALU.add).then_inc(R["router"], 1)
                elif step == 7:
                    v.wait_ge(R["router"], AHEAD + n * ROUTER + 8)
                    TS(ms[:, 6:7], ms[:, 5:6], 1e-10, None, ALU.add).then_inc(R["router"], 1)
                elif step == 8:
                    v.wait_ge(R["router"], AHEAD + n * ROUTER + 9)
                    V.reciprocal(ms[:, 7:8], ms[:, 6:7]).then_inc(R["router"], 1)
                elif step == 9:
                    v.wait_ge(R["router"], AHEAD + n * ROUTER + 10)
                    TT(ms[:, 8:9], ms[:, 5:6], ms[:, 7:8], ALU.mult).then_inc(R["router"], 1)
                elif step == 10:
                    v.wait_ge(R["router"], AHEAD + n * ROUTER + 11)
                    TS(ms[:, 9:10], ms[:, 8:9], 1e-10, None, ALU.max).then_inc(R["router"], 1)
                    TS(ms[:, 12:13], ms[:, 8:9], 1e-10, None, ALU.mult).then_inc(R["router"], 1)
                elif step == 11:
                    v.wait_ge(R["router"], AHEAD + n * ROUTER + 12)
                    V.reciprocal(ms[:, 10:11], ms[:, 9:10]).then_inc(R["router"], 1)
                elif step == 12:
                    v.wait_ge(R["router"], AHEAD + n * ROUTER + 14)
                    TT(ms[:, 11:12], ms[:, 7:8], ms[:, 10:11], ALU.mult).then_inc(R["router"], 1)
                elif step == 13:
                    stored()
                    TS(macc[k][:], mxt[k][:], ms[:, 12:13], None, ALU.add).then_inc(R["ac"], 1)
                elif step == 14:
                    v.wait_ge(R["router"], AHEAD + n * ROUTER + 15)
                    TS(gate[k][:], selp[:], ms[:, 11:12], None, ALU.mult).then_inc(R["router"], 1)
                elif step == 15:
                    v.wait_ge(R["router"], AHEAD + n * ROUTER + 16)

            def route_top(n, k, stored):
                for step in range(16):
                    route_step(n, k, step, stored)

            def expert_sums(n, k, lo, hi, banks=G):
                for e in range(lo, hi):
                    v.wait_ge(R["mm"], AHEAD + n * 8 + e // 2 + 1)
                    v.wait_ge(R["ac"], AHEAD + n * (X + 1) + 1 + e)
                    STT(macc[k][:], banks[(e // 2) % len(banks)][:, (e % 2) * D:(e % 2 + 1) * D], gate[k][:, e:e + 1], macc[k][:],
                        ALU.mult, ALU.add).then_inc(R["ac"], 1)

            def between(i, k, c, stages, j, stored):
                L_, F, B, X_ = ("L" in stages, "F" in stages, "B" in stages, "X" in stages)
                if c == 0:
                    if "S" in stages:
                        V.tensor_copy(ln1r[k][:], ln1[k][:]).then_inc(M["keep"], 1)
                    if F:
                        convolve(i + 1, 1 - k, j, lambda s: route_step(i - 3, 1 - k, s, stored) if "Y" in stages else None)
                    elif "Y" in stages:
                        route_top(i - 3, 1 - k, stored)
                if c == 1 and B:
                    v.wait_ge(M["y"], AHEAD + i * 4)
                    v.wait_ge(M["xd"], AHEAD + i * EB)
                    x4 = xd[1 - k][:].rearrange("p e (h t) -> p h e t", h=4)
                    TT(x4, x4, YP[:].rearrange("p (h e t) -> p h e t", h=4, e=EB), ALU.add).then_inc(M["yd"], 1)
                if c == 1 and X_:
                    route_norm1(i - 2, k, lambda: v.wait_ge(M["x1"], AHEAD + i - 1))
                if c == 2:
                    if X_:
                        route_norm2(i - 2, k)
                    if F:
                        v.wait_ge(M["bc"], AHEAD + i + 2)
                        TS(bcv[:], M0[0:3 * RB, XP:XP + P], b_xp[:], None, ALU.add).then_inc(M["bcv"], 1)
                        v.wait_ge(M["dtp"], AHEAD + i + 2)
                        v.wait_ge(M["dA"], AHEAD + i + 1)
                        v.wait_ge(M["u"], AHEAD + i + 1)
                        TT(dt[:], bank4(F0), bias4(b_dt[:]), ALU.add).then_inc(M["dtb"], 1)
                        split_high(i + 1)
                        v.wait_ge(M["dtb"], AHEAD + i + 2)
                        TS(dt[:], dt[:], 40.0, None, ALU.min).then_inc(M["dtc"], 1)
                        split_rest(i + 1)
                        v.wait_ge(M["ldt"], AHEAD + i + 2)
                        TS(dt[:], dt[:], 1e-4, 10.0, ALU.max, ALU.min).then_inc(M["dt"], 1)
                if c == 4:
                    if X_:
                        route_scores(i - 2, k)
                    if F:
                        v.wait_ge(M["z"], AHEAD + i + 2)
                        v.wait_ge(M["yg"], AHEAD + i)
                        TT(sz[1 - k][:], bank4(F1), bias4(b_in[:, EB:]), ALU.add).then_inc(M["zb"], 1)
                    if L_:
                        v.wait_ge(M["x"], AHEAD + (i + 3) * 16)
                        V.bn_stats(st[:, 0, :], xt[0][:]).then_inc(M["st1"], 1)
                    if F:
                        v.wait_ge(M["zb"], AHEAD + i + 2)
                        TS(sz[1 - k][:], sz[1 - k][:], -40.0, None, ALU.max).then_inc(M["zc"], 1)
                    if L_:
                        v.wait_ge(M["st1"], AHEAD + i + 3)
                        settle()
                        V.bn_aggr(mv[:, 0, :], st[:, 0, :]).then_inc(M["mv1"], 1)
                if c == 5:
                    if L_:
                        v.wait_ge(M["rs1"], AHEAD + i + 3)
                        V.tensor_copy(ln1[k][:, 0:1], mv[:, 0, 0:1])
                        TS(y1[:], xt[0][:], mv[:, 0, 0:1], ln1[k][:, 1:2], ALU.subtract, ALU.mult).then_inc(M["y1"], 1)
                    if B:
                        v.wait_ge(M["xr"], AHEAD + i * 16)
                        TS(yr[:], xt[1][:], ln1r[1 - k][:, 0:1], ln1r[1 - k][:, 1:2], ALU.subtract, ALU.mult)
                    if L_:
                        v.wait_ge(M["y1"], AHEAD + i + 3)
                        V.bn_stats(st[:, 1, :], y1[:]).then_inc(M["st2"], 1)
                    if B:
                        v.wait_ge(M["op"], AHEAD + i)
                        v.wait_ge(M["x1"], AHEAD + i - 1)
                        TT(oo[:], F0[:, 0:D], ob_row[:], ALU.add).then_inc(M["o1"], 1)
                    if L_:
                        v.wait_ge(M["st2"], AHEAD + i + 3)
                        settle()
                        V.bn_aggr(mv[:, 1, :], st[:, 1, :]).then_inc(M["mv2"], 1)
                    if B:
                        v.wait_ge(M["o1"], AHEAD + i)
                        TT(oo[:], oo[:], yr[:], ALU.add).then_inc(M["o2"], 1)
                    if L_:
                        v.wait_ge(M["mv2"], AHEAD + i + 3)
                        TS(sc[:, 2:3], mv[:, 1, 1:2], D / (D - 1.0), 1e-19, ALU.mult, ALU.max).then_inc(M["vc2"], 1)
                    if B:
                        v.wait_ge(M["o2"], AHEAD + i)
                        V.bn_stats(st[:, 2, :], oo[:]).then_inc(M["st3"], 1)
                        v.wait_ge(M["st3"], AHEAD + i)
                        settle()
                        V.bn_aggr(mv[:, 2, :], st[:, 2, :]).then_inc(M["mv3"], 1)
                        v.wait_ge(M["mv3"], AHEAD + i)
                        TS(sc[:, 7:8], mv[:, 2, 1:2], D / (D - 1.0), 1e-19, ALU.mult, ALU.max).then_inc(M["vc3"], 1)
                if c == 6:
                    if L_:
                        v.wait_ge(M["sd2"], AHEAD + i + 3)
                        TS(sc[:, 5:6], sc[:, 4:5], 1e-6, None, ALU.add).then_inc(M["se2"], 1)
                        v.wait_ge(M["se2"], AHEAD + i + 3)
                        V.reciprocal(sc[:, 6:7], sc[:, 5:6]).then_inc(M["r2"], 1)
                        v.wait_ge(M["r2"], AHEAD + i + 3)
                        v.wait_ge(M["xnT"], AHEAD + i + 2)
                        TS(xn[:], y1[:], mv[:, 1, 0:1], sc[:, 6:7], ALU.subtract, ALU.mult).then_inc(M["xn"], 1)
                    if F:
                        v.wait_ge(M["xcv"], AHEAD + i + 2)
                        v.wait_ge(M["op"], AHEAD + i)
                        for e in range(EB):
                            TS(xd[1 - k][:, e, :], xcv[:, e, :], dpar[:, e:e + 1], None, ALU.mult).then_inc(M["xd"], 1)
                if c == 7 and B:
                    v.wait_ge(M["sd3"], AHEAD + i)
                    TS(sc[:, 10:11], sc[:, 9:10], 1e-6, None, ALU.add).then_inc(M["se3"], 1)
                    v.wait_ge(M["se3"], AHEAD + i)
                    V.reciprocal(sc[:, 11:12], sc[:, 10:11]).then_inc(M["r3"], 1)
                    v.wait_ge(M["r3"], AHEAD + i)
                    TS(oo[:], oo[:], mv[:, 2, 0:1], sc[:, 11:12], ALU.subtract, ALU.mult).then_inc(M["o3"], 1)
            def step(i, k, stages):
                if isinstance(i, int):
                    j = (NT // 2 - 1 if (i + 1) % NT == 0 else 0) if (i + 1) % 2 == 0 else None
                    fresh = (NT // 2 - 1 if i % NT == 0 else 0) if i % 2 == 0 else None
                else:
                    pair = i // 2
                    j = pair % (NT // 2) if k == 1 else None
                    fresh = (pair + NT // 2 - 1) % (NT // 2) if k == 0 else None
                if "S" in stages:
                    clip_wait = v.wait_ge(M["dA"], AHEAD + i + 1)
                    clip(i, k, 0)
                    if fresh is not None:
                        v.wait_ge(M["st0"], AHEAD + i * NC)
                        first = hb[0][:, :, 0:1].rearrange("p a b -> p (a b)")
                        TS(first, first, carry[:, bass.ds(fresh, 1)], None, ALU.mult).then_inc(s_zero, 1)
                        v.wait_ge(s_zero, i // 2 + 2)
                def expert(e):
                    if "Y" in stages:
                        expert_sums(i - 3, 1 - k, e, e + 1)

                for c in range(NC):
                    if "S" in stages:
                        scan(i, k, c, lambda m: expert(2 * c + m) if c > 0 else None)
                        if c < NC - 1:
                            clip(i, k, c + 1)
                    elif c > 0:
                        expert(2 * c)
                        expert(2 * c + 1)
                    if "S" in stages and c in EARLY:
                        bound(i, c)
                        if c in PV:
                            product(i, c)
                    between(i, k, c, stages, j, lambda: v.wait_ge(R["o"][1 - k], AHEAD + (i - 4 + k) * 8))
                    if c == 0:
                        expert(0)
                        expert(1)
                    if "S" in stages and c not in EARLY:
                        bound(i, c)
                        if c in PV:
                            product(i, c)
            V.memset(hb[0][:, :, 0:1], 0.0)
            V.memset(xin[:], 0.0)
            V.memset(carry[:, 0:NT // 2 - 1], 1.0)
            V.memset(carry[:, NT // 2 - 1:], 0.0).then_inc(s_zero, 1)
            v.wait_ge(s_zero, 1)
            pipeline(v, step)

            def experts(n0):
                def norm(i, k):
                    route_norm1(i + n0, k, lambda: v.wait_ge(R["x"][k], AHEAD + (i - k + 2) * 8))

                def top(i, k, steps):
                    for s in steps:
                        route_step(i + n0, k, s, lambda: v.wait_ge(R["o"][k], AHEAD + (i + n0 - k) * 8))

                def tile(i, k, more):
                    for e in range(X):
                        expert_sums(i + n0, k, e, e + 1, G4)
                        if more and e == 0:
                            norm(i + 1, 1 - k)
                        if more and e == 1:
                            route_norm2(i + n0 + 1, 1 - k)
                        if more and e == 7:
                            route_scores(i + n0 + 1, 1 - k)
                        if more and e >= 9:
                            top(i + 1, 1 - k, range(2 * (e - 9), min(2 * (e - 8), 13)))
                    if more:
                        top(i + 1, 1 - k, range(13, 16))
                norm(0, 0)
                route_norm2(n0, 0)
                route_scores(n0, 0)
                top(0, 0, range(16))
                tiles(v, tile)

            def columns(first, last):
                return ac[:, first:last]

            def sums(b, t):
                n, k = b * NT + t, t % 2
                buf, sem, before = inputs_a[t % 4]
                v.wait_ge(sem, AHEAD + before + (b * (NT // 4) + t // 4 + 1) * 16)
                V.bn_stats(st[:, k, :], buf[:]).then_inc(A["st"], 1)

            def moments(b, t):
                n, k = b * NT + t, t % 2
                v.wait_ge(A["st"], AHEAD + n + 1)
                settle()
                V.bn_aggr(mv[:, k, :], st[:, k, :]).then_inc(A["mv"], 1)

            def norm(b, t):
                n, k = b * NT + t, t % 2
                v.wait_ge(A["rn"], AHEAD + n + 1)
                v.wait_ge(A["xT"], AHEAD + n)
                TS(mxn[:], inputs_a[t % 4][0][:], mv[:, k, 0:1], sc[:, 2 * k + 1:2 * k + 2], ALU.subtract, ALU.mult).then_inc(A["xn"], 1)

            def attend(b, more):
                v.wait_ge(A["pjs"], AHEAD + b * 12 + 8)
                V.tensor_reduce(columns(8, 12), columns(0, 8).rearrange("p (a g) -> p a g", g=NG), AX.X, ALU.add).then_inc(A["qk1"], 1)
                v.wait_ge(A["qk1"], AHEAD + b + 1)
                TS(columns(12, 16), columns(8, 12), 1e-6, None, ALU.add).then_inc(A["qk2"], 1)
                v.wait_ge(A["qk2"], AHEAD + b + 1)
                for m, c in enumerate((14, 15, 12, 13)):
                    TS(mats[:, m, :], hmask[:], columns(c, c + 1), None, ALU.mult).then_inc(A["hm"], 1)
                v.wait_ge(A["cv0"], AHEAD + b + 1)
                V.tensor_copy(columns(16, 20), M0[:, 0:4]).then_inc(A["cv"], 1)
                for src, dst, r, s, c0 in ((qa, r1, "r1", "qs", 20), (ka, r2, "r2", "ks", 24)):
                    for m in range(4):
                        j, g = m // NG, m % NG
                        v.wait_ge(A[r], AHEAD + b * 4 + m + 1)
                        o = dst[:, j, g * TG:(g + 1) * TG]
                        STT(o, src[:, j, g * TG:(g + 1) * TG], 1.0, o, ALU.mult, ALU.mult,
                                accum_out=columns(c0 + m, c0 + m + 1)).then_inc(A[s], 1)
                v.wait_ge(A["qs"], AHEAD + (b + 1) * 4)
                v.wait_ge(A["ks"], AHEAD + (b + 1) * 4)
                V.tensor_reduce(columns(28, 32), columns(20, 28).rearrange("p (a g) -> p a g", g=NG), AX.X, ALU.add).then_inc(A["s1"], 1)
                v.wait_ge(A["s1"], AHEAD + b + 1)
                TS(columns(32, 36), columns(28, 32), 1e-6, None, ALU.add).then_inc(A["s2"], 1)
                v.wait_ge(A["s2"], AHEAD + b + 1)
                for m, c in enumerate((34, 35, 32, 33)):
                    TS(mats[:, 4 + m, :], hmask[:], columns(c, c + 1), None, ALU.mult).then_inc(A["hn"], 1)
                v.wait_ge(A["cw0"], AHEAD + b + 1)
                V.tensor_copy(columns(36, 40), M0[:, 0:4]).then_inc(A["cw"], 1)
                v.wait_ge(A["cw"], AHEAD + b + 1)
                for m in range(4):
                    j, g = m // NG, m % NG
                    v.wait_ge(A["co"], AHEAD + b * 4 + m + 1)
                    TS(xTa[:, j, g * TG:(g + 1) * TG], (F0, F1, M0, M1)[m][:], columns(38 + j, 39 + j), 1.0, ALU.add, ALU.min).then_inc(A["cs"], 1)
                v.wait_ge(A["cs"], AHEAD + (b + 1) * 4)
                TS(xTa, xTa, -1.0, None, ALU.max).then_inc(A["cc"], 1)
                v.wait_ge(A["cc"], AHEAD + b + 1)
                V.tensor_reduce(columns(40, 42), xTa, AX.X, ALU.max).then_inc(A["mx"], 1)
                v.wait_ge(A["mx"], AHEAD + b + 1)
                TS(columns(42, 44), columns(40, 42), -1.0, None, ALU.mult).then_inc(A["nm"], 1)
                v.wait_ge(A["e"], AHEAD + (b + 1) * KD)
                V.reciprocal(columns(46, 48), columns(44, 46)).then_inc(A["rs"], 1)
                v.wait_ge(A["rs"], AHEAD + b + 1)
                TS(columns(48, 50), columns(46, 48), float(L), None, ALU.mult).then_inc(A["rl"], 1)
                v.wait_ge(A["rl"], AHEAD + b + 1)
                for j in range(KD):
                    STT(va[:, j, :], xTa[:, j, :], columns(48 + j, 49 + j), va[:, j, :], ALU.mult, ALU.mult).then_inc(A["v"], 1)
                v.wait_ge(A["kv0"], AHEAD + b + 1)
                for j in range(KD):
                    TT(mats[:, 8 + j, :], M0[:, j * P:(j + 1) * P], hmask[:], ALU.mult).then_inc(A["kvm"], 1)
                for m in range(4):
                    j, g = m // NG, m % NG
                    v.wait_ge(A["om"], AHEAD + b * 4 + m + 1)
                    o = r2[:, j, g * TG:(g + 1) * TG]
                    TT(o, (F0, F1, M1, G1)[m][:], o, ALU.mult).then_inc(A["og"], 1)
                for t in range(NT):
                    n = b * NT + t
                    v.wait_ge(A["om2"], AHEAD + n + 1)
                    v.wait_ge(A["o"][t % 2], AHEAD + (b * (NT // 2) + t // 2) * 16)
                    TT(x1b[t % 2][:], (BC, YP)[t % 2][:, 0:D], bo_row[:], ALU.add).then_inc(A["x2"], 1)
                    if more:
                        sums(b + 1, t)
                    v.wait_ge(A["x2"], AHEAD + n + 1)
                    v.wait_ge(A["q"][t % 2], AHEAD + (b * (NT // 2) + t // 2 + 1) * 16)
                    TT(x1b[t % 2][:], x1b[t % 2][:], xq[t % 2][:], ALU.add).then_inc(A["x3"], 1)
                    if more:
                        moments(b + 1, t)
                        if t > 0:
                            norm(b + 1, t - 1)
                if more:
                    norm(b + 1, NT - 1)

            for t in range(NT):
                sums(0, t)
                moments(0, t)
                if t > 0:
                    norm(0, t - 1)
            norm(0, NT - 1)
            with v.Fori(0, NB - 1) as b:
                attend(b, True)
            attend(NB - 1, False)
            experts(NTILES)


def _param(a, blocks):
    import numpy as np
    return np.ascontiguousarray(a.reshape(blocks, P, -1).transpose(1, 0, 2))


def layout(i):
    import numpy as np
    g = {k.replace("L0_", ""): np.asarray(v) for k, v in i.items()}
    row = lambda a: np.ascontiguousarray(np.broadcast_to(a, (P, a.shape[0])))
    col = lambda a: np.ascontiguousarray(a.reshape(-1, P).T)
    sel = np.tile(np.eye(RB, dtype=np.float32), (3, 1))
    hmask = np.kron(np.eye(P // 16), np.ones((16, 16))).astype(np.float32)
    xw = g["ffn_expert_w"]
    return {
        "x": g["attn_a_x"],
        "w_in": _param(g["attn_a_in_proj_w"].T, KD), "w_dt": _param(g["attn_a_dt_proj_w"].T, EB),
        "w_xp": _param(np.tile(g["attn_a_x_proj_w"].T, (1, 3)), EB), "w_out": _param(g["attn_a_out_proj_w"].T, EB),
        "w_r": _param(g["ffn_router_w"].T, KD),
        "w_x": np.ascontiguousarray(xw.reshape(X, KD, P, D).transpose(2, 1, 0, 3)).reshape(P, KD, X * D),
        "ident": np.eye(P, dtype=np.float32), "sel": sel, "hmask": hmask,
        "b_in": col(g["attn_a_in_proj_b"]), "cw": _param(g["attn_a_conv_w"].reshape(E, TAPS), EB),
        "cb": col(g["attn_a_conv_b"]), "b_dt": col(g["attn_a_dt_proj_b"]), "dpar": col(g["attn_a_D_param"]),
        "A_log": _param(g["attn_a_A_log"], EB).reshape(P, ST),
        "b_xp": np.tile(g["attn_a_x_proj_b"], 3).reshape(3 * RB, 1),
        "ga_in": col(g["attn_a_in_norm_alpha"]), "be_in": col(g["attn_a_in_norm_bias"]),
        "ob_row": row(g["attn_a_out_proj_b"]), "ga_row": row(g["attn_a_norm_alpha"]), "be_row": row(g["attn_a_norm_bias"]),
        "bo_row": row(g["attn_b_bo"]), "rb_row": row(g["ffn_router_b"]),
        "b_qkv": np.ascontiguousarray(np.stack([col(g[f"attn_b_b{c}"]) for c in "qkv"], 1)),
        "w_qkvo": np.ascontiguousarray(np.stack([_param(g[f"attn_b_W{c}"].T, KD) for c in "qkvo"], 1)),
    }


def kernel(**inputs):
    import numpy as _np
    import concourse.bacc as _bacc
    from concourse import mybir as _mybir
    from concourse.bass_utils import run_bass_kernel_spmd as _run

    nc = _bacc.Bacc("TRN2", target_bir_lowering=False, num_devices=1)
    arrays, dram = {}, {}
    for name, a in layout(inputs).items():
        a = _np.ascontiguousarray(a)
        arrays[f"in_{name}"] = a
        dram[name] = nc.dram_tensor(f"in_{name}", a.shape, _mybir.dt.from_np(a.dtype), kind="ExternalInput").ap()
    for name in ("x1d", "x2d", "x3d"):
        dram[name] = nc.dram_tensor(name, (NB, L, D), _mybir.dt.float32, kind="Internal").ap()
    out = nc.dram_tensor("out_dram", (NB, L, D), _mybir.dt.float32, kind="ExternalOutput").ap()
    build(nc, dram, out)
    r = _run(nc, [arrays], core_ids=[0])
    return r.results[0]["out_dram"]
```
